# Optimizing a Trainium2 kernel written in Bass

```python
import numpy as np
import jax
import jax.numpy as jnp

def _softmax(x, axis=-1):
    return jax.nn.softmax(x, axis=axis)

def _gelu(x):
    return jax.nn.gelu(x, approximate=True)

def _silu(x):
    return jax.nn.silu(x)

def _sigmoid(x):
    return jax.nn.sigmoid(x)

def _layernorm(x, axis=-1, eps=1e-05):
    m = jnp.mean(x, axis=axis, keepdims=True)
    v = jnp.var(x, axis=axis, keepdims=True)
    return (x - m) / jnp.sqrt(v + eps)

def _scatter_add(tgt, idx, src, axis=0):
    return tgt.at[idx].add(src)

def _segment_sum(src, seg, n):
    return jax.ops.segment_sum(src, seg, n)
kernel_name = 'mk_gps_d2_gnn_r8_3b41a7'

def setup_inputs(seed: int=0):
    np.random.seed(seed)
    _w = jnp.asarray

    def _rec_inputs():
        import jax
        import jax.numpy as jnp
        _gk = jax.random.key(seed)
        x = -8.776e-05 + 1 * jax.random.normal(jax.random.fold_in(_gk, 1), (1250, 512), jnp.float32)
        src = jax.random.randint(jax.random.fold_in(_gk, 2), (20000,), 0, 1250, jnp.int32)
        dst = jnp.minimum((1250 * jax.random.uniform(jax.random.fold_in(_gk, 3), (20000,)) ** 2.0).astype(jnp.int32), 9999)
        _o = jnp.argsort(dst, stable=True)
        src = src[_o]
        dst = dst[_o]
        return (x, src, dst)
    x, src, dst = _rec_inputs()

    def _L0_gnn_setup():
        import jax, jax.numpy as jnp
        import numpy as np
        N_NODES = 1250
        N_EDGES = 20000
        IN_DIM = 512
        OUT_DIM = 512
        LN_EPS = 1e-05
        key = jax.random.key(seed)
        k_x, k_src, k_ws, k_wn = jax.random.split(key, 4)
        x = jax.random.normal(k_x, (N_NODES, IN_DIM), dtype=jnp.float32)
        edge_src = jax.random.randint(k_src, (N_EDGES,), 0, N_NODES, dtype=jnp.int32)
        edge_dst = jnp.repeat(jnp.arange(N_NODES, dtype=jnp.int32), N_EDGES // N_NODES)
        deg = jnp.full((N_NODES,), float(N_EDGES // N_NODES), dtype=jnp.float32)
        scale = 1.0 / np.sqrt(IN_DIM)
        W_self = jax.random.normal(k_ws, (OUT_DIM, IN_DIM), dtype=jnp.float32) * scale
        W_neigh = jax.random.normal(k_wn, (OUT_DIM, IN_DIM), dtype=jnp.float32) * scale
        bias = jnp.zeros((OUT_DIM,), dtype=jnp.float32)
        gamma = jnp.ones((OUT_DIM,), dtype=jnp.float32)
        beta = jnp.zeros((OUT_DIM,), dtype=jnp.float32)
        return {'x': x, 'edge_src': edge_src, 'edge_dst': edge_dst, 'deg': deg, 'W_self': W_self, 'W_neigh': W_neigh, 'bias': bias, 'gamma': gamma, 'beta': beta}
    _L0_gnn_all = _L0_gnn_setup()
    _L0_gnn_in = {k: v for k, v in _L0_gnn_all.items() if k in ('W_self', 'W_neigh', 'bias', 'gamma', 'beta')}
    del _L0_gnn_all

    def _L0_mix_setup():
        import jax, jax.numpy as jnp
        import numpy as np
        import math
        D_MODEL = 512
        key = jax.random.key(seed)
        k1, k2, k3 = jax.random.split(key, 3)
        X = jax.random.normal(k1, (4, 1024, D_MODEL), dtype=jnp.float32)
        s = 1.0 / math.sqrt(D_MODEL)
        W_v = jax.random.uniform(k2, (D_MODEL, D_MODEL), dtype=jnp.float32, minval=-s, maxval=s)
        W_theta = jax.random.uniform(k3, (D_MODEL, D_MODEL), dtype=jnp.float32, minval=-s, maxval=s)
        return {'X': X, 'W_v': W_v, 'W_theta': W_theta}
    _L0_mix_all = _L0_mix_setup()
    _L0_mix_in = {k: v for k, v in _L0_mix_all.items() if k in ('W_v', 'W_theta')}
    del _L0_mix_all

    def _L0_ffn_setup():
        import jax, jax.numpy as jnp
        import numpy as np
        from jax import lax
        N_HEADS = 8
        D_KEYS = 128
        HALF = D_KEYS // 2
        N_KEYS = 256
        TOP_K = 8
        D_MODEL = 512

        def _forward(queries, Wq, bq, keys, w_down, w_up):
            N, T, D = queries.shape
            x = queries.reshape(-1, D)
            q = (x @ Wq + bq).reshape(-1, N_HEADS, D_KEYS)
            q1, q2 = (q[..., :HALF], q[..., HALF:])
            s1 = jnp.einsum('bhc,hnc->bhn', q1, keys[:, 0])
            s2 = jnp.einsum('bhc,hnc->bhn', q2, keys[:, 1])
            s1t, i1 = lax.top_k(s1, TOP_K)
            s2t, i2 = lax.top_k(s2, TOP_K)
            all_scores = (s1t[..., :, None] + s2t[..., None, :]).reshape(-1, N_HEADS, TOP_K * TOP_K)
            all_idx = (i1[..., :, None] * N_KEYS + i2[..., None, :]).reshape(-1, N_HEADS, TOP_K * TOP_K)
            scores, best = lax.top_k(all_scores, TOP_K)
            indices = jnp.take_along_axis(all_idx, best, axis=-1)
            w_d = w_down[indices]
            w_u = w_up[indices]
            inner = jnp.einsum('bd,bhkd->bhk', x, w_d)
            vals = jax.nn.relu(inner) * jax.nn.softmax(scores, axis=-1)
            out = jnp.einsum('bhk,bhkd->bd', vals, w_u)
            return out.reshape(N, T, D)
        key = jax.random.key(seed)
        ks = jax.random.split(key, 6)
        N, T = (2, 1024)
        queries = jax.random.normal(ks[0], (N, T, D_MODEL), dtype=jnp.float32)
        Wq = jax.random.normal(ks[1], (D_MODEL, N_HEADS * D_KEYS), dtype=jnp.float32) / np.sqrt(D_MODEL)
        bq = jnp.zeros((N_HEADS * D_KEYS,), dtype=jnp.float32)
        bound = 1.0 / np.sqrt(HALF)
        keys = jax.random.uniform(ks[2], (N_HEADS, 2, N_KEYS, HALF), dtype=jnp.float32, minval=-bound, maxval=bound)
        w_down = jax.random.normal(ks[3], (N_KEYS * N_KEYS, D_MODEL), dtype=jnp.float32) * 0.02
        w_up = jax.random.normal(ks[4], (N_KEYS * N_KEYS, D_MODEL), dtype=jnp.float32) * 0.02
        return {'queries': queries, 'Wq': Wq, 'bq': bq, 'keys': keys, 'w_down': w_down, 'w_up': w_up}
    _L0_ffn_all = _L0_ffn_setup()
    _L0_ffn_in = {k: v for k, v in _L0_ffn_all.items() if k in ('Wq', 'bq', 'keys', 'w_down', 'w_up')}
    del _L0_ffn_all

    def _L1_gnn_setup():
        import jax, jax.numpy as jnp
        import numpy as np
        from math import sqrt
        N = 6250
        E = 100000
        D_EMB = 512
        DK = 64
        DV = 64
        HEADS = 8

        def _attention_message(Q, K, V, senders, receivers, n_nodes):
            scale = 1.0 / sqrt(Q.shape[-1])
            scores = jnp.einsum('ehd,ehd->eh', Q[receivers], K[senders]) * scale
            smax = jax.ops.segment_max(scores, receivers, num_segments=n_nodes)
            ex = jnp.exp(scores - smax[receivers])
            denom = jax.ops.segment_sum(ex, receivers, num_segments=n_nodes)
            att = ex / denom[receivers]
            out = jax.ops.segment_sum(att[:, :, None] * V[senders], receivers, num_segments=n_nodes)
            return (out, att)
        key = jax.random.key(seed)
        k1, k2, k3, k4 = jax.random.split(key, 4)
        x = jax.random.normal(k1, (N, D_EMB), dtype=jnp.float32)
        edge_index = jax.random.randint(k2, (2, E), 0, N, dtype=jnp.int64)
        out_qkv = (2 * DK + DV) * HEADS
        W_qkv = jax.random.normal(k3, (out_qkv, D_EMB), dtype=jnp.float32) / sqrt(D_EMB)
        b_qkv = jnp.zeros((out_qkv,), dtype=jnp.float32)
        W_ff = jax.random.normal(k4, (D_EMB, DV * HEADS), dtype=jnp.float32) / sqrt(DV * HEADS)
        b_ff = jnp.zeros((D_EMB,), dtype=jnp.float32)
        return {'x': x, 'edge_index': edge_index, 'W_qkv': W_qkv, 'b_qkv': b_qkv, 'W_ff': W_ff, 'b_ff': b_ff}
    _L1_gnn_all = _L1_gnn_setup()
    _L1_gnn_in = {k: v for k, v in _L1_gnn_all.items() if k in ('W_qkv', 'b_qkv', 'W_ff', 'b_ff')}
    del _L1_gnn_all

    def _L1_mix_setup():
        import jax, jax.numpy as jnp
        import numpy as np
        DIM = 512
        HEADS = 8
        DIM_HEAD = 64
        INNER = HEADS * DIM_HEAD
        key = jax.random.key(seed)
        k1, k2, k3, k4 = jax.random.split(key, 4)
        x = jax.random.normal(k1, (2, 256, DIM), dtype=jnp.float32)
        w_qkv = jax.random.normal(k2, (INNER * 3, DIM), dtype=jnp.float32) * (1.0 / np.sqrt(DIM))
        w_out = jax.random.normal(k3, (DIM, INNER), dtype=jnp.float32) * (1.0 / np.sqrt(INNER))
        b_out = jax.random.normal(k4, (DIM,), dtype=jnp.float32) * 0.01
        return {'x': x, 'w_qkv': w_qkv, 'w_out': w_out, 'b_out': b_out}
    _L1_mix_all = _L1_mix_setup()
    _L1_mix_in = {k: v for k, v in _L1_mix_all.items() if k in ('w_qkv', 'w_out', 'b_out')}
    del _L1_mix_all

    def _L1_ffn_setup():
        import jax, jax.numpy as jnp
        import numpy as np
        E = 8
        TOP_K = 2
        D = 512
        H = 1024
        B, S = (16, 512)
        key = jax.random.key(seed)
        ks = jax.random.split(key, 10)
        sd = lambda fan_in: 1.0 / np.sqrt(fan_in)
        x = jax.random.normal(ks[0], (B, S, D), dtype=jnp.float32)
        gw1 = jax.random.uniform(ks[1], (D, D // 2), jnp.float32, -sd(D), sd(D))
        gb1 = jnp.zeros((D // 2,), jnp.float32)
        gw2 = jax.random.uniform(ks[2], (D // 2, E), jnp.float32, -sd(D // 2), sd(D // 2))
        gb2 = jnp.zeros((E,), jnp.float32)
        we1 = jax.random.uniform(ks[3], (E, D, H), jnp.float32, -sd(D), sd(D))
        be1 = jnp.zeros((E, H), jnp.float32)
        we2 = jax.random.uniform(ks[4], (E, H, D), jnp.float32, -sd(H), sd(H))
        be2 = jnp.zeros((E, D), jnp.float32)
        return {'x': x, 'gw1': gw1, 'gb1': gb1, 'gw2': gw2, 'gb2': gb2, 'we1': we1, 'be1': be1, 'we2': we2, 'be2': be2}
    _L1_ffn_all = _L1_ffn_setup()
    _L1_ffn_in = {k: v for k, v in _L1_ffn_all.items() if k in ('gw1', 'gb1', 'gw2', 'gb2', 'we1', 'be1', 'we2', 'be2')}
    del _L1_ffn_all
    return {'x': x, 'src': src, 'dst': dst, 'L0_gnn_W_self': _L0_gnn_in['W_self'], 'L0_gnn_W_neigh': _L0_gnn_in['W_neigh'], 'L0_gnn_bias': _L0_gnn_in['bias'], 'L0_gnn_gamma': _L0_gnn_in['gamma'], 'L0_gnn_beta': _L0_gnn_in['beta'], 'L0_mix_W_v': _L0_mix_in['W_v'], 'L0_mix_W_theta': _L0_mix_in['W_theta'], 'L0_ffn_Wq': _L0_ffn_in['Wq'], 'L0_ffn_bq': _L0_ffn_in['bq'], 'L0_ffn_keys': _L0_ffn_in['keys'], 'L0_ffn_w_down': _L0_ffn_in['w_down'], 'L0_ffn_w_up': _L0_ffn_in['w_up'], 'L1_gnn_W_qkv': _L1_gnn_in['W_qkv'], 'L1_gnn_b_qkv': _L1_gnn_in['b_qkv'], 'L1_gnn_W_ff': _L1_gnn_in['W_ff'], 'L1_gnn_b_ff': _L1_gnn_in['b_ff'], 'L1_mix_w_qkv': _L1_mix_in['w_qkv'], 'L1_mix_w_out': _L1_mix_in['w_out'], 'L1_mix_b_out': _L1_mix_in['b_out'], 'L1_ffn_gw1': _L1_ffn_in['gw1'], 'L1_ffn_gb1': _L1_ffn_in['gb1'], 'L1_ffn_gw2': _L1_ffn_in['gw2'], 'L1_ffn_gb2': _L1_ffn_in['gb2'], 'L1_ffn_we1': _L1_ffn_in['we1'], 'L1_ffn_be1': _L1_ffn_in['be1'], 'L1_ffn_we2': _L1_ffn_in['we2'], 'L1_ffn_be2': _L1_ffn_in['be2']}

def reference(x, src, dst, L0_gnn_W_self, L0_gnn_W_neigh, L0_gnn_bias, L0_gnn_gamma, L0_gnn_beta, L0_mix_W_v, L0_mix_W_theta, L0_ffn_Wq, L0_ffn_bq, L0_ffn_keys, L0_ffn_w_down, L0_ffn_w_up, L1_gnn_W_qkv, L1_gnn_b_qkv, L1_gnn_W_ff, L1_gnn_b_ff, L1_mix_w_qkv, L1_mix_w_out, L1_mix_b_out, L1_ffn_gw1, L1_ffn_gb1, L1_ffn_gw2, L1_ffn_gb2, L1_ffn_we1, L1_ffn_be1, L1_ffn_we2, L1_ffn_be2):
    import jax
    import jax.numpy as jnp

    def _L0_gnn_ref(x, edge_src, edge_dst, deg, W_self, W_neigh, bias, gamma, beta):
        import jax, jax.numpy as jnp
        import numpy as np
        N_NODES = 1250
        N_EDGES = 20000
        IN_DIM = 512
        OUT_DIM = 512
        LN_EPS = 1e-05
        n = x.shape[0]
        h_self = jnp.einsum('nd,od->no', x, W_self)
        neigh_sum = jax.ops.segment_sum(x[edge_src], edge_dst, num_segments=n)
        neigh_mean = neigh_sum / jnp.maximum(deg, 1.0)[:, None]
        h_neigh = jnp.einsum('nd,od->no', neigh_mean, W_neigh)
        h = h_self + h_neigh + bias
        mu = jnp.mean(h, axis=-1, keepdims=True)
        var = jnp.mean(jnp.square(h - mu), axis=-1, keepdims=True)
        h = (h - mu) * jax.lax.rsqrt(var + LN_EPS)
        return h * gamma + beta

    def _L0_mix_ref(X, W_v, W_theta):
        import jax, jax.numpy as jnp
        import numpy as np
        import math
        D_MODEL = 512
        n = X.shape[1]
        d = X.shape[2]
        XW_v = X @ W_v.T
        theta_X = X @ W_theta.T
        first_term = jnp.mean(XW_v, axis=1, keepdims=True)
        kv = jnp.einsum('bnd,bne->bde', theta_X, XW_v)
        second_term = X @ kv / (n * math.sqrt(d))
        return first_term + second_term

    def _L0_ffn_ref(queries, Wq, bq, keys, w_down, w_up):
        import jax, jax.numpy as jnp
        import numpy as np
        from jax import lax
        N_HEADS = 8
        D_KEYS = 128
        HALF = D_KEYS // 2
        N_KEYS = 256
        TOP_K = 8
        D_MODEL = 512

        def _forward(queries, Wq, bq, keys, w_down, w_up):
            N, T, D = queries.shape
            x = queries.reshape(-1, D)
            q = (x @ Wq + bq).reshape(-1, N_HEADS, D_KEYS)
            q1, q2 = (q[..., :HALF], q[..., HALF:])
            s1 = jnp.einsum('bhc,hnc->bhn', q1, keys[:, 0])
            s2 = jnp.einsum('bhc,hnc->bhn', q2, keys[:, 1])
            s1t, i1 = lax.top_k(s1, TOP_K)
            s2t, i2 = lax.top_k(s2, TOP_K)
            all_scores = (s1t[..., :, None] + s2t[..., None, :]).reshape(-1, N_HEADS, TOP_K * TOP_K)
            all_idx = (i1[..., :, None] * N_KEYS + i2[..., None, :]).reshape(-1, N_HEADS, TOP_K * TOP_K)
            scores, best = lax.top_k(all_scores, TOP_K)
            indices = jnp.take_along_axis(all_idx, best, axis=-1)
            w_d = w_down[indices]
            w_u = w_up[indices]
            inner = jnp.einsum('bd,bhkd->bhk', x, w_d)
            vals = jax.nn.relu(inner) * jax.nn.softmax(scores, axis=-1)
            out = jnp.einsum('bhk,bhkd->bd', vals, w_u)
            return out.reshape(N, T, D)
        return _forward(queries, Wq, bq, keys, w_down, w_up)

    def _L1_gnn_ref(x, edge_index, W_qkv, b_qkv, W_ff, b_ff):
        import jax, jax.numpy as jnp
        import numpy as np
        from math import sqrt
        N = 6250
        E = 100000
        D_EMB = 512
        DK = 64
        DV = 64
        HEADS = 8

        def _attention_message(Q, K, V, senders, receivers, n_nodes):
            scale = 1.0 / sqrt(Q.shape[-1])
            scores = jnp.einsum('ehd,ehd->eh', Q[receivers], K[senders]) * scale
            smax = jax.ops.segment_max(scores, receivers, num_segments=n_nodes)
            ex = jnp.exp(scores - smax[receivers])
            denom = jax.ops.segment_sum(ex, receivers, num_segments=n_nodes)
            att = ex / denom[receivers]
            out = jax.ops.segment_sum(att[:, :, None] * V[senders], receivers, num_segments=n_nodes)
            return (out, att)
        n_nodes = x.shape[0]
        qkv = x @ W_qkv.T + b_qkv
        Q, K, V = jnp.split(qkv, [DK * HEADS, 2 * DK * HEADS], axis=-1)
        Q = Q.reshape(n_nodes, HEADS, DK)
        K = K.reshape(n_nodes, HEADS, DK)
        V = V.reshape(n_nodes, HEADS, DV)
        senders, receivers = (edge_index[0], edge_index[1])
        msg, _ = _attention_message(Q, K, V, senders, receivers, n_nodes)
        out = msg.reshape(n_nodes, HEADS * DV) @ W_ff.T + b_ff
        return out

    def _L1_mix_ref(x, w_qkv, w_out, b_out):
        import jax, jax.numpy as jnp
        import numpy as np
        DIM = 512
        HEADS = 8
        DIM_HEAD = 64
        INNER = HEADS * DIM_HEAD
        b, n, _ = x.shape
        qkv = x @ w_qkv.T
        q, k, v = jnp.split(qkv, 3, axis=-1)

        def to_heads(t):
            return t.reshape(b, n, HEADS, DIM_HEAD).transpose(0, 2, 1, 3)
        q, k, v = map(to_heads, (q, k, v))
        q = jax.nn.softmax(q, axis=-1)
        k = jax.nn.softmax(k, axis=-2)
        context = jnp.einsum('bhid,bhjd->bhij', k, v)
        out = jnp.einsum('bhij,bhie->bhje', context, q)
        out = out.transpose(0, 2, 1, 3).reshape(b, n, INNER)
        return out @ w_out.T + b_out

    def _L1_ffn_ref(x, gw1, gb1, gw2, gb2, we1, be1, we2, be2):
        import jax, jax.numpy as jnp
        import numpy as np
        E = 8
        TOP_K = 2
        D = 512
        H = 1024
        B, S = (16, 512)
        b, s, d = x.shape
        xf = x.reshape(-1, d)
        T = xf.shape[0]
        gate_logits = jax.nn.relu(xf @ gw1 + gb1) @ gw2 + gb2
        gate_weights = jax.nn.softmax(gate_logits, axis=-1)
        top_w, top_idx = jax.lax.top_k(gate_weights, TOP_K)
        top_w = jax.nn.softmax(top_w, axis=-1)
        combine = jnp.zeros((T, E), dtype=xf.dtype)
        combine = combine.at[jnp.arange(T)[:, None], top_idx].add(top_w)
        out = jnp.zeros_like(xf)
        for e in range(E):
            h = jax.nn.gelu(xf @ we1[e] + be1[e], approximate=False)
            y = h @ we2[e] + be2[e]
            out = out + combine[:, e:e + 1] * y
        return out.reshape(b, s, d)
    edge_index = jnp.stack([src, dst])
    deg = jnp.maximum(jax.ops.segment_sum(jnp.ones(dst.shape, jnp.float32), dst, num_segments=1250), 1.0)
    xn = _layernorm(x, axis=-1)
    x = x + _L0_gnn_ref(xn, src, dst, deg, L0_gnn_W_self, L0_gnn_W_neigh, L0_gnn_bias, L0_gnn_gamma, L0_gnn_beta) + _L0_mix_ref(xn[None], L0_mix_W_v, L0_mix_W_theta)[0]
    x = x + _L0_ffn_ref(_layernorm(x, axis=-1)[None], L0_ffn_Wq, L0_ffn_bq, L0_ffn_keys, L0_ffn_w_down, L0_ffn_w_up)[0]
    xn = _layernorm(x, axis=-1)
    x = x + _L1_gnn_ref(xn, edge_index, L1_gnn_W_qkv, L1_gnn_b_qkv, L1_gnn_W_ff, L1_gnn_b_ff) + _L1_mix_ref(xn[None], L1_mix_w_qkv, L1_mix_w_out, L1_mix_b_out)[0]
    x = x + _L1_ffn_ref(_layernorm(x, axis=-1)[None], L1_ffn_gw1, L1_ffn_gb1, L1_ffn_gw2, L1_ffn_gb2, L1_ffn_we1, L1_ffn_be1, L1_ffn_we2, L1_ffn_be2)[0]
    return x

_drawn_inputs = setup_inputs


def setup_inputs(seed=0):
    import zlib

    import numpy as np

    out = dict(_drawn_inputs(seed))
    spreads = {'L0_gnn_bias': (0.0, 0.1),
     'L0_gnn_gamma': (1.0, 0.2),
     'L0_gnn_beta': (0.0, 0.1),
     'L0_ffn_bq': (0.0, 0.8),
     'L1_gnn_b_qkv': (0.0, 0.1),
     'L1_gnn_b_ff': (0.0, 0.1),
     'L1_ffn_gb1': (0.0, 0.1),
     'L1_ffn_gb2': (0.0, 0.1),
     'L1_ffn_be1': (0.0, 0.491),
     'L1_ffn_be2': (0.0, 0.1)}
    factors = {'L0_mix_W_theta': 2.72,
     'L0_ffn_Wq': 6.842,
     'L0_ffn_keys': 7.913,
     'L0_ffn_w_down': 8.0,
     'L0_ffn_w_up': 7.94,
     'L1_mix_b_out': 5.622}
    for name, (base, spread) in spreads.items():
        noise = np.random.default_rng([zlib.crc32(name.encode()), seed]).standard_normal(out[name].shape)
        drawn = base * np.exp(spread * noise) if base else spread * noise
        out[name] = jnp.asarray(drawn.astype(out[name].dtype))
    for name, factor in factors.items():
        out[name] = (out[name] * factor).astype(out[name].dtype)
    return out
```

```python
from contextlib import ExitStack

import concourse.bass as bass
from concourse import mybir

F32 = mybir.dt.float32
BF16 = mybir.dt.bfloat16
F16 = mybir.dt.float16
I32 = mybir.dt.int32
U32 = mybir.dt.uint32
U16 = mybir.dt.uint16
ALU = mybir.AluOpType
ACT = mybir.ActivationFunctionType
AX = mybir.AxisListType.X

P = 128
N = 1250
NT = -(-N // P)
NP = NT * P
TAIL = N - (NT - 1) * P
D = 512
KC = D // P
E = 20000
EPAIR = 250
EC = EPAIR // 2
NG = E // EPAIR
HEADS = 8
NKEYS = 256
TOPK = 8
EXP = 8
HID = 1024
HC = HID // P
EPS = 1e-5
NEG = -1e30
CHUNKS = [(0, 512), (512, 512), (1024, 256)]


class Core:

    def __init__(self, nc, ctx, ins, out):
        self.nc, self.ctx, self.ins, self.out = nc, ctx, ins, out
        self.x = ctx.enter_context(nc.sbuf_tensor("x_rows", [P, NT, D], F32))
        self.xnT = ctx.enter_context(nc.sbuf_tensor("xnT", [P, KC, NP], F32))
        self.ident = ctx.enter_context(nc.sbuf_tensor("ident", [P, P], F32))
        self.counts = nc.dram_tensor("edge_counts", (NT, P, NP), U16, kind="Internal").ap()

        self.live = []
        self.stage, self.passed = 0, None

    def sem(self, name):
        self.live.append(self.nc.alloc_semaphore(name=name))
        return self.live[-1]

    def end_stage(self):
        self.nc.clear_and_free_semaphores(self.live)
        self.live, self.passed = [], None
        self.nc.all_engine_barrier()


class RowStats:

    def __init__(self, c, st, tag):
        sb = lambda n, s: st.enter_context(c.nc.sbuf_tensor(tag + n, s, F32))
        self.c, self.stats, self.mv, self.rstd = c, sb("stats", [P, NT, 6]), sb("mv", [P, NT, 2]), sb("rstd", [P, NT])
        self.root = sb("root", [P, NT])
        self.s_mv, self.s_root = c.sem(tag + "moments"), c.sem(tag + "root")

    def moments(self, dve):
        for t in range(NT):
            dve.bn_stats(self.stats[:, t, :], self.c.x[:, t, :])
        dve.drain()
        for t in range(NT):
            dve.bn_aggr(self.mv[:, t, :], self.stats[:, t, :])
        dve.drain()
        dve.tensor_scalar(self.rstd[:, :], self.mv[:, :, 1], EPS, None, ALU.add).then_inc(self.s_mv, 1)
        dve.wait_ge(self.s_root, 1)
        dve.reciprocal(self.rstd[:, :], self.root[:, :])
        dve.drain()

    def roots(self, act):
        act.wait_ge(self.s_mv, 1)
        act.activation(self.root[:, :], self.rstd[:, :], ACT.Sqrt).then_inc(self.s_root, 1)

    def normalise(self, dve, t, dst):
        one = bass.ds(t, 1)
        return dve.tensor_scalar(dst, self.c.x[:, one, :], self.mv[:, one, 0], self.rstd[:, one], ALU.subtract, ALU.mult)


def wait_alone(c, eng, sem, value):
    eng.wait_ge(sem, value)
    if c.passed is None:
        c.stage += 1
        c.passed = c.sem(f"passed{c.stage}")
    eng.sem_inc(c.passed, 1)


def column(t):
    return bass.ds(t * P, P)


def stage_prepare(c, keep):
    nc, ins = c.nc, c.ins
    xn, kv, mean_row = keep
    with ExitStack() as st:
        sb = lambda n, s, d: st.enter_context(nc.sbuf_tensor(n, s, d))
        ps = lambda n, s: st.enter_context(nc.psum_tensor(n, s, F32))
        wv, wth = sb("wv", [P, KC, D], F32), sb("wth", [P, KC, D], F32)
        rows = sb("rows", [P, D], F32)
        norm = RowStats(c, st, "p_")
        gram, m1 = sb("gram", [P, KC, D], F32), sb("m1", [P, KC, D], F32)
        xsum, xbar = sb("xsum", [P, KC], F32), sb("xbar", [P, KC, P], F32)
        ones = sb("ones", [P, P], F32)
        psT, psG, psM = ps("psT", [P, D]), ps("psG", [P, KC, D]), ps("psM", [P, 2, D])
        s_tail, s_x, s_w, s_id0, s_id, s_ones = (c.sem("p_" + n) for n in ("tail", "x", "w", "id0", "id", "ones"))
        s_rows, s_tr, s_tdone, s_copied = (c.sem("p_" + n) for n in ("rows", "tr", "tdone", "copied"))
        s_gram, s_gdone, s_bar, s_mm, s_ev = (c.sem("p_" + n) for n in ("gram", "gdone", "bar", "mm", "ev"))
        block = st.enter_context(nc.Block())

        @block.sync
        def _(sp):
            sp.dma_start(c.x[:, 0:NT - 1, :], ins["x"][0:(NT - 1) * P, :].rearrange("(t p) d -> p t d", p=P)).then_inc(s_x, 16)
            sp.wait_ge(s_tail, 1)
            sp.dma_start(c.x[0:TAIL, NT - 1, :], ins["x"][(NT - 1) * P:N, :]).then_inc(s_x, 16)
            sp.dma_start(wv[:, :, :], ins["W_vT"].rearrange("(k p) n -> p k n", p=P)).then_inc(s_w, 16)
            sp.dma_start(wth[:, :, :], ins["W_thetaT"].rearrange("(k p) n -> p k n", p=P)).then_inc(s_w, 16)

        @block.gpsimd
        def _(pool):
            pool.memset(c.x[96:P, NT - 1, :], 0.0).then_inc(s_tail, 1)
            pool.wait_ge(s_tail, 1)
            pool.memset(c.ident[:, :], 0.0).then_inc(s_id0, 1)
            pool.wait_ge(s_id0, 1)
            pool.affine_select(out=c.ident[:, :], in_=c.ident[:, :], compare_op=ALU.not_equal, fill=1.0,
                               base=0, pattern=[[-1, P]], channel_multiplier=1).then_inc(s_id, 1)
            pool.memset(ones[:, :], 1.0).then_inc(s_ones, 1)

        @block.vector
        def _(dve):
            dve.wait_ge(s_x, 32)
            norm.moments(dve)
            with dve.Fori(0, NT) as t:
                dve.wait_ge(s_gram, t)
                dve.wait_ge(s_copied, t)
                norm.normalise(dve, t, rows[:, :]).then_inc(s_rows, 1)
            dve.wait_ge(s_tdone, NT)
            dve.tensor_reduce(xsum[:, :], c.xnT[:, :, :], AX, ALU.add)
            dve.wait_ge(s_ones, 1)
            dve.drain()
            for k in range(KC):
                bar = dve.tensor_scalar(xbar[:, k, :], ones[:, :], xsum[:, k:k + 1], 1.0 / N, ALU.mult, ALU.mult)
            bar.then_inc(s_bar, 1)

        @block.scalar
        def _(act):
            norm.roots(act)
            with act.Fori(0, NT) as t:
                wait_alone(c, act, s_rows, t + 1)
                act.activation(xn[:, bass.ds(t, 1), :], rows[:, :], ACT.Copy).then_inc(s_copied, 1)
                wait_alone(c, act, s_tr, t + 1)
                act.activation(c.xnT[:, :, column(t)], psT[:, :].rearrange("p (k n) -> p k n", k=KC),
                               ACT.Copy).then_inc(s_tdone, 1)
            act.wait_ge(s_gdone, 1)
            act.activation(gram[:, :, :], psG[:, :, :], ACT.Copy).then_inc(s_ev, 1)
            for m in range(2 * KC):
                act.wait_ge(s_mm, m + 1)
                dst, scale = (m1, 1.0) if m < KC else (kv, 1.0 / (N * D ** 0.5))
                act.activation(dst[:, m % KC, :], psM[:, m % 2, :], ACT.Copy, scale=scale).then_inc(s_ev, 1)
            act.wait_ge(s_mm, 2 * KC + 1)
            act.activation(mean_row[:, :], psM[:, 0, :], ACT.Copy).then_inc(s_ev, 1)

        @block.tensor
        def _(pe):
            pe.wait_ge(s_id, 1)

            def tile(t, first):
                pe.wait_ge(s_rows, t + 1)
                pe.wait_ge(s_tdone, t)
                for k in range(KC):
                    mm = pe.transpose(psT[:, k * P:(k + 1) * P], rows[:, k * P:(k + 1) * P], c.ident[:, :])
                mm.then_inc(s_tr, 1)
                for m in range(KC):
                    mm = pe.matmul(psG[:, m, :], rows[:, m * P:(m + 1) * P], rows[:, :], start=first, stop=True,
                                   skip_group_check=True)
                mm.then_inc(s_gram, 1)

            tile(0, True)
            with pe.Fori(1, NT) as t:
                tile(t, False)
            pe.matmul(psM[:, 0, 0:P], rows[:, 0:P], c.ident[:, :], start=True, stop=True).then_inc(s_gdone, 1)
            pe.wait_ge(s_w, 32)
            pe.wait_ge(s_ev, 1)
            for m in range(2 * KC):
                left, right = (gram, wv) if m < KC else (wth, m1)
                if m >= 2:
                    pe.wait_ge(s_ev, m)
                if m == KC:
                    pe.wait_ge(s_ev, KC + 1)
                for k in range(KC):
                    mm = pe.matmul(psM[:, m % 2, :], left[:, k, m % KC * P:(m % KC + 1) * P], right[:, k, :],
                                   start=k == 0, stop=k == KC - 1)
                mm.then_inc(s_mm, 1)
            pe.wait_ge(s_ev, 2 * KC)
            pe.wait_ge(s_bar, 1)
            for k in range(KC):
                mm = pe.matmul(psM[:, 0, :], xbar[:, k, :], wv[:, k, :], start=k == 0, stop=k == KC - 1)
            mm.then_inc(s_mm, 1)


def stage_graph(c, keep):
    nc, ins = c.nc, c.ins
    xn, kv, mean_row = keep
    with ExitStack() as st:
        sb = lambda n, s, d: st.enter_context(nc.sbuf_tensor(n, s, d))
        ps = lambda n, s: st.enter_context(nc.psum_tensor(n, s, F32))
        ws, wn = sb("ws", [P, KC, D], F32), sb("wn", [P, KC, D], F32)
        bias, gamma, beta = sb("bias", [P, D], F32), sb("gamma", [P, D], F32), sb("beta", [P, D], F32)
        edge_i, edge_f = sb("edge_i", [NG, 2, EPAIR], I32), sb("edge_f", [NG, 2, EPAIR], F32)
        ends = sb("ends", [NG, 2], F32)
        edges = sb("edges", [EC, 4, 2 * NG], F32)
        shifted = sb("shifted", [EC, 2, 2 * NG], F32)
        row = sb("row", [1, 6, NT * NG], F32)
        group_i, group_id = sb("group_i", [1, NG], I32), sb("group_id", [1, NG], F32)
        tile_i, tile_lo, tile_hi = sb("tile_i", [P, NT], I32), sb("tile_lo", [P, NT], F32), sb("tile_hi", [P, NT], F32)
        bounds_f, bounds = sb("bounds_f", [1, 4, NT], F32), sb("bounds", [1, 2 * NT], I32)
        node_i, node_id = sb("node_i", [P, NP], I32), sb("node_id", [P, NP], F16)
        zero = sb("zero", [P, D], BF16)
        hot_dst, hot_src = sb("hot_dst", [EC, 2, P], BF16), sb("hot_src", [EC, 2, NP], BF16)
        cnt, cnt16, cntT = sb("cnt", [P, NP], F32), sb("cnt16", [P, NP], U16), sb("cntT", [P, NT, P], F32)
        deg, rdeg = sb("deg", [P, 1], F32), sb("rdeg", [P, 1], F32)
        xt, aggT = sb("xt", [P, KC, P], F32), sb("aggT", [P, KC, P], F32)
        h, h2, h3 = sb("h", [P, D], F32), sb("h2", [P, D], F32), sb("h3", [P, D], F32)
        stats, mv, rstd = sb("g_stats", [P, 6], F32), sb("g_mv", [P, 2], F32), sb("g_rstd", [P, 1], F32)
        root = sb("g_root", [P, 1], F32)
        psC, psT, psA, psH = ps("psC", [P, 3 * D]), ps("psCT", [P, 2, D]), ps("psA", [P, KC, P]), ps("psH", [P, 2, D])
        names = ("edges_in", "w", "const", "zero", "edge_f", "ends", "tr", "edges", "bounds", "hot", "hot_free", "cnt",
                 "cnt_out", "cnt16", "stored", "xt", "hs", "ctT", "ct_out", "agg", "agg_out", "hn", "x1", "moments", "root")
        s = {n: c.sem("g_" + n) for n in names}
        block = st.enter_context(nc.Block())

        @block.sync
        def _(sp):
            sp.dma_start(edge_i[:, 0, :], ins["src"].rearrange("(g e) -> g e", g=NG)).then_inc(s["edges_in"], 16)
            sp.dma_start(edge_i[:, 1, :], ins["dst"].rearrange("(g e) -> g e", g=NG)).then_inc(s["edges_in"], 16)
            sp.dma_start(ws[:, :, :], ins["W_selfT"].rearrange("(k p) n -> p k n", p=P)).then_inc(s["w"], 16)
            sp.dma_start(wn[:, :, :], ins["W_neighT"].rearrange("(k p) n -> p k n", p=P)).then_inc(s["w"], 16)
            for dst, name in ((bias, "bias"), (gamma, "gamma"), (beta, "beta")):
                sp.dma_start(dst[:, :], ins[name].partition_broadcast(P)).then_inc(s["w"], 16)
            with sp.Fori(0, NT) as t:
                sp.wait_ge(s["cnt16"], t + 1)
                sp.dma_start(c.counts[bass.ds(t, 1), :, :].rearrange("a p n -> p (a n)"), cnt16[:, :]).then_inc(s["stored"], 16)
            sp.wait_ge(s["stored"], 16 * NT)

        @block.gpsimd
        def _(pool):
            pool.memset(zero[:, :], 0.0).then_inc(s["zero"], 1)
            pool.iota(group_i[:, :], pattern=[[1, NG]], base=0, channel_multiplier=0).then_inc(s["const"], 1)
            pool.iota(tile_i[:, :], pattern=[[P, NT]], base=0, channel_multiplier=0).then_inc(s["const"], 1)
            pool.iota(node_i[:, :], pattern=[[1, NP]], base=0, channel_multiplier=0).then_inc(s["const"], 1)
            pool.wait_ge(s["const"], 3)
            pool.tensor_copy(group_id[:, :], group_i[:, :]).then_inc(s["const"], 1)
            pool.tensor_copy(tile_lo[:, :], tile_i[:, :]).then_inc(s["const"], 1)
            pool.tensor_copy(node_id[:, :], node_i[:, :]).then_inc(s["const"], 1)
            with pool.Fori(0, NT) as t:
                pool.wait_ge(s["cnt_out"], t + 1)
                wait_alone(c, pool, s["stored"], 16 * t)
                pool.tensor_copy(cnt16[:, :], cnt[:, :]).then_inc(s["cnt16"], 1)

        @block.vector
        def _(dve):
            dve.wait_ge(s["edges_in"], 32)
            dve.tensor_copy(edge_f[:, :, :], edge_i[:, :, :]).then_inc(s["edge_f"], 1)
            dve.drain()
            dve.tensor_reduce(ends[:, 0:1], edge_f[:, 1, :], AX, ALU.min)
            dve.tensor_reduce(ends[:, 1:2], edge_f[:, 1, :], AX, ALU.max).then_inc(s["ends"], 1)
            dve.wait_ge(s["tr"], 1)
            dve.tensor_copy(edges[:, :, 0:NG], psT[0:EC, 0, 0:4 * NG].rearrange("p (a g) -> p a g", a=4)).then_inc(s["edges"], 1)
            r = [row[0:1, i, :].rearrange("p (t g) -> p t g", t=NT) for i in range(6)]
            lowest = row[0:1, 4, 0:NG].unsqueeze(1).to_broadcast([1, NT, NG])
            highest = row[0:1, 5, 0:NG].unsqueeze(1).to_broadcast([1, NT, NG])
            gid = group_id[0:1, :].unsqueeze(1).to_broadcast([1, NT, NG])
            dve.tensor_copy(row[0:1, 4, 0:NG], psT[0:1, 1, 0:NG])
            dve.tensor_copy(row[0:1, 5, 0:NG], psT[0:1, 1, NG:2 * NG])
            dve.wait_ge(s["const"], 6)
            dve.tensor_scalar(tile_hi[:, :], tile_lo[:, :], float(P - 1), None, ALU.add)
            dve.drain()
            dve.tensor_tensor(r[0], highest, tile_lo[0:1, :].unsqueeze(2).to_broadcast([1, NT, NG]), ALU.is_ge)
            dve.tensor_tensor(r[1], tile_hi[0:1, :].unsqueeze(2).to_broadcast([1, NT, NG]), lowest, ALU.is_ge)
            dve.drain()
            dve.tensor_tensor(r[2], r[0], r[1], ALU.mult)
            dve.drain()
            dve.scalar_tensor_tensor(out=r[0], in0=r[2], scalar=-1000.0, in1=gid, op0=ALU.mult, op1=ALU.add)
            dve.scalar_tensor_tensor(out=r[1], in0=gid, scalar=1.0, in1=r[2], op0=ALU.add, op1=ALU.mult)
            dve.drain()
            dve.tensor_reduce(bounds_f[:, 0, :], r[0], AX, ALU.min)
            dve.tensor_reduce(bounds_f[:, 1, :], r[1], AX, ALU.max)
            dve.drain()
            dve.tensor_scalar(bounds_f[:, 2, :], bounds_f[:, 0, :], 0.0, 1000.0, ALU.is_lt, ALU.mult)
            dve.drain()
            dve.tensor_tensor(bounds_f[:, 0, :], bounds_f[:, 0, :], bounds_f[:, 2, :], ALU.add)
            dve.drain()
            dve.tensor_tensor(bounds_f[:, 3, :], bounds_f[:, 1, :], bounds_f[:, 0, :], ALU.subtract)
            dve.drain()
            dve.tensor_scalar(bounds[:, NT:2 * NT], bounds_f[:, 3, :], 1.0, None, ALU.max)
            dve.tensor_copy(bounds[:, 0:NT], bounds_f[:, 0, :]).then_inc(s["bounds"], 1)
            dve.wait_ge(s["bounds"], 1)
            dve.wait_ge(s["w"], 80)
            dve.tensor_tensor(beta[:, :], beta[:, :], mean_row[:, :], ALU.add)
            done = dve.alloc_register("groups_done")
            dve.reg_mov(done, 0)
            with dve.Fori(0, NT) as t:
                first = dve.value_load(bounds[0:1, bass.ds(t, 1)], min_val=0, max_val=NG - 1)
                many = dve.value_load(bounds[0:1, bass.ds(t + NT, 1)], min_val=1, max_val=NG)
                before = dve.snap(done)
                dve.tensor_scalar(shifted[:, :, 0:NG], edges[:, 2:4, 0:NG], tile_lo[0:EC, bass.ds(t, 1)], None, ALU.subtract)
                dve.drain()
                with dve.Fori(0, many) as i:
                    for j in range(2):
                        dve.wait_ge(s["hot_free"], (before + i) * 2 + (j + 1))
                        dve.tensor_scalar(hot_dst[:, j, :], node_id[0:EC, 0:P], shifted[:, j, bass.ds(first + i, 1)],
                                          None, ALU.is_equal)
                        dve.tensor_scalar(hot_src[:, j, :], node_id[0:EC, :], edges[:, j, bass.ds(first + i, 1)],
                                          None, ALU.is_equal).then_inc(s["hot"], 1)
                dve.reg_add(done, done, many)
                dve.wait_ge(s["cnt_out"], t + 1)
                dve.tensor_scalar(rdeg[:, :], deg[:, :], 1.0, None, ALU.max)
                dve.drain()
                dve.reciprocal(rdeg[:, :], rdeg[:, :])
                dve.wait_ge(s["hs"], t + 1)
                dve.tensor_tensor(h[:, :], psH[:, 0, :], bias[:, :], ALU.add)
                dve.drain()
                dve.wait_ge(s["hn"], t + 1)
                dve.scalar_tensor_tensor(out=h2[:, :], in0=psT[:, 1, :], scalar=rdeg[:, 0:1], in1=h[:, :],
                                         op0=ALU.mult, op1=ALU.add)
                dve.drain()
                dve.bn_stats(stats[:, :], h2[:, :])
                dve.drain()
                dve.bn_aggr(mv[:, :], stats[:, :])
                dve.drain()
                dve.tensor_scalar(rstd[:, :], mv[:, 1:2], EPS, None, ALU.add).then_inc(s["moments"], 1)
                dve.wait_ge(s["root"], t + 1)
                dve.reciprocal(rstd[:, :], root[:, :])
                dve.drain()
                dve.tensor_scalar(h[:, :], h2[:, :], mv[:, 0:1], rstd[:, 0:1], ALU.subtract, ALU.mult)
                dve.drain()
                dve.tensor_tensor(h2[:, :], h[:, :], gamma[:, :], ALU.mult)
                dve.tensor_tensor(h3[:, :], psH[:, 1, :], beta[:, :], ALU.add)
                dve.drain()
                dve.tensor_tensor(h2[:, :], h2[:, :], h3[:, :], ALU.add)
                dve.drain()
                dve.tensor_tensor(c.x[:, bass.ds(t, 1), :], c.x[:, bass.ds(t, 1), :],
                                  h2[:, :].unsqueeze(1), ALU.add).then_inc(s["x1"], 1)

        @block.scalar
        def _(act):
            with act.Fori(0, NT) as t:
                wait_alone(c, act, s["hs"], t)
                act.activation(xt[:, :, :], c.xnT[:, :, column(t)], ACT.Copy).then_inc(s["xt"], 1)
                act.wait_ge(s["cnt"], t + 1)
                act.wait_ge(s["ctT"], 3 * t)
                act.wait_ge(s["cnt16"], t)
                act.wait_ge(s["x1"], t)
                act.activation(cnt[:, :], psC[:, 0:NP], ACT.Copy, accum_out=deg[:, 0:1]).then_inc(s["cnt_out"], 1)
                act.wait_ge(s["agg"], t)
                for g in range(3):
                    n = min(4, NT - 4 * g)
                    act.wait_ge(s["ctT"], 3 * t + (g + 1))
                    act.activation(cntT[:, 4 * g:4 * g + n, :], psT[:, g % 2, 0:n * P].rearrange("p (a n) -> p a n", a=n),
                                   ACT.Copy).then_inc(s["ct_out"], 1)
                act.wait_ge(s["agg"], t + 1)
                act.wait_ge(s["hn"], t)
                act.activation(aggT[:, :, :], psA[:, :, :], ACT.Copy).then_inc(s["agg_out"], 1)
                act.wait_ge(s["moments"], t + 1)
                act.activation(root[:, :], rstd[:, :], ACT.Sqrt).then_inc(s["root"], 1)

        @block.tensor
        def _(pe):
            pe.wait_ge(s["edge_f"], 1)
            for a in range(4):
                pe.transpose(psT[0:EC, 0, a * NG:(a + 1) * NG], edge_f[:, a // 2, a % 2 * EC:(a % 2 + 1) * EC],
                             c.ident[0:NG, 0:NG])
            pe.wait_ge(s["ends"], 1)
            for a in range(2):
                mm = pe.matmul(psT[0:1, 1, a * NG:(a + 1) * NG], ends[:, a:a + 1], c.ident[0:NG, 0:NG], start=True, stop=True)
            mm.then_inc(s["tr"], 1)
            pe.wait_ge(s["zero"], 1)
            pe.wait_ge(s["w"], 80)
            pe.sem_inc(s["hot_free"], 2)
            pe.wait_ge(s["bounds"], 1)
            done = pe.alloc_register("groups_done")
            pe.reg_mov(done, 0)
            with pe.Fori(0, NT) as t:
                many = pe.value_load(bounds[0:1, bass.ds(t + NT, 1)], min_val=1, max_val=NG)
                before = pe.snap(done)
                pe.wait_ge(s["cnt_out"], t)
                for a, n in CHUNKS:
                    pe.matmul(psC[:, a:a + n], zero[:, 0:P], zero[:, 0:n], start=True, stop=True, skip_group_check=True)
                with pe.Fori(0, many) as i:
                    for j in range(2):
                        pe.wait_ge(s["hot"], (before + i) * 2 + (j + 1))
                        for a, n in CHUNKS:
                            mm = pe.matmul(psC[:, a:a + n], hot_dst[:, j, :], hot_src[:, j, a:a + n], start=False,
                                           stop=True, skip_group_check=True)
                        mm.then_inc(s["hot_free"], 1)
                pe.reg_add(done, done, many)
                pe.matmul(psC[:, 0:P], zero[:, 0:P], zero[:, 0:P], start=False, stop=True,
                          skip_group_check=True).then_inc(s["cnt"], 1)
                pe.wait_ge(s["xt"], t + 1)
                pe.wait_ge(s["x1"], t)
                for i, w in enumerate((ws, kv)):
                    for k in range(KC):
                        mm = pe.matmul(psH[:, i, :], xt[:, k, :], w[:, k, :], start=k == 0, stop=k == KC - 1)
                mm.then_inc(s["hs"], 1)
                pe.wait_ge(s["cnt_out"], t + 1)
                for g in range(3):
                    if g == 2:
                        pe.wait_ge(s["ct_out"], 3 * t + 1)
                    for a in range(4 * g, min(4 * g + 4, NT)):
                        mm = pe.transpose(psT[:, g % 2, a % 4 * P:(a % 4 + 1) * P], cnt[:, a * P:(a + 1) * P], c.ident[:, :])
                    mm.then_inc(s["ctT"], 1)
                pe.wait_ge(s["ct_out"], 3 * t + 3)
                pe.wait_ge(s["agg_out"], t)
                for f in range(KC):
                    for a in range(NT):
                        mm = pe.matmul(psA[:, f, :], xn[:, a, f * P:(f + 1) * P], cntT[:, a, :], start=a == 0, stop=a == NT - 1)
                mm.then_inc(s["agg"], 1)
                pe.wait_ge(s["agg_out"], t + 1)
                for k in range(KC):
                    mm = pe.matmul(psT[:, 1, :], aggT[:, k, :], wn[:, k, :], start=k == 0, stop=k == KC - 1)
                mm.then_inc(s["hn"], 1)


RING = 16
AHEAD = RING // TOPK


def stage_memory(c):
    nc, ins = c.nc, c.ins
    with ExitStack() as st:
        sb = lambda n, s, d=F32: st.enter_context(nc.sbuf_tensor("m_" + n, s, d))
        ps = lambda n, s: st.enter_context(nc.psum_tensor("m_" + n, s, F32))
        norm = RowStats(c, st, "m_")
        ring = sb("ring", [P, RING, 2 * D])
        wq, bq, keys = sb("wq", [P, KC, HEADS * P]), sb("bq", [P, HEADS]), sb("keys", [P, HEADS, 2 * NKEYS])
        coming, current, xT = sb("coming", [P, D]), sb("current", [P, D]), sb("xT", [P, KC, P])
        qT = sb("qT", [P, HEADS, P])
        product = sb("product", [P, D])
        diag = sb("diag", [P, AHEAD * TOPK, P])
        top, top_at, top_id = sb("top", [P, 2, TOPK]), sb("top_at", [P, 2, TOPK], U32), sb("top_id", [P, 2, TOPK])
        pairs, best = sb("pairs", [P, TOPK, TOPK]), sb("best", [P, HEADS, TOPK])
        best_at, side, side_f = sb("best_at", [P, TOPK], U32), sb("side", [P, 2, TOPK], U32), sb("side_f", [P, 2, TOPK])
        pick, chosen = sb("pick", [P, 2, TOPK, TOPK]), sb("chosen", [P, 2, TOPK])
        number_i, number = sb("number_i", [P, TOPK], I32), sb("number", [P, TOPK])
        rows_at = sb("rows_at", [P, HEADS, TOPK], U32)
        lowest, expo, total = sb("lowest", [P, HEADS]), sb("expo", [P, HEADS, TOPK]), sb("total", [P, HEADS])
        inner, share, rtotal = sb("inner", [P, TOPK]), sb("share", [P, TOPK]), sb("rtotal", [P, 1])
        weight = sb("weight", [P, AHEAD, TOPK])
        psT, psQ, psS, acc = ps("psT", [P, D]), ps("psQ", [P, 2, D]), ps("psS", [P, 2, D]), ps("acc", [P, D])
        names = ("w", "keys0", "number0", "number", "coming", "tr", "xT", "q", "qT", "score", "found", "soft", "weight",
                 "diag", "slot_free", "x2")
        s = {n: c.sem("m_" + n) for n in names}
        s_land = [c.sem(f"m_landed{i}") for i in range(RING)]
        block = st.enter_context(nc.Block())

        @block.sync
        def _(sp):
            sp.dma_start(wq[:, :, :], ins["Wq"].rearrange("(k p) n -> p k n", p=P)).then_inc(s["w"], 16)
            sp.dma_start(bq[:, :], ins["bqT"]).then_inc(s["w"], 16)
            sp.wait_ge(s["keys0"], 1)
            for i in range(2):
                sp.dma_start(keys[64 * i:64 * i + 64, :, NKEYS * i:NKEYS * (i + 1)], ins["keysT"][i]).then_inc(s["w"], 16)

        @block.gpsimd
        def _(pool):
            pool.memset(keys[:, :, :], 0.0).then_inc(s["keys0"], 1)
            pool.iota(number_i[:, :], pattern=[[1, TOPK]], base=0, channel_multiplier=0).then_inc(s["number0"], 1)
            pool.wait_ge(s["number0"], 1)
            pool.tensor_copy(number[:, :], number_i[:, :]).then_inc(s["number"], 1)
            with pool.Fori(0, NT) as t:
                for h in range(HEADS):
                    pool.wait_ge(s["found"], t * HEADS + (h + 1))
                    for k in range(TOPK):
                        slot = (h * TOPK + k) % RING
                        wait_alone(c, pool, s["slot_free"], t * (HEADS * TOPK) + (h * TOPK + k + 1))
                        pool.indirect_dma_start(ring[:, slot, :], None, ins["table"],
                                                bass.IndirectOffsetOnAxis(rows_at[:, h, k:k + 1], 0)).then_inc(s_land[slot], 16)

        def search(dve, h, nth):
            wait_alone(c, dve, s["score"], nth + 1)
            b = h % 2
            for i in range(2):
                dve.max(top[:, i, :], psS[:, b, NKEYS * i:NKEYS * (i + 1)])
            dve.drain()
            for i in range(2):
                dve.max_index(top_at[:, i, :], top[:, i, :], psS[:, b, NKEYS * i:NKEYS * (i + 1)])
            dve.tensor_tensor(pairs[:, :, :], top[:, 0, :].unsqueeze(2).to_broadcast([P, TOPK, TOPK]),
                              top[:, 1, :].unsqueeze(1).to_broadcast([P, TOPK, TOPK]), ALU.add)
            dve.drain()
            dve.tensor_copy(top_id[:, :, :], top_at[:, :, :])
            dve.max(best[:, h, :], pairs[:, :, :].rearrange("p a b -> p (a b)"))
            dve.drain()
            dve.max_index(best_at[:, :], best[:, h, :], pairs[:, :, :].rearrange("p a b -> p (a b)"))
            dve.tensor_scalar(lowest[:, h:h + 1], best[:, h, 0:1], -1.0, None, ALU.mult)
            dve.drain()
            dve.tensor_scalar(side[:, 0, :], best_at[:, :], 3, None, ALU.logical_shift_right)
            dve.tensor_scalar(side[:, 1, :], best_at[:, :], TOPK - 1, None, ALU.bitwise_and)
            dve.drain()
            dve.tensor_copy(side_f[:, :, :], side[:, :, :])
            dve.drain()
            dve.tensor_tensor(pick[:, :, :, :], side_f[:, :, :].unsqueeze(3).to_broadcast([P, 2, TOPK, TOPK]),
                              number[:, :].unsqueeze(1).unsqueeze(1).to_broadcast([P, 2, TOPK, TOPK]), ALU.is_equal)
            dve.drain()
            dve.tensor_tensor(pick[:, :, :, :], pick[:, :, :, :],
                              top_id[:, :, :].unsqueeze(2).to_broadcast([P, 2, TOPK, TOPK]), ALU.mult)
            dve.drain()
            dve.tensor_reduce(chosen[:, :, :], pick[:, :, :, :], AX, ALU.add)
            dve.drain()
            dve.scalar_tensor_tensor(out=rows_at[:, h, :], in0=chosen[:, 0, :], scalar=float(NKEYS), in1=chosen[:, 1, :],
                                     op0=ALU.mult, op1=ALU.add).then_inc(s["found"], 1)

        def use(dve, h, nth, t):
            dve.wait_ge(s["soft"], nth + 1)
            dve.reciprocal(rtotal[:, :], total[:, h:h + 1])
            for k in range(TOPK):
                slot = (h * TOPK + k) % RING
                if k:
                    dve.drain()
                dve.wait_ge(s_land[slot], (t * (HEADS // AHEAD) + (h // AHEAD + 1)) * 16)
                dve.tensor_tensor_reduce(product[:, :], ring[:, slot, 0:D], current[:, :], 1.0, 0.0, ALU.mult, ALU.add,
                                         inner[:, k:k + 1])
            dve.tensor_scalar(share[:, :], expo[:, h, :], rtotal[:, 0:1], None, ALU.mult)
            dve.drain()
            dve.scalar_tensor_tensor(out=weight[:, h % AHEAD, :], in0=inner[:, :], scalar=0.0, in1=share[:, :],
                                     op0=ALU.max, op1=ALU.mult).then_inc(s["weight"], 1)
            dve.drain()

        @block.vector
        def _(dve):
            norm.moments(dve)
            norm.normalise(dve, 0, coming[:, :]).then_inc(s["coming"], 1)
            dve.wait_ge(s["number"], 1)
            for h in range(HEADS):
                search(dve, h, h)

            def tile(t, last):
                dve.drain()
                dve.tensor_copy(current[:, :], coming[:, :])
                dve.drain()
                if not last:
                    norm.normalise(dve, t + 1, coming[:, :]).then_inc(s["coming"], 1)
                for h in range(HEADS):
                    use(dve, h, t * HEADS + h, t)
                    if not last:
                        search(dve, h, t * HEADS + (HEADS + h))
                dve.wait_ge(s["slot_free"], (t + 1) * (HEADS * TOPK) + RING)
                dve.tensor_tensor(c.x[:, bass.ds(t, 1), :], c.x[:, bass.ds(t, 1), :], acc[:, :].unsqueeze(1),
                                  ALU.add).then_inc(s["x2"], 1)

            with dve.Fori(0, NT - 1) as t:
                tile(t, False)
            tile(NT - 1, True)

        def queries(act, nth):
            act.wait_ge(s["tr"], nth + 1)
            act.activation(xT[:, :, :], psT[:, :].rearrange("p (k n) -> p k n", k=KC), ACT.Copy).then_inc(s["xT"], 1)
            for h in range(HEADS):
                if h % 4 == 0:
                    act.wait_ge(s["q"], nth * 2 + (h // 4 + 1))
                act.activation(qT[:, h, :], psQ[:, h // 4, h % 4 * P:(h % 4 + 1) * P], ACT.Identity,
                               bias=bq[:, h:h + 1]).then_inc(s["qT"], 1)

        def soften(act, h, nth):
            act.wait_ge(s["found"], nth + 1)
            act.activation(expo[:, h, :], best[:, h, :], ACT.Exp, bias=lowest[:, h:h + 1],
                           accum_out=total[:, h:h + 1]).then_inc(s["soft"], 1)

        @block.scalar
        def _(act):
            norm.roots(act)
            act.wait_ge(s["w"], 64)
            queries(act, 0)
            for h in range(HEADS):
                soften(act, h, h)

            def tile(t, last):
                if not last:
                    queries(act, t + 1)
                for h in range(HEADS):
                    act.wait_ge(s["weight"], t * HEADS + (h + 1))
                    act.wait_ge(s["slot_free"], t * (HEADS * TOPK) + (h + 1) * TOPK)
                    for k in range(TOPK):
                        act.activation(diag[:, h % AHEAD * TOPK + k, :], c.ident[:, :], ACT.Copy,
                                       scale=weight[:, h % AHEAD, k:k + 1]).then_inc(s["diag"], 1)
                    if not last:
                        soften(act, h, t * HEADS + (HEADS + h))

            with act.Fori(0, NT - 1) as t:
                tile(t, False)
            tile(NT - 1, True)

        def project(pe, nth, first):
            pe.wait_ge(s["coming"], nth + 1)
            for k in range(KC):
                mm = pe.transpose(psT[:, k * P:(k + 1) * P], coming[:, k * P:(k + 1) * P], c.ident[:, :])
            mm.then_inc(s["tr"], 1)
            pe.wait_ge(s["xT"], nth + 1)
            if not first:
                pe.wait_ge(s["qT"], nth * HEADS)
            for h in range(HEADS):
                for k in range(KC):
                    mm = pe.matmul(psQ[:, h // 4, h % 4 * P:(h % 4 + 1) * P], wq[:, k, h * P:(h + 1) * P], xT[:, k, :],
                                   start=k == 0, stop=k == KC - 1)
                if h % 4 == 3:
                    mm.then_inc(s["q"], 1)

        def scores(pe, h, nth, first):
            pe.wait_ge(s["qT"], nth + 1)
            if not (first and h < 2):
                pe.wait_ge(s["found"], nth - 1)
            pe.matmul(psS[:, h % 2, :], qT[:, h, :], keys[:, h, :], start=True, stop=True).then_inc(s["score"], 1)

        @block.tensor
        def _(pe):
            pe.wait_ge(s["w"], 64)
            pe.sem_inc(s["slot_free"], RING)
            project(pe, 0, True)
            for h in range(HEADS):
                scores(pe, h, h, True)

            def tile(t, last):
                if not last:
                    project(pe, t + 1, False)
                for h in range(HEADS):
                    if not last:
                        scores(pe, h, t * HEADS + (HEADS + h), False)
                    if h == 0:
                        pe.wait_ge(s["x2"], t)
                    for k in range(TOPK):
                        pe.wait_ge(s["diag"], t * (HEADS * TOPK) + (h * TOPK + k + 1))
                        pe.matmul(acc[:, :], diag[:, h % AHEAD * TOPK + k, :], ring[:, (h * TOPK + k) % RING, D:2 * D],
                                  start=h + k == 0, stop=h * TOPK + k == HEADS * TOPK - 1).then_inc(s["slot_free"], 1)

            with pe.Fori(0, NT - 1) as t:
                tile(t, False)
            tile(NT - 1, True)


PAIRS = HEADS // 2


def transposed_norm(c, tag):
    nc = c.nc
    with ExitStack() as st:
        norm = RowStats(c, st, tag)
        rows = st.enter_context(nc.sbuf_tensor(tag + "rows", [P, D], F32))
        psT = st.enter_context(nc.psum_tensor(tag + "psT", [P, D], F32))
        s_rows, s_tr, s_out = (c.sem(tag + n) for n in ("rows_ready", "turned", "stored"))
        block = st.enter_context(nc.Block())

        @block.vector
        def _(dve):
            norm.moments(dve)
            with dve.Fori(0, NT) as t:
                dve.wait_ge(s_tr, t)
                norm.normalise(dve, t, rows[:, :]).then_inc(s_rows, 1)

        @block.tensor
        def _(pe):
            with pe.Fori(0, NT) as t:
                pe.wait_ge(s_rows, t + 1)
                pe.wait_ge(s_out, t)
                for k in range(KC):
                    mm = pe.transpose(psT[:, k * P:(k + 1) * P], rows[:, k * P:(k + 1) * P], c.ident[:, :])
                mm.then_inc(s_tr, 1)

        @block.scalar
        def _(act):
            norm.roots(act)
            with act.Fori(0, NT) as t:
                wait_alone(c, act, s_tr, t + 1)
                act.activation(c.xnT[:, :, column(t)], psT[:, :].rearrange("p (k n) -> p k n", k=KC),
                               ACT.Copy).then_inc(s_out, 1)


def stage_token_mix(c, mix):
    nc, ins = c.nc, c.ins
    with ExitStack() as st:
        sb = lambda n, s, d=F32: st.enter_context(nc.sbuf_tensor("t_" + n, s, d))
        ps = lambda n, s: st.enter_context(nc.psum_tensor("t_" + n, s, F32))
        wqk, wv, wo = sb("wqk", [P, KC, 2 * D]), sb("wv", [P, KC, D]), sb("wo", [P, KC, D])
        q, k_rows = sb("q", [P, NT, D]), sb("k_rows", [P, NT, P])
        kT = sb("kT", [P, NP])
        low, ksum, rk = sb("low", [P, PAIRS]), sb("ksum", [P, PAIRS]), sb("rk", [P, PAIRS])
        qmax, qsum, qr = sb("qmax", [P, HEADS]), sb("qsum", [P, HEADS]), sb("qr", [P, HEADS])
        qe, qs = sb("qe", [P, 2, D]), sb("qs", [P, 2, D])
        kq, z = sb("kq", [P, PAIRS, P]), sb("z", [P, PAIRS, D])
        psQ, psK, psR, psM = ps("psQ", [P, 2, D]), ps("psK", [P, 3 * D]), ps("psR", [P, 2, D]), ps("psM", [P, D])
        names = ("w", "q", "qd", "qexp", "qout", "kq0", "k", "low", "kexp", "tr", "krows", "kq", "kqout", "z", "zout", "y", "yout",
                 "rk", "pad")
        s = {n: c.sem("t_" + n) for n in names}
        block = st.enter_context(nc.Block())

        @block.sync
        def _(sp):
            sp.dma_start(wqk[:, :, :], ins["mix_qkT"].rearrange("(k p) n -> p k n", p=P)).then_inc(s["w"], 16)
            sp.dma_start(wv[:, :, :], ins["mix_v"].rearrange("(k p) n -> p k n", p=P)).then_inc(s["w"], 16)
            sp.dma_start(wo[:, :, :], ins["mix_outT"].rearrange("(k p) n -> p k n", p=P)).then_inc(s["w"], 16)

        @block.gpsimd
        def _(pool):
            pool.memset(kq[:, :, :], 0.0).then_inc(s["kq0"], 1)
            pool.memset(kT[:, N:NP], 0.0).then_inc(s["pad"], 1)

        @block.tensor
        def _(pe):
            pe.wait_ge(s["w"], 48)
            for t in range(NT):
                if t >= 2:
                    pe.wait_ge(s["qd"], t - 1)
                for k in range(KC):
                    mm = pe.matmul(psQ[:, t % 2, :], c.xnT[:, k, t * P:(t + 1) * P], wqk[:, k, 0:D], start=k == 0, stop=k == KC - 1)
                mm.then_inc(s["q"], 1)
            for m in range(PAIRS):
                if m:
                    pe.wait_ge(s["kexp"], m)
                for a, n in CHUNKS:
                    for k in range(KC):
                        mm = pe.matmul(psK[:, a:a + n], wqk[:, k, D + m * P:D + (m + 1) * P], c.xnT[:, k, a:a + n],
                                       start=k == 0, stop=k == KC - 1)
                mm.then_inc(s["k"], 1)
                pe.wait_ge(s["kexp"], m + 1)
                for g in range(3):
                    if 3 * m + g >= 2:
                        pe.wait_ge(s["krows"], 3 * m + g - 1)
                    for a in range(4 * g, min(4 * g + 4, NT)):
                        mm = pe.transpose(psR[:, (3 * m + g) % 2, a % 4 * P:(a % 4 + 1) * P], kT[:, a * P:(a + 1) * P], c.ident[:, :])
                    mm.then_inc(s["tr"], 1)
                pe.wait_ge(s["qout"], NT)
                pe.wait_ge(s["krows"], 3 * m + 3)
                if m:
                    pe.wait_ge(s["kqout"], 2 * m)
                for t in range(NT):
                    mm = pe.matmul(psM[:, 0:P], k_rows[:, t, :], q[:, t, m * P:(m + 1) * P], start=t == 0, stop=t == NT - 1)
                mm.then_inc(s["kq"], 1)
            pe.wait_ge(s["kqout"], 2 * PAIRS)
            for m in range(PAIRS):
                if m >= 2:
                    pe.wait_ge(s["zout"], m - 1)
                pe.transpose(psM[:, 0:P], kq[:, m, :], c.ident[:, :]).then_inc(s["z"], 1)
                pe.wait_ge(s["zout"], 2 * m + 1)
                pe.matmul(psQ[:, m % 2, :], kT[:, 0:P], wo[:, m, :], start=True, stop=True).then_inc(s["z"], 1)
                pe.wait_ge(s["zout"], 2 * m + 2)
            for m in range(KC):
                if m >= 2:
                    pe.wait_ge(s["yout"], m - 1)
                for k in range(KC):
                    mm = pe.matmul(psQ[:, m % 2, :], wv[:, k, m * P:(m + 1) * P], z[:, k, :], start=k == 0, stop=k == KC - 1)
                mm.then_inc(s["y"], 1)

        def heads(ap):
            return ap.rearrange("p (h e) -> p h e", h=HEADS)

        @block.vector
        def _(dve):
            dve.wait_ge(s["kq0"], 1)
            dve.wait_ge(s["pad"], 1)
            for t in range(NT):
                b = t % 2
                dve.wait_ge(s["q"], t + 1)
                dve.tensor_reduce(qmax[:, :], heads(psQ[:, b, :]), AX, ALU.max)
                dve.drain()
                dve.tensor_tensor(heads(qs[:, b, :]), heads(psQ[:, b, :]), qmax[:, :].unsqueeze(2).to_broadcast([P, HEADS, D // HEADS]),
                                  ALU.subtract).then_inc(s["qd"], 1)
                dve.wait_ge(s["qexp"], t + 1)
                dve.tensor_reduce(qsum[:, :], heads(qe[:, b, :]), AX, ALU.add)
                dve.drain()
                dve.reciprocal(qr[:, :], qsum[:, :])
                dve.drain()
                dve.tensor_tensor(heads(q[:, t, :]), heads(qe[:, b, :]), qr[:, :].unsqueeze(2).to_broadcast([P, HEADS, D // HEADS]),
                                  ALU.mult).then_inc(s["qout"], 1)
                dve.drain()
            for m in range(PAIRS):
                dve.wait_ge(s["k"], m + 1)
                dve.tensor_reduce(low[:, m:m + 1], psK[:, 0:N], AX, ALU.max)
                dve.drain()
                dve.tensor_scalar(low[:, m:m + 1], low[:, m:m + 1], -1.0, None, ALU.mult).then_inc(s["low"], 1)
                dve.wait_ge(s["kexp"], m + 1)
                dve.reciprocal(rk[:, m:m + 1], ksum[:, m:m + 1]).then_inc(s["rk"], 1)
                dve.wait_ge(s["kq"], m + 1)
                dve.drain()
                for i in range(2):
                    a = slice(64 * i, 64 * i + 64)
                    dve.tensor_scalar(kq[a, m, a], psM[a, a], rk[a, m:m + 1], None, ALU.mult).then_inc(s["kqout"], 1)

        @block.scalar
        def _(act):
            for t in range(NT):
                act.wait_ge(s["qd"], t + 1)
                act.activation(qe[:, t % 2, :], qs[:, t % 2, :], ACT.Exp).then_inc(s["qexp"], 1)
            for m in range(PAIRS):
                act.wait_ge(s["low"], m + 1)
                if m:
                    act.wait_ge(s["tr"], 3 * m)
                act.activation(kT[:, 0:N], psK[:, 0:N], ACT.Exp, bias=low[:, m:m + 1],
                               accum_out=ksum[:, m:m + 1]).then_inc(s["kexp"], 1)
                for g in range(3):
                    n = min(4, NT - 4 * g)
                    act.wait_ge(s["tr"], 3 * m + g + 1)
                    if m:
                        act.wait_ge(s["kq"], m)
                    act.activation(k_rows[:, 4 * g:4 * g + n, :], psR[:, (3 * m + g) % 2, 0:n * P].rearrange("p (a n) -> p a n", a=n),
                                   ACT.Copy).then_inc(s["krows"], 1)
            for m in range(PAIRS):
                act.wait_ge(s["z"], 2 * m + 1)
                act.activation(kT[:, 0:P], psM[:, 0:P], ACT.Copy).then_inc(s["zout"], 1)
                act.wait_ge(s["z"], 2 * m + 2)
                act.activation(z[:, m, :], psQ[:, m % 2, :], ACT.Copy).then_inc(s["zout"], 1)
            for m in range(KC):
                act.wait_ge(s["y"], m + 1)
                act.activation(mix[:, m, :], psQ[:, m % 2, :], ACT.Copy).then_inc(s["yout"], 1)
            act.wait_ge(s["yout"], KC)


def stage_edge_attention(c, msg):
    nc, ins = c.nc, c.ins
    with ExitStack() as st:
        sb = lambda n, s, d=F32: st.enter_context(nc.sbuf_tensor("a_" + n, s, d))
        ps = lambda n, s: st.enter_context(nc.psum_tensor("a_" + n, s, F32))
        cnt, mask = sb("cnt", [P, 2, NP], U16), sb("mask", [P, 2, NP], BF16)
        w, bqk, bq8, bv = sb("w", [P, KC, 3, P]), sb("bqk", [P, 2 * PAIRS]), sb("bq8", [P, PAIRS]), sb("bv", [P, D])
        qz, kT, v = sb("qz", [P, 2, NP]), sb("kT", [P, NP]), sb("v", [P, NT, P])
        qt = sb("qt", [P, 2, P])
        prob, pT = sb("prob", [P, 2, NP]), sb("pT", [P, 2, NT, P])
        low, den, rden = sb("low", [P, 2]), sb("den", [P, 2]), sb("rden", [P, 2])
        junk = sb("junk", [P, N], BF16)
        psS, psT, psV = ps("psS", [P, 3 * D]), ps("psT", [P, 3 * D]), ps("psV", [P, 2, D])
        names = ("cnt0", "cnt1", "b", "bq8", "zero", "w", "q", "qout", "v", "vout", "k", "kout", "staged", "score", "low", "exp",
                 "weighed", "turned", "pT", "sums", "msg", "rden", "pad")
        s = {n: c.sem("a_" + n) for n in names}
        U = 2 * NT
        block = st.enter_context(nc.Block())

        @block.sync
        def _(sp):
            sp.dma_start(bqk[:, :], ins["b_qkT"]).then_inc(s["b"], 16)
            sp.dma_start(bv[:, :], ins["b_v"].partition_broadcast(P)).then_inc(s["b"], 16)
            wt = ins["W_qkvT"].rearrange("(k p) (a n) -> p k a n", p=P, a=3)
            with sp.Fori(0, PAIRS) as m:
                sp.wait_ge(s["v"], m * 3)
                for i in range(3):
                    sp.dma_start(w[:, :, i, :], wt[:, :, i, bass.ds(m * P, P)]).then_inc(s["w"], 16)
                with sp.Fori(0, NT // 2) as j:
                    for b in range(2):
                        sp.wait_ge(s["weighed"], m * U + j * 4 + (2 * b + 2))
                        sp.dma_start(cnt[:, b, :], c.counts[bass.ds(j * 2 + b, 1), :, :].rearrange("a p n -> p (a n)"))\
                          .then_inc(s[f"cnt{b}"], 16)

        @block.gpsimd
        def _(pool):
            pool.memset(qz[:, :, :], 0.0).then_inc(s["zero"], 1)
            pool.memset(prob[:, :, N:NP], 0.0).then_inc(s["pad"], 1)
            with pool.Fori(0, PAIRS) as m:
                wait_alone(c, pool, s["qout"], m * 2 + 2)
                with pool.Fori(0, NT) as t:
                    for h in range(2):
                        wait_alone(c, pool, s["score"], m * U + t * 2 + (h + 1))
                        pool.tensor_copy(qt[:, h, :], qz[:, h, column(t)]).then_inc(s["staged"], 1)

        @block.tensor
        def _(pe):
            pe.sem_inc(s["score"], 2)
            pe.sem_inc(s["sums"], 1)

            def score(n, h):
                pe.wait_ge(s["staged"], n + 1)
                pe.wait_ge(s["exp"], n)
                for a, width in CHUNKS:
                    mm = pe.matmul(psS[:, a:a + width], qt[:, h, :], kT[:, a:a + width], start=True, stop=True)
                mm.then_inc(s["score"], 1)

            def turn(n, h):
                pe.wait_ge(s["weighed"], n + 5)
                pe.wait_ge(s["pT"], n)
                for a in range(NT):
                    mm = pe.transpose(psT[:, a * P:(a + 1) * P], prob[:, h, a * P:(a + 1) * P], c.ident[:, :])
                mm.then_inc(s["turned"], 1)

            def sums(n, h):
                pe.wait_ge(s["pT"], n + 1)
                pe.wait_ge(s["msg"], n)
                for a in range(NT):
                    mm = pe.matmul(psV[:, h, 0:P], pT[:, h, a, :], v[:, a, :], start=a == 0, stop=a == NT - 1)
                mm.then_inc(s["sums"], 1)

            with pe.Fori(0, PAIRS) as m:
                pe.wait_ge(s["w"], m * 48 + 48)
                pe.wait_ge(s["exp"], m * U)
                pe.wait_ge(s["pT"], m * U)
                pe.wait_ge(s["msg"], m * U + 1)
                for i, dst in enumerate((psS, psT)):
                    for a, width in CHUNKS:
                        for k in range(KC):
                            mm = pe.matmul(dst[:, a:a + width], w[:, k, i, :], c.xnT[:, k, a:a + width],
                                           start=k == 0, stop=k == KC - 1)
                    mm.then_inc(s["qk"[i]], 1)
                for t in range(NT):
                    if t == 8:
                        pe.wait_ge(s["vout"], m * 3 + 1)
                    for k in range(KC):
                        mm = pe.matmul(psV[:, t // 4 % 2, t % 4 * P:(t % 4 + 1) * P], c.xnT[:, k, t * P:(t + 1) * P],
                                       w[:, k, 2, :], start=k == 0, stop=k == KC - 1)
                    if t in (3, 7, NT - 1):
                        mm.then_inc(s["v"], 1)
                pe.wait_ge(s["kout"], m + 1)
                pe.wait_ge(s["qout"], m * 2 + 2)
                pe.wait_ge(s["vout"], m * 3 + 3)
                score(m * U, 0)

                def tiles(j, first, last):
                    for i in range(4):
                        n, h = m * U + j * 4 + i, i % 2
                        if not (last and i == 3):
                            score(n + 1, 1 - h)
                        turn(n, h)
                        if not (first and i == 0):
                            sums(m * U + j * 4 + i - 1 if i else m * U + (j * 4 - 1), 1 - h)

                tiles(0, True, False)
                with pe.Fori(1, NT // 2 - 1) as j:
                    tiles(j, False, False)
                tiles(NT // 2 - 1, False, True)
                sums(m * U + (U - 1), 1)

        @block.vector
        def _(dve):
            dve.sem_inc(s["weighed"], 4)
            dve.wait_ge(s["b"], 32)
            dve.tensor_scalar(bq8[:, :], bqk[:, 0:PAIRS], 64 ** -0.5, None, ALU.mult).then_inc(s["bq8"], 1)
            dve.wait_ge(s["pad"], 1)
            with dve.Fori(0, PAIRS) as m:
                for g in range(3):
                    n = min(4, NT - 4 * g)
                    dve.wait_ge(s["v"], m * 3 + (g + 1))
                    dve.tensor_tensor(v[:, 4 * g:4 * g + n, :], psV[:, g % 2, 0:n * P].rearrange("p (a n) -> p a n", a=n),
                                      bv[:, bass.ds(m * P, P)].unsqueeze(1).to_broadcast([P, n, P]), ALU.add).then_inc(s["vout"], 1)
                with dve.Fori(0, NT // 2) as j:
                    for i in range(4):
                        n, b, h = m * U + j * 4 + i, i // 2, i % 2
                        if h == 0:
                            dve.wait_ge(s[f"cnt{b}"], (m * (NT // 2) + j + 1) * 16)
                            dve.tensor_scalar(mask[:, b, 0:N], cnt[:, b, 0:N], 0.0, NEG, ALU.is_equal, ALU.mult)
                            dve.drain()
                        wait_alone(c, dve, s["score"], n + 3)
                        dve.tensor_tensor_reduce(junk[:, :], psS[:, 0:N], mask[:, b, 0:N], -1.0, 3e38, ALU.add, ALU.min,
                                                 low[:, h:h + 1])
                        dve.drain()
                        dve.scalar_tensor_tensor(out=low[:, h:h + 1], in0=low[:, h:h + 1], scalar=-0.1 * NEG, in1=low[:, h:h + 1],
                                                 op0=ALU.is_lt, op1=ALU.mult).then_inc(s["low"], 1)
                        dve.wait_ge(s["exp"], n + 1)
                        dve.scalar_tensor_tensor(out=prob[:, h, 0:N], in0=prob[:, h, 0:N], scalar=1.0, in1=cnt[:, b, 0:N],
                                                 op0=ALU.min, op1=ALU.mult, accum_out=den[:, h:h + 1]).then_inc(s["weighed"], 1)
                        dve.drain()
                        dve.tensor_scalar(den[:, h:h + 1], den[:, h:h + 1], 1e-30, None, ALU.max)
                        dve.drain()
                        dve.wait_ge(s["msg"], n)
                        dve.reciprocal(rden[:, h:h + 1], den[:, h:h + 1]).then_inc(s["rden"], 1)

        @block.scalar
        def _(act):
            act.sem_inc(s["msg"], 1)
            act.wait_ge(s["bq8"], 1)
            act.wait_ge(s["zero"], 1)

            def exponent(n, h):
                act.wait_ge(s["low"], n + 1)
                act.activation(prob[:, h, 0:N], psS[:, 0:N], ACT.Exp, bias=low[:, h:h + 1]).then_inc(s["exp"], 1)

            def message(m, t, n, h):
                act.wait_ge(s["sums"], n + 2)
                wait_alone(c, act, s["rden"], n + 1)
                act.activation(msg[:, bass.ds(t, 1), bass.ds(m * P + 64 * h, 64)].rearrange("p a n -> p (a n)"),
                               psV[:, h, 64 * h:64 * h + 64], ACT.Copy, scale=rden[:, h:h + 1]).then_inc(s["msg"], 1)

            def keep_turned(n, h):
                act.wait_ge(s["turned"], n + 1)
                act.wait_ge(s["sums"], n)
                act.activation(pT[:, h, :, :], psT[:, 0:NP].rearrange("p (a n) -> p a n", a=NT), ACT.Copy).then_inc(s["pT"], 1)

            with act.Fori(0, PAIRS) as m:
                wait_alone(c, act, s["q"], m + 1)
                for h in range(2):
                    a = slice(64 * h, 64 * h + 64)
                    act.activation(qz[a, h, :], psS[a, 0:NP], ACT.Identity, bias=bq8[a, bass.ds(m, 1)],
                                   scale=64 ** -0.5).then_inc(s["qout"], 1)
                wait_alone(c, act, s["k"], m + 1)
                act.activation(kT[:, :], psT[:, 0:NP], ACT.Identity, bias=bqk[:, bass.ds(m + PAIRS, 1)]).then_inc(s["kout"], 1)

                def tile(t, first):
                    for h in range(2):
                        n = m * U + t * 2 + h
                        exponent(n, h)
                        if not first:
                            message(m, t - 1, m * U + (t - 1) * 2 + h, h)
                        keep_turned(n, h)

                tile(0, True)
                with act.Fori(1, NT) as t:
                    tile(t, False)
                for h in range(2):
                    message(m, NT - 1, m * U + (U - 2 + h), h)


def stage_join(c, msg, mix):
    nc, ins = c.nc, c.ins
    with ExitStack() as st:
        sb = lambda n, s, d=F32: st.enter_context(nc.sbuf_tensor("j_" + n, s, d))
        ps = lambda n, s: st.enter_context(nc.psum_tensor("j_" + n, s, F32))
        wff, bff, bout = sb("wff", [P, KC, D]), sb("bff", [P, D]), sb("bout", [P, D])
        xt, mt, mT, y = sb("xt", [P, KC, P]), sb("mt", [P, D]), sb("mT", [P, KC, P]), sb("y", [P, D])
        psT, psO = ps("psT", [P, D]), ps("psO", [P, D])
        s = {n: c.sem("j_" + n) for n in ("w", "bias", "mt", "xt", "turned", "mT", "out", "x3")}
        block = st.enter_context(nc.Block())

        @block.sync
        def _(sp):
            sp.dma_start(wff[:, :, :], ins["W_ffT"].rearrange("(k p) n -> p k n", p=P)).then_inc(s["w"], 16)
            for dst, name in ((bff, "b_ff"), (bout, "b_out")):
                sp.dma_start(dst[:, :], ins[name].partition_broadcast(P)).then_inc(s["w"], 16)

        @block.gpsimd
        def _(pool):
            with pool.Fori(0, NT) as t:
                wait_alone(c, pool, s["turned"], t)
                pool.tensor_copy(mt[:, :], msg[:, bass.ds(t, 1), :].rearrange("p a n -> p (a n)")).then_inc(s["mt"], 1)

        @block.scalar
        def _(act):
            with act.Fori(0, NT) as t:
                wait_alone(c, act, s["out"], t)
                act.activation(xt[:, :, :], c.xnT[:, :, column(t)], ACT.Copy).then_inc(s["xt"], 1)
                act.wait_ge(s["turned"], t + 1)
                act.activation(mT[:, :, :], psT[:, :].rearrange("p (k n) -> p k n", k=KC), ACT.Copy).then_inc(s["mT"], 1)

        @block.tensor
        def _(pe):
            pe.wait_ge(s["w"], 48)
            with pe.Fori(0, NT) as t:
                pe.wait_ge(s["mt"], t + 1)
                pe.wait_ge(s["mT"], t)
                for k in range(KC):
                    mm = pe.transpose(psT[:, k * P:(k + 1) * P], mt[:, k * P:(k + 1) * P], c.ident[:, :])
                mm.then_inc(s["turned"], 1)
                pe.wait_ge(s["xt"], t + 1)
                pe.wait_ge(s["x3"], t)
                for k in range(KC):
                    pe.matmul(psO[:, :], xt[:, k, :], mix[:, k, :], start=k == 0, stop=False)
                pe.wait_ge(s["mT"], t + 1)
                for k in range(KC):
                    mm = pe.matmul(psO[:, :], mT[:, k, :], wff[:, k, :], start=False, stop=k == KC - 1)
                mm.then_inc(s["out"], 1)

        @block.vector
        def _(dve):
            dve.wait_ge(s["w"], 48)
            dve.tensor_tensor(bff[:, :], bff[:, :], bout[:, :], ALU.add)
            with dve.Fori(0, NT) as t:
                dve.drain()
                dve.wait_ge(s["out"], t + 1)
                dve.tensor_tensor(y[:, :], psO[:, :], bff[:, :], ALU.add)
                dve.drain()
                dve.tensor_tensor(c.x[:, bass.ds(t, 1), :], c.x[:, bass.ds(t, 1), :], y[:, :].unsqueeze(1),
                                  ALU.add).then_inc(s["x3"], 1)


def stage_attention(c):
    with ExitStack() as st:
        mix = st.enter_context(c.nc.sbuf_tensor("mix", [P, KC, D], F32))
        transposed_norm(c, "n3_")
        c.end_stage()
        stage_token_mix(c, mix)
        c.end_stage()
        msg = st.enter_context(c.nc.sbuf_tensor("msg", [P, NT, D], F32))
        stage_edge_attention(c, msg)
        c.end_stage()
        stage_join(c, msg, mix)
        c.end_stage()


UPS = [(0, 512), (512, 512), (1024, N - 1024)]


def rows_of(t):
    return P if t < NT - 1 else TAIL


def stage_gate(c, comb):
    nc, ins = c.nc, c.ins
    with ExitStack() as st:
        sb = lambda n, s, d=F32: st.enter_context(nc.sbuf_tensor("r_" + n, s, d))
        ps = lambda n, s: st.enter_context(nc.psum_tensor("r_" + n, s, F32))
        gw1, gw2, gb1, gb2, be2 = sb("gw1", [P, KC, 2 * P]), sb("gw2", [P, 2, EXP]), sb("gb1", [P, 2]), sb("gb2", [P, EXP]), sb("be2", [EXP, D])
        gT = sb("gT", [P, 2, NP])
        logit, expo, gate = sb("logit", [P, NT, EXP]), sb("expo", [P, NT, EXP]), sb("gate", [P, NT, EXP])
        peak, total, top, top_at = sb("peak", [P, NT]), sb("total", [P, NT]), sb("top", [P, NT, 8]), sb("top_at", [P, NT, 8], U32)
        at, expert_i, expert = sb("at", [P, NT, 8]), sb("expert_i", [P, EXP], I32), sb("expert", [P, EXP])
        gap, second, first, hit = sb("gap", [P, NT]), sb("second", [P, NT]), sb("first", [P, NT]), sb("hit", [P, 2, NT, EXP])
        combT = sb("combT", [EXP, NT, P])
        psG, psL, psC, psB = ps("psG", [P, 2, D]), ps("psL", [P, NT, EXP]), ps("psC", [EXP, 3, D]), ps("psB", [P, 2, D])
        s = {n: c.sem("r_" + n) for n in ("w", "iota", "expert", "hidden", "relu", "logits", "shifted", "exp", "gap", "exp2", "comb",
                                          "turned", "combT", "bias", "x")}
        block = st.enter_context(nc.Block())

        def wide(ap):
            return ap.unsqueeze(2).to_broadcast([P, NT, EXP])

        @block.sync
        def _(sp):
            sp.dma_start(gw1[:, :, :], ins["gw1"].rearrange("(k p) n -> p k n", p=P)).then_inc(s["w"], 16)
            sp.dma_start(gw2[:, :, :], ins["gw2"].rearrange("(k p) n -> p k n", p=P)).then_inc(s["w"], 16)
            sp.dma_start(gb1[:, :], ins["gb1T"]).then_inc(s["w"], 16)
            sp.dma_start(gb2[:, :], ins["gb2"].partition_broadcast(P)).then_inc(s["w"], 16)
            sp.dma_start(be2[:, :], ins["be2"]).then_inc(s["w"], 16)

        @block.gpsimd
        def _(pool):
            pool.iota(expert_i[:, :], pattern=[[1, EXP]], base=0, channel_multiplier=0).then_inc(s["iota"], 1)
            pool.wait_ge(s["iota"], 1)
            pool.tensor_copy(expert[:, :], expert_i[:, :]).then_inc(s["expert"], 1)

        @block.tensor
        def _(pe):
            pe.wait_ge(s["w"], 80)
            for m in range(2):
                for i, (a, n) in enumerate(CHUNKS):
                    u = 3 * m + i
                    if u >= 2:
                        pe.wait_ge(s["relu"], u - 1)
                    for k in range(KC):
                        mm = pe.matmul(psG[:, u % 2, 0:n], gw1[:, k, m * P:(m + 1) * P], c.xnT[:, k, a:a + n],
                                       start=k == 0, stop=k == KC - 1)
                    mm.then_inc(s["hidden"], 1)
            pe.wait_ge(s["relu"], 6)
            for t in range(NT):
                for m in range(2):
                    mm = pe.matmul(psL[:, t, :], gT[:, m, t * P:(t + 1) * P], gw2[:, m, :], start=m == 0, stop=m == 1)
            mm.then_inc(s["logits"], 1)
            pe.wait_ge(s["comb"], 1)
            for t in range(NT):
                mm = pe.transpose(psC[:, t // 4, t % 4 * P:(t % 4 + 1) * P], comb[:, t, :], c.ident[:, :])
            mm.then_inc(s["turned"], 1)
            pe.wait_ge(s["combT"], 1)
            for t in range(NT):
                if t >= 2:
                    pe.wait_ge(s["x"], t - 1)
                pe.matmul(psB[:, t % 2, :], combT[:, t, :], be2[:, :], start=True, stop=True).then_inc(s["bias"], 1)

        @block.scalar
        def _(act):
            act.wait_ge(s["w"], 80)
            for m in range(2):
                for i, (a, n) in enumerate(CHUNKS):
                    u = 3 * m + i
                    act.wait_ge(s["hidden"], u + 1)
                    act.activation(gT[:, m, a:a + n], psG[:, u % 2, 0:n], ACT.Relu, bias=gb1[:, m:m + 1]).then_inc(s["relu"], 1)
            act.wait_ge(s["shifted"], 1)
            act.activation(expo[:, :, :], logit[:, :, :], ACT.Exp).then_inc(s["exp"], 1)
            act.wait_ge(s["gap"], 1)
            act.activation(second[:, :], gap[:, :], ACT.Exp).then_inc(s["exp2"], 1)
            act.wait_ge(s["turned"], 1)
            act.activation(combT[:, :, :], psC[:, :, :].rearrange("p a (b n) -> p (a b) n", n=P)[:, 0:NT, :],
                           ACT.Copy).then_inc(s["combT"], 1)

        @block.vector
        def _(dve):
            dve.wait_ge(s["w"], 80)
            dve.wait_ge(s["logits"], 1)
            dve.tensor_tensor(logit[:, :, :], psL[:, :, :], gb2[:, :].unsqueeze(1).to_broadcast([P, NT, EXP]), ALU.add)
            dve.drain()
            dve.tensor_reduce(peak[:, :], logit[:, :, :], AX, ALU.max)
            dve.drain()
            dve.tensor_tensor(logit[:, :, :], logit[:, :, :], wide(peak[:, :]), ALU.subtract).then_inc(s["shifted"], 1)
            dve.wait_ge(s["exp"], 1)
            dve.tensor_reduce(total[:, :], expo[:, :, :], AX, ALU.add)
            dve.drain()
            dve.reciprocal(peak[:, :], total[:, :])
            dve.drain()
            dve.tensor_tensor(gate[:, :, :], expo[:, :, :], wide(peak[:, :]), ALU.mult)
            dve.drain()
            for t in range(NT):
                dve.max(top[:, t, :], gate[:, t, :])
            dve.drain()
            for t in range(NT):
                dve.max_index(top_at[:, t, :], top[:, t, :], gate[:, t, :])
            dve.tensor_tensor(gap[:, :], top[:, :, 1], top[:, :, 0], ALU.subtract).then_inc(s["gap"], 1)
            dve.drain()
            dve.tensor_copy(at[:, :, :], top_at[:, :, :])
            dve.wait_ge(s["exp2"], 1)
            dve.tensor_scalar(first[:, :], second[:, :], 1.0, None, ALU.add)
            dve.drain()
            dve.reciprocal(gap[:, :], first[:, :])
            dve.drain()
            dve.tensor_tensor(second[:, :], second[:, :], gap[:, :], ALU.mult)
            dve.wait_ge(s["expert"], 1)
            ids = expert[:, :].unsqueeze(1).to_broadcast([P, NT, EXP])
            for i in range(2):
                dve.tensor_tensor(hit[:, i, :, :], wide(at[:, :, i]), ids, ALU.is_equal)
            dve.drain()
            for i, share in enumerate((gap, second)):
                dve.tensor_tensor(hit[:, i, :, :], hit[:, i, :, :], wide(share[:, :]), ALU.mult)
            dve.drain()
            dve.tensor_tensor(comb[:, :, :], hit[:, 0, :, :], hit[:, 1, :, :], ALU.add).then_inc(s["comb"], 1)
            for t in range(NT):
                dve.wait_ge(s["bias"], t + 1)
                dve.tensor_tensor(c.x[:, t, :], c.x[:, t, :], psB[:, t % 2, :], ALU.add).then_inc(s["x"], 1)


def stage_expert_layers(c, comb):
    nc, ins = c.nc, c.ins
    with ExitStack() as st:
        sb = lambda n, s, d=F32: st.enter_context(nc.sbuf_tensor("e_" + n, s, d))
        ps = lambda n, s: st.enter_context(nc.psum_tensor("e_" + n, s, F32))
        w1, w2, be1 = sb("w1", [P, 2, KC, HID]), sb("w2", [P, 2, HC, D]), sb("be1", [P, EXP * HC])
        hT = sb("hT", [P, HC, N])
        psU, psY = ps("psU", [P, 4, D]), ps("psY", [P, 4, D])
        s = {n: c.sem("e_" + n) for n in ("b", "w1_0", "w1_1", "w2_0", "w2_1", "up", "gelu", "down", "x")}
        UP = HC * len(UPS)
        block = st.enter_context(nc.Block())

        @block.sync
        def _(sp):
            sp.dma_start(be1[:, :], ins["be1T"]).then_inc(s["b"], 16)

            def load(e, b):
                one = bass.ds(e, 1)
                sp.dma_start(w1[:, b, :, :], ins["we1"][one, :, :].rearrange("e (k p) n -> p (e k) n", p=P)).then_inc(s[f"w1_{b}"], 16)
                sp.dma_start(w2[:, b, :, :], ins["we2"][one, :, :].rearrange("e (k p) n -> p (e k) n", p=P)).then_inc(s[f"w2_{b}"], 16)

            for b in range(2):
                load(b, b)
            with sp.Fori(1, EXP // 2) as j:
                for b in range(2):
                    sp.wait_ge(s["down"], (j * 2 + (b - 1)) * NT)
                    load(j * 2 + b, b)

        @block.tensor
        def _(pe):
            with pe.Fori(0, EXP // 2) as j:
                for b in range(2):
                    e = j * 2 + b
                    pe.wait_ge(s[f"w1_{b}"], j * 16 + 16)
                    for m in range(HC):
                        for i, (a, n) in enumerate(UPS):
                            u = m * len(UPS) + i
                            if u >= 4:
                                pe.wait_ge(s["gelu"], e * UP + (u - 3))
                            elif u == 0:
                                pe.wait_ge(s["gelu"], e * UP)
                            for k in range(KC):
                                mm = pe.matmul(psU[:, u % 4, 0:n], w1[:, b, k, m * P:(m + 1) * P], c.xnT[:, k, a:a + n],
                                               start=k == 0, stop=k == KC - 1)
                            mm.then_inc(s["up"], 1)
                    pe.wait_ge(s[f"w2_{b}"], j * 16 + 16)
                    for t in range(NT):
                        pe.wait_ge(s["gelu"], e * UP + (UP - len(UPS) + 1 + min(t * P + P - 1, N - 1) // D))
                        if t >= 4:
                            pe.wait_ge(s["x"], e * NT + (t - 3))
                        elif t == 0:
                            pe.wait_ge(s["x"], e * NT)
                        r = rows_of(t)
                        for m in range(HC):
                            mm = pe.matmul(psY[0:r, t % 4, :], hT[:, m, t * P:t * P + r], w2[:, b, m, :],
                                           start=m == 0, stop=m == HC - 1)
                        mm.then_inc(s["down"], 1)

        @block.scalar
        def _(act):
            act.wait_ge(s["b"], 16)
            with act.Fori(0, EXP) as e:
                act.wait_ge(s["down"], e * NT)
                for m in range(HC):
                    for i, (a, n) in enumerate(UPS):
                        u = m * len(UPS) + i
                        wait_alone(c, act, s["up"], e * UP + (u + 1))
                        act.activation(hT[:, m, a:a + n], psU[:, u % 4, 0:n], ACT.Gelu,
                                       bias=be1[:, bass.ds(e * HC + m, 1)]).then_inc(s["gelu"], 1)

        @block.vector
        def _(dve):
            with dve.Fori(0, EXP) as e:
                for t in range(NT):
                    r = rows_of(t)
                    dve.wait_ge(s["down"], e * NT + (t + 1))
                    dve.scalar_tensor_tensor(out=c.x[0:r, t, :], in0=psY[0:r, t % 4, :], scalar=comb[0:r, t, bass.ds(e, 1)],
                                             in1=c.x[0:r, t, :], op0=ALU.mult, op1=ALU.add).then_inc(s["x"], 1)


def stage_experts(c):
    with ExitStack() as st:
        comb = st.enter_context(c.nc.sbuf_tensor("comb", [P, NT, EXP], F32))
        transposed_norm(c, "n4_")
        c.end_stage()
        stage_gate(c, comb)
        c.end_stage()
        stage_expert_layers(c, comb)
        c.end_stage()


def stage_store(c):
    nc = c.nc
    with ExitStack() as st:
        s_out = c.sem("o_out")
        block = st.enter_context(nc.Block())

        @block.sync
        def _(sp):
            sp.dma_start(c.out[0:(NT - 1) * P, :].rearrange("(t p) d -> p t d", p=P), c.x[:, 0:NT - 1, :]).then_inc(s_out, 16)
            sp.dma_start(c.out[(NT - 1) * P:N, :], c.x[0:TAIL, NT - 1, :]).then_inc(s_out, 16)
            sp.wait_ge(s_out, 32)


def build(nc, ins, out):
    with ExitStack() as ctx:
        c = Core(nc, ctx, ins, out)
        with ExitStack() as first:
            keep = tuple(first.enter_context(nc.sbuf_tensor(n, sh, F32)) for n, sh in
                         (("xn", [P, NT, D]), ("kv", [P, KC, D]), ("mean_row", [P, D])))
            stage_prepare(c, keep)
            c.end_stage()
            stage_graph(c, keep)
            c.end_stage()
        stage_memory(c)
        c.end_stage()
        stage_attention(c)
        stage_experts(c)
        stage_store(c)


def host_layout(a):
    import numpy as np

    def cc(v):
        return np.ascontiguousarray(v)

    def T(v):
        return cc(np.asarray(v).T)

    return {
        "x": cc(a["x"]), "src": cc(a["src"]), "dst": cc(a["dst"]),
        "W_selfT": T(a["L0_gnn_W_self"]), "W_neighT": T(a["L0_gnn_W_neigh"]),
        "bias": cc(a["L0_gnn_bias"]), "gamma": cc(a["L0_gnn_gamma"]), "beta": cc(a["L0_gnn_beta"]),
        "W_vT": T(a["L0_mix_W_v"]), "W_thetaT": T(a["L0_mix_W_theta"]),
        "Wq": cc(a["L0_ffn_Wq"]), "bqT": T(np.asarray(a["L0_ffn_bq"]).reshape(HEADS, P)),
        "keysT": cc(np.asarray(a["L0_ffn_keys"]).transpose(1, 3, 0, 2)),
        "mix_qkT": T(np.asarray(a["L1_mix_w_qkv"])[0:2 * D]), "mix_v": cc(np.asarray(a["L1_mix_w_qkv"])[2 * D:]),
        "mix_outT": T(a["L1_mix_w_out"]), "b_out": cc(a["L1_mix_b_out"]),
        "W_qkvT": T(a["L1_gnn_W_qkv"]), "W_ffT": T(a["L1_gnn_W_ff"]), "b_ff": cc(a["L1_gnn_b_ff"]),
        "b_qkT": T(np.asarray(a["L1_gnn_b_qkv"])[0:2 * D].reshape(2 * PAIRS, P)), "b_v": cc(np.asarray(a["L1_gnn_b_qkv"])[2 * D:]),
        "gw1": cc(a["L1_ffn_gw1"]), "gb1T": T(np.asarray(a["L1_ffn_gb1"]).reshape(2, P)), "gw2": cc(a["L1_ffn_gw2"]),
        "gb2": cc(a["L1_ffn_gb2"]), "we1": cc(a["L1_ffn_we1"]), "we2": cc(a["L1_ffn_we2"]), "be2": cc(a["L1_ffn_be2"]),
        "be1T": T(np.asarray(a["L1_ffn_be1"]).reshape(EXP * HC, P)),
        "table": np.concatenate([np.asarray(a["L0_ffn_w_down"]), np.asarray(a["L0_ffn_w_up"])], axis=1),
    }


def kernel(**inputs):
    import concourse.bacc as bacc
    from concourse.bass_utils import run_bass_kernel_spmd

    arrays = host_layout(inputs)
    nc = bacc.Bacc("TRN2", target_bir_lowering=False, num_devices=1)
    ins = {name: nc.dram_tensor("in_" + name, a.shape, mybir.dt.from_np(a.dtype), kind="ExternalInput").ap()
           for name, a in arrays.items()}
    out = nc.dram_tensor("out", (N, D), F32, kind="ExternalOutput").ap()
    build(nc, ins, out)
    return run_bass_kernel_spmd(nc, [{"in_" + name: a for name, a in arrays.items()}], core_ids=[0]).results[0]["out"]
```

```python
from contextlib import ExitStack

import concourse.bass as bass
from concourse import mybir

F32 = mybir.dt.float32
BF16 = mybir.dt.bfloat16
F16 = mybir.dt.float16
I32 = mybir.dt.int32
U32 = mybir.dt.uint32
U16 = mybir.dt.uint16
ALU = mybir.AluOpType
ACT = mybir.ActivationFunctionType
AX = mybir.AxisListType.X

P = 128
N = 1250
NT = -(-N // P)
NP = NT * P
TAIL = N - (NT - 1) * P
D = 512
KC = D // P
E = 20000
EPAIR = 250
EC = EPAIR // 2
NG = E // EPAIR
HEADS = 8
NKEYS = 256
TOPK = 8
EXP = 8
HID = 1024
HC = HID // P
EPS = 1e-5
NEG = -1e30
CHUNKS = [(0, 512), (512, 512), (1024, 256)]


class Core:

    def __init__(self, nc, ctx, ins, out):
        self.nc, self.ctx, self.ins, self.out = nc, ctx, ins, out
        self.x = ctx.enter_context(nc.sbuf_tensor("x_rows", [P, NT, D], F32))
        self.xnT = ctx.enter_context(nc.sbuf_tensor("xnT", [P, KC, NP], F32))
        self.ident = ctx.enter_context(nc.sbuf_tensor("ident", [P, P], F32))
        self.counts = nc.dram_tensor("edge_counts", (NT, P, NP), U16, kind="Internal").ap()

        self.norm_rows = nc.dram_tensor("norm_rows", (NP, D), F32, kind="Internal").ap()
        self.slot_list = nc.dram_tensor("slot_list", (BLOCKS * P, 1), U32, kind="Internal").ap()
        self.slot_rows = nc.dram_tensor("slot_rows", (BLOCKS * P, D), F32, kind="Internal").ap()
        self.live = []
        self.stage, self.passed = 0, None

    def sem(self, name):
        self.live.append(self.nc.alloc_semaphore(name=name))
        return self.live[-1]

    def end_stage(self):
        self.nc.clear_and_free_semaphores(self.live)
        self.live, self.passed = [], None
        self.nc.all_engine_barrier()


class RowStats:

    def __init__(self, c, st, tag):
        sb = lambda n, s: st.enter_context(c.nc.sbuf_tensor(tag + n, s, F32))
        self.c, self.stats, self.mv, self.rstd = c, sb("stats", [P, NT, 6]), sb("mv", [P, NT, 2]), sb("rstd", [P, NT])
        self.root = sb("root", [P, NT])
        self.s_mv, self.s_root = c.sem(tag + "moments"), c.sem(tag + "root")

    def moments(self, dve):
        for t in range(NT):
            dve.bn_stats(self.stats[:, t, :], self.c.x[:, t, :])
        dve.drain()
        for t in range(NT):
            dve.bn_aggr(self.mv[:, t, :], self.stats[:, t, :])
        dve.drain()
        dve.tensor_scalar(self.rstd[:, :], self.mv[:, :, 1], EPS, None, ALU.add).then_inc(self.s_mv, 1)
        dve.wait_ge(self.s_root, 1)
        dve.reciprocal(self.rstd[:, :], self.root[:, :])
        dve.drain()

    def roots(self, act):
        act.wait_ge(self.s_mv, 1)
        act.activation(self.root[:, :], self.rstd[:, :], ACT.Sqrt).then_inc(self.s_root, 1)

    def normalise(self, dve, t, dst):
        one = bass.ds(t, 1)
        return dve.tensor_scalar(dst, self.c.x[:, one, :], self.mv[:, one, 0], self.rstd[:, one], ALU.subtract, ALU.mult)


def wait_alone(c, eng, sem, value):
    eng.wait_ge(sem, value)
    if c.passed is None:
        c.stage += 1
        c.passed = c.sem(f"passed{c.stage}")
    eng.sem_inc(c.passed, 1)


def column(t):
    return bass.ds(t * P, P)


def stage_prepare(c, keep):
    nc, ins = c.nc, c.ins
    xn, kv, mean_row = keep
    with ExitStack() as st:
        sb = lambda n, s, d: st.enter_context(nc.sbuf_tensor(n, s, d))
        ps = lambda n, s: st.enter_context(nc.psum_tensor(n, s, F32))
        wv, wth = sb("wv", [P, KC, D], F32), sb("wth", [P, KC, D], F32)
        rows = sb("rows", [P, D], F32)
        norm = RowStats(c, st, "p_")
        gram, m1 = sb("gram", [P, KC, D], F32), sb("m1", [P, KC, D], F32)
        xsum, xbar = sb("xsum", [P, KC], F32), sb("xbar", [P, KC, P], F32)
        ones = sb("ones", [P, P], F32)
        psT, psG, psM = ps("psT", [P, D]), ps("psG", [P, KC, D]), ps("psM", [P, 2, D])
        s_tail, s_x, s_w, s_id0, s_id, s_ones = (c.sem("p_" + n) for n in ("tail", "x", "w", "id0", "id", "ones"))
        s_rows, s_tr, s_tdone, s_copied = (c.sem("p_" + n) for n in ("rows", "tr", "tdone", "copied"))
        s_gram, s_gdone, s_bar, s_mm, s_ev = (c.sem("p_" + n) for n in ("gram", "gdone", "bar", "mm", "ev"))
        block = st.enter_context(nc.Block())

        @block.sync
        def _(sp):
            sp.dma_start(c.x[:, 0:NT - 1, :], ins["x"][0:(NT - 1) * P, :].rearrange("(t p) d -> p t d", p=P)).then_inc(s_x, 16)
            sp.wait_ge(s_tail, 1)
            sp.dma_start(c.x[0:TAIL, NT - 1, :], ins["x"][(NT - 1) * P:N, :]).then_inc(s_x, 16)
            sp.dma_start(wv[:, :, :], ins["W_vT"].rearrange("(k p) n -> p k n", p=P)).then_inc(s_w, 16)
            sp.dma_start(wth[:, :, :], ins["W_thetaT"].rearrange("(k p) n -> p k n", p=P)).then_inc(s_w, 16)

        @block.gpsimd
        def _(pool):
            pool.memset(c.x[96:P, NT - 1, :], 0.0).then_inc(s_tail, 1)
            pool.wait_ge(s_tail, 1)
            pool.memset(c.ident[:, :], 0.0).then_inc(s_id0, 1)
            pool.wait_ge(s_id0, 1)
            pool.affine_select(out=c.ident[:, :], in_=c.ident[:, :], compare_op=ALU.not_equal, fill=1.0,
                               base=0, pattern=[[-1, P]], channel_multiplier=1).then_inc(s_id, 1)
            pool.memset(ones[:, :], 1.0).then_inc(s_ones, 1)

        @block.vector
        def _(dve):
            dve.wait_ge(s_x, 32)
            norm.moments(dve)
            with dve.Fori(0, NT) as t:
                dve.wait_ge(s_gram, t)
                dve.wait_ge(s_copied, t)
                norm.normalise(dve, t, rows[:, :]).then_inc(s_rows, 1)
            dve.wait_ge(s_tdone, NT)
            dve.tensor_reduce(xsum[:, :], c.xnT[:, :, :], AX, ALU.add)
            dve.wait_ge(s_ones, 1)
            dve.drain()
            for k in range(KC):
                bar = dve.tensor_scalar(xbar[:, k, :], ones[:, :], xsum[:, k:k + 1], 1.0 / N, ALU.mult, ALU.mult)
            bar.then_inc(s_bar, 1)

        @block.scalar
        def _(act):
            norm.roots(act)
            with act.Fori(0, NT) as t:
                wait_alone(c, act, s_rows, t + 1)
                act.activation(xn[:, bass.ds(t, 1), :], rows[:, :], ACT.Copy).then_inc(s_copied, 1)
                wait_alone(c, act, s_tr, t + 1)
                act.activation(c.xnT[:, :, column(t)], psT[:, :].rearrange("p (k n) -> p k n", k=KC),
                               ACT.Copy).then_inc(s_tdone, 1)
            act.wait_ge(s_gdone, 1)
            act.activation(gram[:, :, :], psG[:, :, :], ACT.Copy).then_inc(s_ev, 1)
            for m in range(2 * KC):
                act.wait_ge(s_mm, m + 1)
                dst, scale = (m1, 1.0) if m < KC else (kv, 1.0 / (N * D ** 0.5))
                act.activation(dst[:, m % KC, :], psM[:, m % 2, :], ACT.Copy, scale=scale).then_inc(s_ev, 1)
            act.wait_ge(s_mm, 2 * KC + 1)
            act.activation(mean_row[:, :], psM[:, 0, :], ACT.Copy).then_inc(s_ev, 1)

        @block.tensor
        def _(pe):
            pe.wait_ge(s_id, 1)

            def tile(t, first):
                pe.wait_ge(s_rows, t + 1)
                pe.wait_ge(s_tdone, t)
                for k in range(KC):
                    mm = pe.transpose(psT[:, k * P:(k + 1) * P], rows[:, k * P:(k + 1) * P], c.ident[:, :])
                mm.then_inc(s_tr, 1)
                for m in range(KC):
                    mm = pe.matmul(psG[:, m, :], rows[:, m * P:(m + 1) * P], rows[:, :], start=first, stop=True,
                                   skip_group_check=True)
                mm.then_inc(s_gram, 1)

            tile(0, True)
            with pe.Fori(1, NT) as t:
                tile(t, False)
            pe.matmul(psM[:, 0, 0:P], rows[:, 0:P], c.ident[:, :], start=True, stop=True).then_inc(s_gdone, 1)
            pe.wait_ge(s_w, 32)
            pe.wait_ge(s_ev, 1)
            for m in range(2 * KC):
                left, right = (gram, wv) if m < KC else (wth, m1)
                if m >= 2:
                    pe.wait_ge(s_ev, m)
                if m == KC:
                    pe.wait_ge(s_ev, KC + 1)
                for k in range(KC):
                    mm = pe.matmul(psM[:, m % 2, :], left[:, k, m % KC * P:(m % KC + 1) * P], right[:, k, :],
                                   start=k == 0, stop=k == KC - 1)
                mm.then_inc(s_mm, 1)
            pe.wait_ge(s_ev, 2 * KC)
            pe.wait_ge(s_bar, 1)
            for k in range(KC):
                mm = pe.matmul(psM[:, 0, :], xbar[:, k, :], wv[:, k, :], start=k == 0, stop=k == KC - 1)
            mm.then_inc(s_mm, 1)


def stage_graph(c, keep):
    nc, ins = c.nc, c.ins
    xn, kv, mean_row = keep
    with ExitStack() as st:
        sb = lambda n, s, d: st.enter_context(nc.sbuf_tensor(n, s, d))
        ps = lambda n, s: st.enter_context(nc.psum_tensor(n, s, F32))
        ws, wn = sb("ws", [P, KC, D], F32), sb("wn", [P, KC, D], F32)
        bias, gamma, beta = sb("bias", [P, D], F32), sb("gamma", [P, D], F32), sb("beta", [P, D], F32)
        edge_i, edge_f = sb("edge_i", [NG, 2, EPAIR], I32), sb("edge_f", [NG, 2, EPAIR], F32)
        ends = sb("ends", [NG, 2], F32)
        edges = sb("edges", [EC, 4, 2 * NG], F32)
        shifted = sb("shifted", [EC, 2, 2 * NG], F32)
        row = sb("row", [1, 6, NT * NG], F32)
        group_i, group_id = sb("group_i", [1, NG], I32), sb("group_id", [1, NG], F32)
        tile_i, tile_lo, tile_hi = sb("tile_i", [P, NT], I32), sb("tile_lo", [P, NT], F32), sb("tile_hi", [P, NT], F32)
        bounds_f, bounds = sb("bounds_f", [1, 4, NT], F32), sb("bounds", [1, 2 * NT], I32)
        node_i, node_id = sb("node_i", [P, NP], I32), sb("node_id", [P, NP], F16)
        zero = sb("zero", [P, D], BF16)
        hot_dst, hot_src = sb("hot_dst", [EC, 2, P], BF16), sb("hot_src", [EC, 2, NP], BF16)
        cnt, cnt16, cntT = sb("cnt", [P, NP], F32), sb("cnt16", [P, NP], U16), sb("cntT", [P, NT, P], F32)
        deg, rdeg = sb("deg", [P, 1], F32), sb("rdeg", [P, 1], F32)
        xt, aggT = sb("xt", [P, KC, P], F32), sb("aggT", [P, KC, P], F32)
        h, h2, h3 = sb("h", [P, D], F32), sb("h2", [P, D], F32), sb("h3", [P, D], F32)
        stats, mv, rstd = sb("g_stats", [P, 6], F32), sb("g_mv", [P, 2], F32), sb("g_rstd", [P, 1], F32)
        root = sb("g_root", [P, 1], F32)
        psC, psT, psA, psH = ps("psC", [P, 3 * D]), ps("psCT", [P, 2, D]), ps("psA", [P, KC, P]), ps("psH", [P, 2, D])
        names = ("edges_in", "w", "const", "zero", "edge_f", "ends", "tr", "edges", "bounds", "hot", "hot_free", "cnt",
                 "cnt_out", "cnt16", "stored", "xt", "hs", "ctT", "ct_out", "agg", "agg_out", "hn", "x1", "moments", "root")
        s = {n: c.sem("g_" + n) for n in names}
        block = st.enter_context(nc.Block())

        @block.sync
        def _(sp):
            sp.dma_start(edge_i[:, 0, :], ins["src"].rearrange("(g e) -> g e", g=NG)).then_inc(s["edges_in"], 16)
            sp.dma_start(edge_i[:, 1, :], ins["dst"].rearrange("(g e) -> g e", g=NG)).then_inc(s["edges_in"], 16)
            sp.dma_start(ws[:, :, :], ins["W_selfT"].rearrange("(k p) n -> p k n", p=P)).then_inc(s["w"], 16)
            sp.dma_start(wn[:, :, :], ins["W_neighT"].rearrange("(k p) n -> p k n", p=P)).then_inc(s["w"], 16)
            for dst, name in ((bias, "bias"), (gamma, "gamma"), (beta, "beta")):
                sp.dma_start(dst[:, :], ins[name].partition_broadcast(P)).then_inc(s["w"], 16)
            with sp.Fori(0, NT) as t:
                sp.wait_ge(s["cnt16"], t + 1)
                sp.dma_start(c.counts[bass.ds(t, 1), :, :].rearrange("a p n -> p (a n)"), cnt16[:, :]).then_inc(s["stored"], 16)
            sp.wait_ge(s["stored"], 16 * NT)

        @block.gpsimd
        def _(pool):
            pool.memset(zero[:, :], 0.0).then_inc(s["zero"], 1)
            pool.iota(group_i[:, :], pattern=[[1, NG]], base=0, channel_multiplier=0).then_inc(s["const"], 1)
            pool.iota(tile_i[:, :], pattern=[[P, NT]], base=0, channel_multiplier=0).then_inc(s["const"], 1)
            pool.iota(node_i[:, :], pattern=[[1, NP]], base=0, channel_multiplier=0).then_inc(s["const"], 1)
            pool.wait_ge(s["const"], 3)
            pool.tensor_copy(group_id[:, :], group_i[:, :]).then_inc(s["const"], 1)
            pool.tensor_copy(tile_lo[:, :], tile_i[:, :]).then_inc(s["const"], 1)
            pool.tensor_copy(node_id[:, :], node_i[:, :]).then_inc(s["const"], 1)
            with pool.Fori(0, NT) as t:
                pool.wait_ge(s["cnt_out"], t + 1)
                wait_alone(c, pool, s["stored"], 16 * t)
                pool.tensor_copy(cnt16[:, :], cnt[:, :]).then_inc(s["cnt16"], 1)

        @block.vector
        def _(dve):
            dve.wait_ge(s["edges_in"], 32)
            dve.tensor_copy(edge_f[:, :, :], edge_i[:, :, :]).then_inc(s["edge_f"], 1)
            dve.drain()
            dve.tensor_reduce(ends[:, 0:1], edge_f[:, 1, :], AX, ALU.min)
            dve.tensor_reduce(ends[:, 1:2], edge_f[:, 1, :], AX, ALU.max).then_inc(s["ends"], 1)
            dve.wait_ge(s["tr"], 1)
            dve.tensor_copy(edges[:, :, 0:NG], psT[0:EC, 0, 0:4 * NG].rearrange("p (a g) -> p a g", a=4)).then_inc(s["edges"], 1)
            r = [row[0:1, i, :].rearrange("p (t g) -> p t g", t=NT) for i in range(6)]
            lowest = row[0:1, 4, 0:NG].unsqueeze(1).to_broadcast([1, NT, NG])
            highest = row[0:1, 5, 0:NG].unsqueeze(1).to_broadcast([1, NT, NG])
            gid = group_id[0:1, :].unsqueeze(1).to_broadcast([1, NT, NG])
            dve.tensor_copy(row[0:1, 4, 0:NG], psT[0:1, 1, 0:NG])
            dve.tensor_copy(row[0:1, 5, 0:NG], psT[0:1, 1, NG:2 * NG])
            dve.wait_ge(s["const"], 6)
            dve.tensor_scalar(tile_hi[:, :], tile_lo[:, :], float(P - 1), None, ALU.add)
            dve.drain()
            dve.tensor_tensor(r[0], highest, tile_lo[0:1, :].unsqueeze(2).to_broadcast([1, NT, NG]), ALU.is_ge)
            dve.tensor_tensor(r[1], tile_hi[0:1, :].unsqueeze(2).to_broadcast([1, NT, NG]), lowest, ALU.is_ge)
            dve.drain()
            dve.tensor_tensor(r[2], r[0], r[1], ALU.mult)
            dve.drain()
            dve.scalar_tensor_tensor(out=r[0], in0=r[2], scalar=-1000.0, in1=gid, op0=ALU.mult, op1=ALU.add)
            dve.scalar_tensor_tensor(out=r[1], in0=gid, scalar=1.0, in1=r[2], op0=ALU.add, op1=ALU.mult)
            dve.drain()
            dve.tensor_reduce(bounds_f[:, 0, :], r[0], AX, ALU.min)
            dve.tensor_reduce(bounds_f[:, 1, :], r[1], AX, ALU.max)
            dve.drain()
            dve.tensor_scalar(bounds_f[:, 2, :], bounds_f[:, 0, :], 0.0, 1000.0, ALU.is_lt, ALU.mult)
            dve.drain()
            dve.tensor_tensor(bounds_f[:, 0, :], bounds_f[:, 0, :], bounds_f[:, 2, :], ALU.add)
            dve.drain()
            dve.tensor_tensor(bounds_f[:, 3, :], bounds_f[:, 1, :], bounds_f[:, 0, :], ALU.subtract)
            dve.drain()
            dve.tensor_scalar(bounds[:, NT:2 * NT], bounds_f[:, 3, :], 1.0, None, ALU.max)
            dve.tensor_copy(bounds[:, 0:NT], bounds_f[:, 0, :]).then_inc(s["bounds"], 1)
            dve.wait_ge(s["bounds"], 1)
            dve.wait_ge(s["w"], 80)
            dve.tensor_tensor(beta[:, :], beta[:, :], mean_row[:, :], ALU.add)
            done = dve.alloc_register("groups_done")
            dve.reg_mov(done, 0)
            with dve.Fori(0, NT) as t:
                first = dve.value_load(bounds[0:1, bass.ds(t, 1)], min_val=0, max_val=NG - 1)
                many = dve.value_load(bounds[0:1, bass.ds(t + NT, 1)], min_val=1, max_val=NG)
                before = dve.snap(done)
                dve.tensor_scalar(shifted[:, :, 0:NG], edges[:, 2:4, 0:NG], tile_lo[0:EC, bass.ds(t, 1)], None, ALU.subtract)
                dve.drain()
                with dve.Fori(0, many) as i:
                    for j in range(2):
                        dve.wait_ge(s["hot_free"], (before + i) * 2 + (j + 1))
                        dve.tensor_scalar(hot_dst[:, j, :], node_id[0:EC, 0:P], shifted[:, j, bass.ds(first + i, 1)],
                                          None, ALU.is_equal)
                        dve.tensor_scalar(hot_src[:, j, :], node_id[0:EC, :], edges[:, j, bass.ds(first + i, 1)],
                                          None, ALU.is_equal).then_inc(s["hot"], 1)
                dve.reg_add(done, done, many)
                dve.wait_ge(s["cnt_out"], t + 1)
                dve.tensor_scalar(rdeg[:, :], deg[:, :], 1.0, None, ALU.max)
                dve.drain()
                dve.reciprocal(rdeg[:, :], rdeg[:, :])
                dve.wait_ge(s["hs"], t + 1)
                dve.tensor_tensor(h[:, :], psH[:, 0, :], bias[:, :], ALU.add)
                dve.drain()
                dve.wait_ge(s["hn"], t + 1)
                dve.scalar_tensor_tensor(out=h2[:, :], in0=psT[:, 1, :], scalar=rdeg[:, 0:1], in1=h[:, :],
                                         op0=ALU.mult, op1=ALU.add)
                dve.drain()
                dve.bn_stats(stats[:, :], h2[:, :])
                dve.drain()
                dve.bn_aggr(mv[:, :], stats[:, :])
                dve.drain()
                dve.tensor_scalar(rstd[:, :], mv[:, 1:2], EPS, None, ALU.add).then_inc(s["moments"], 1)
                dve.wait_ge(s["root"], t + 1)
                dve.reciprocal(rstd[:, :], root[:, :])
                dve.drain()
                dve.tensor_scalar(h[:, :], h2[:, :], mv[:, 0:1], rstd[:, 0:1], ALU.subtract, ALU.mult)
                dve.drain()
                dve.tensor_tensor(h2[:, :], h[:, :], gamma[:, :], ALU.mult)
                dve.tensor_tensor(h3[:, :], psH[:, 1, :], beta[:, :], ALU.add)
                dve.drain()
                dve.tensor_tensor(h2[:, :], h2[:, :], h3[:, :], ALU.add)
                dve.drain()
                dve.tensor_tensor(c.x[:, bass.ds(t, 1), :], c.x[:, bass.ds(t, 1), :],
                                  h2[:, :].unsqueeze(1), ALU.add).then_inc(s["x1"], 1)

        @block.scalar
        def _(act):
            with act.Fori(0, NT) as t:
                wait_alone(c, act, s["hs"], t)
                act.activation(xt[:, :, :], c.xnT[:, :, column(t)], ACT.Copy).then_inc(s["xt"], 1)
                act.wait_ge(s["cnt"], t + 1)
                act.wait_ge(s["ctT"], 3 * t)
                act.wait_ge(s["cnt16"], t)
                act.wait_ge(s["x1"], t)
                act.activation(cnt[:, :], psC[:, 0:NP], ACT.Copy, accum_out=deg[:, 0:1]).then_inc(s["cnt_out"], 1)
                act.wait_ge(s["agg"], t)
                for g in range(3):
                    n = min(4, NT - 4 * g)
                    act.wait_ge(s["ctT"], 3 * t + (g + 1))
                    act.activation(cntT[:, 4 * g:4 * g + n, :], psT[:, g % 2, 0:n * P].rearrange("p (a n) -> p a n", a=n),
                                   ACT.Copy).then_inc(s["ct_out"], 1)
                act.wait_ge(s["agg"], t + 1)
                act.wait_ge(s["hn"], t)
                act.activation(aggT[:, :, :], psA[:, :, :], ACT.Copy).then_inc(s["agg_out"], 1)
                act.wait_ge(s["moments"], t + 1)
                act.activation(root[:, :], rstd[:, :], ACT.Sqrt).then_inc(s["root"], 1)

        @block.tensor
        def _(pe):
            pe.wait_ge(s["edge_f"], 1)
            for a in range(4):
                pe.transpose(psT[0:EC, 0, a * NG:(a + 1) * NG], edge_f[:, a // 2, a % 2 * EC:(a % 2 + 1) * EC],
                             c.ident[0:NG, 0:NG])
            pe.wait_ge(s["ends"], 1)
            for a in range(2):
                mm = pe.matmul(psT[0:1, 1, a * NG:(a + 1) * NG], ends[:, a:a + 1], c.ident[0:NG, 0:NG], start=True, stop=True)
            mm.then_inc(s["tr"], 1)
            pe.wait_ge(s["zero"], 1)
            pe.wait_ge(s["w"], 80)
            pe.sem_inc(s["hot_free"], 2)
            pe.wait_ge(s["bounds"], 1)
            done = pe.alloc_register("groups_done")
            pe.reg_mov(done, 0)
            with pe.Fori(0, NT) as t:
                many = pe.value_load(bounds[0:1, bass.ds(t + NT, 1)], min_val=1, max_val=NG)
                before = pe.snap(done)
                pe.wait_ge(s["cnt_out"], t)
                for a, n in CHUNKS:
                    pe.matmul(psC[:, a:a + n], zero[:, 0:P], zero[:, 0:n], start=True, stop=True, skip_group_check=True)
                with pe.Fori(0, many) as i:
                    for j in range(2):
                        pe.wait_ge(s["hot"], (before + i) * 2 + (j + 1))
                        for a, n in CHUNKS:
                            mm = pe.matmul(psC[:, a:a + n], hot_dst[:, j, :], hot_src[:, j, a:a + n], start=False,
                                           stop=True, skip_group_check=True)
                        mm.then_inc(s["hot_free"], 1)
                pe.reg_add(done, done, many)
                pe.matmul(psC[:, 0:P], zero[:, 0:P], zero[:, 0:P], start=False, stop=True,
                          skip_group_check=True).then_inc(s["cnt"], 1)
                pe.wait_ge(s["xt"], t + 1)
                pe.wait_ge(s["x1"], t)
                for i, w in enumerate((ws, kv)):
                    for k in range(KC):
                        mm = pe.matmul(psH[:, i, :], xt[:, k, :], w[:, k, :], start=k == 0, stop=k == KC - 1)
                mm.then_inc(s["hs"], 1)
                pe.wait_ge(s["cnt_out"], t + 1)
                for g in range(3):
                    if g == 2:
                        pe.wait_ge(s["ct_out"], 3 * t + 1)
                    for a in range(4 * g, min(4 * g + 4, NT)):
                        mm = pe.transpose(psT[:, g % 2, a % 4 * P:(a % 4 + 1) * P], cnt[:, a * P:(a + 1) * P], c.ident[:, :])
                    mm.then_inc(s["ctT"], 1)
                pe.wait_ge(s["ct_out"], 3 * t + 3)
                pe.wait_ge(s["agg_out"], t)
                for f in range(KC):
                    for a in range(NT):
                        mm = pe.matmul(psA[:, f, :], xn[:, a, f * P:(f + 1) * P], cntT[:, a, :], start=a == 0, stop=a == NT - 1)
                mm.then_inc(s["agg"], 1)
                pe.wait_ge(s["agg_out"], t + 1)
                for k in range(KC):
                    mm = pe.matmul(psT[:, 1, :], aggT[:, k, :], wn[:, k, :], start=k == 0, stop=k == KC - 1)
                mm.then_inc(s["hn"], 1)


RING = 16
AHEAD = RING // TOPK


def stage_memory(c):
    nc, ins = c.nc, c.ins
    with ExitStack() as st:
        sb = lambda n, s, d=F32: st.enter_context(nc.sbuf_tensor("m_" + n, s, d))
        ps = lambda n, s: st.enter_context(nc.psum_tensor("m_" + n, s, F32))
        norm = RowStats(c, st, "m_")
        ring = sb("ring", [P, RING, 2 * D])
        wq, bq, keys = sb("wq", [P, KC, HEADS * P]), sb("bq", [P, HEADS]), sb("keys", [P, HEADS, 2 * NKEYS])
        coming, current, xT = sb("coming", [P, D]), sb("current", [P, D]), sb("xT", [P, KC, P])
        qT = sb("qT", [P, HEADS, P])
        product = sb("product", [P, D])
        diag = sb("diag", [P, AHEAD * TOPK, P])
        top, top_at, top_id = sb("top", [P, 2, TOPK]), sb("top_at", [P, 2, TOPK], U32), sb("top_id", [P, 2, TOPK])
        pairs, best = sb("pairs", [P, TOPK, TOPK]), sb("best", [P, HEADS, TOPK])
        best_at, side, side_f = sb("best_at", [P, TOPK], U32), sb("side", [P, 2, TOPK], U32), sb("side_f", [P, 2, TOPK])
        pick, chosen = sb("pick", [P, 2, TOPK, TOPK]), sb("chosen", [P, 2, TOPK])
        number_i, number = sb("number_i", [P, TOPK], I32), sb("number", [P, TOPK])
        rows_at = sb("rows_at", [P, HEADS, TOPK], U32)
        lowest, expo, total = sb("lowest", [P, HEADS]), sb("expo", [P, HEADS, TOPK]), sb("total", [P, HEADS])
        inner, share, rtotal = sb("inner", [P, TOPK]), sb("share", [P, TOPK]), sb("rtotal", [P, 1])
        weight = sb("weight", [P, AHEAD, TOPK])
        psT, psQ, psS, acc = ps("psT", [P, D]), ps("psQ", [P, 2, D]), ps("psS", [P, 2, D]), ps("acc", [P, D])
        names = ("w", "keys0", "number0", "number", "coming", "tr", "xT", "q", "qT", "score", "found", "soft", "weight",
                 "diag", "slot_free", "x2")
        s = {n: c.sem("m_" + n) for n in names}
        s_land = [c.sem(f"m_landed{i}") for i in range(RING)]
        block = st.enter_context(nc.Block())

        @block.sync
        def _(sp):
            sp.dma_start(wq[:, :, :], ins["Wq"].rearrange("(k p) n -> p k n", p=P)).then_inc(s["w"], 16)
            sp.dma_start(bq[:, :], ins["bqT"]).then_inc(s["w"], 16)
            sp.wait_ge(s["keys0"], 1)
            for i in range(2):
                sp.dma_start(keys[64 * i:64 * i + 64, :, NKEYS * i:NKEYS * (i + 1)], ins["keysT"][i]).then_inc(s["w"], 16)

        @block.gpsimd
        def _(pool):
            pool.memset(keys[:, :, :], 0.0).then_inc(s["keys0"], 1)
            pool.iota(number_i[:, :], pattern=[[1, TOPK]], base=0, channel_multiplier=0).then_inc(s["number0"], 1)
            pool.wait_ge(s["number0"], 1)
            pool.tensor_copy(number[:, :], number_i[:, :]).then_inc(s["number"], 1)
            with pool.Fori(0, NT) as t:
                for h in range(HEADS):
                    pool.wait_ge(s["found"], t * HEADS + (h + 1))
                    for k in range(TOPK):
                        slot = (h * TOPK + k) % RING
                        wait_alone(c, pool, s["slot_free"], t * (HEADS * TOPK) + (h * TOPK + k + 1))
                        pool.indirect_dma_start(ring[:, slot, :], None, ins["table"],
                                                bass.IndirectOffsetOnAxis(rows_at[:, h, k:k + 1], 0)).then_inc(s_land[slot], 16)

        def search(dve, h, nth):
            wait_alone(c, dve, s["score"], nth + 1)
            b = h % 2
            for i in range(2):
                dve.max(top[:, i, :], psS[:, b, NKEYS * i:NKEYS * (i + 1)])
            dve.drain()
            for i in range(2):
                dve.max_index(top_at[:, i, :], top[:, i, :], psS[:, b, NKEYS * i:NKEYS * (i + 1)])
            dve.tensor_tensor(pairs[:, :, :], top[:, 0, :].unsqueeze(2).to_broadcast([P, TOPK, TOPK]),
                              top[:, 1, :].unsqueeze(1).to_broadcast([P, TOPK, TOPK]), ALU.add)
            dve.drain()
            dve.tensor_copy(top_id[:, :, :], top_at[:, :, :])
            dve.max(best[:, h, :], pairs[:, :, :].rearrange("p a b -> p (a b)"))
            dve.drain()
            dve.max_index(best_at[:, :], best[:, h, :], pairs[:, :, :].rearrange("p a b -> p (a b)"))
            dve.tensor_scalar(lowest[:, h:h + 1], best[:, h, 0:1], -1.0, None, ALU.mult)
            dve.drain()
            dve.tensor_scalar(side[:, 0, :], best_at[:, :], 3, None, ALU.logical_shift_right)
            dve.tensor_scalar(side[:, 1, :], best_at[:, :], TOPK - 1, None, ALU.bitwise_and)
            dve.drain()
            dve.tensor_copy(side_f[:, :, :], side[:, :, :])
            dve.drain()
            dve.tensor_tensor(pick[:, :, :, :], side_f[:, :, :].unsqueeze(3).to_broadcast([P, 2, TOPK, TOPK]),
                              number[:, :].unsqueeze(1).unsqueeze(1).to_broadcast([P, 2, TOPK, TOPK]), ALU.is_equal)
            dve.drain()
            dve.tensor_tensor(pick[:, :, :, :], pick[:, :, :, :],
                              top_id[:, :, :].unsqueeze(2).to_broadcast([P, 2, TOPK, TOPK]), ALU.mult)
            dve.drain()
            dve.tensor_reduce(chosen[:, :, :], pick[:, :, :, :], AX, ALU.add)
            dve.drain()
            dve.scalar_tensor_tensor(out=rows_at[:, h, :], in0=chosen[:, 0, :], scalar=float(NKEYS), in1=chosen[:, 1, :],
                                     op0=ALU.mult, op1=ALU.add).then_inc(s["found"], 1)

        def use(dve, h, nth, t):
            dve.wait_ge(s["soft"], nth + 1)
            dve.reciprocal(rtotal[:, :], total[:, h:h + 1])
            for k in range(TOPK):
                slot = (h * TOPK + k) % RING
                if k:
                    dve.drain()
                dve.wait_ge(s_land[slot], (t * (HEADS // AHEAD) + (h // AHEAD + 1)) * 16)
                dve.tensor_tensor_reduce(product[:, :], ring[:, slot, 0:D], current[:, :], 1.0, 0.0, ALU.mult, ALU.add,
                                         inner[:, k:k + 1])
            dve.tensor_scalar(share[:, :], expo[:, h, :], rtotal[:, 0:1], None, ALU.mult)
            dve.drain()
            dve.scalar_tensor_tensor(out=weight[:, h % AHEAD, :], in0=inner[:, :], scalar=0.0, in1=share[:, :],
                                     op0=ALU.max, op1=ALU.mult).then_inc(s["weight"], 1)
            dve.drain()

        @block.vector
        def _(dve):
            norm.moments(dve)
            norm.normalise(dve, 0, coming[:, :]).then_inc(s["coming"], 1)
            dve.wait_ge(s["number"], 1)
            for h in range(HEADS):
                search(dve, h, h)

            def tile(t, last):
                dve.drain()
                dve.tensor_copy(current[:, :], coming[:, :])
                dve.drain()
                if not last:
                    norm.normalise(dve, t + 1, coming[:, :]).then_inc(s["coming"], 1)
                for h in range(HEADS):
                    use(dve, h, t * HEADS + h, t)
                    if not last:
                        search(dve, h, t * HEADS + (HEADS + h))
                dve.wait_ge(s["slot_free"], (t + 1) * (HEADS * TOPK) + RING)
                dve.tensor_tensor(c.x[:, bass.ds(t, 1), :], c.x[:, bass.ds(t, 1), :], acc[:, :].unsqueeze(1),
                                  ALU.add).then_inc(s["x2"], 1)

            with dve.Fori(0, NT - 1) as t:
                tile(t, False)
            tile(NT - 1, True)

        def queries(act, nth):
            act.wait_ge(s["tr"], nth + 1)
            act.activation(xT[:, :, :], psT[:, :].rearrange("p (k n) -> p k n", k=KC), ACT.Copy).then_inc(s["xT"], 1)
            for h in range(HEADS):
                if h % 4 == 0:
                    act.wait_ge(s["q"], nth * 2 + (h // 4 + 1))
                act.activation(qT[:, h, :], psQ[:, h // 4, h % 4 * P:(h % 4 + 1) * P], ACT.Identity,
                               bias=bq[:, h:h + 1]).then_inc(s["qT"], 1)

        def soften(act, h, nth):
            act.wait_ge(s["found"], nth + 1)
            act.activation(expo[:, h, :], best[:, h, :], ACT.Exp, bias=lowest[:, h:h + 1],
                           accum_out=total[:, h:h + 1]).then_inc(s["soft"], 1)

        @block.scalar
        def _(act):
            norm.roots(act)
            act.wait_ge(s["w"], 64)
            queries(act, 0)
            for h in range(HEADS):
                soften(act, h, h)

            def tile(t, last):
                if not last:
                    queries(act, t + 1)
                for h in range(HEADS):
                    act.wait_ge(s["weight"], t * HEADS + (h + 1))
                    act.wait_ge(s["slot_free"], t * (HEADS * TOPK) + (h + 1) * TOPK)
                    for k in range(TOPK):
                        act.activation(diag[:, h % AHEAD * TOPK + k, :], c.ident[:, :], ACT.Copy,
                                       scale=weight[:, h % AHEAD, k:k + 1]).then_inc(s["diag"], 1)
                    if not last:
                        soften(act, h, t * HEADS + (HEADS + h))

            with act.Fori(0, NT - 1) as t:
                tile(t, False)
            tile(NT - 1, True)

        def project(pe, nth, first):
            pe.wait_ge(s["coming"], nth + 1)
            for k in range(KC):
                mm = pe.transpose(psT[:, k * P:(k + 1) * P], coming[:, k * P:(k + 1) * P], c.ident[:, :])
            mm.then_inc(s["tr"], 1)
            pe.wait_ge(s["xT"], nth + 1)
            if not first:
                pe.wait_ge(s["qT"], nth * HEADS)
            for h in range(HEADS):
                for k in range(KC):
                    mm = pe.matmul(psQ[:, h // 4, h % 4 * P:(h % 4 + 1) * P], wq[:, k, h * P:(h + 1) * P], xT[:, k, :],
                                   start=k == 0, stop=k == KC - 1)
                if h % 4 == 3:
                    mm.then_inc(s["q"], 1)

        def scores(pe, h, nth, first):
            pe.wait_ge(s["qT"], nth + 1)
            if not (first and h < 2):
                pe.wait_ge(s["found"], nth - 1)
            pe.matmul(psS[:, h % 2, :], qT[:, h, :], keys[:, h, :], start=True, stop=True).then_inc(s["score"], 1)

        @block.tensor
        def _(pe):
            pe.wait_ge(s["w"], 64)
            pe.sem_inc(s["slot_free"], RING)
            project(pe, 0, True)
            for h in range(HEADS):
                scores(pe, h, h, True)

            def tile(t, last):
                if not last:
                    project(pe, t + 1, False)
                for h in range(HEADS):
                    if not last:
                        scores(pe, h, t * HEADS + (HEADS + h), False)
                    if h == 0:
                        pe.wait_ge(s["x2"], t)
                    for k in range(TOPK):
                        pe.wait_ge(s["diag"], t * (HEADS * TOPK) + (h * TOPK + k + 1))
                        pe.matmul(acc[:, :], diag[:, h % AHEAD * TOPK + k, :], ring[:, (h * TOPK + k) % RING, D:2 * D],
                                  start=h + k == 0, stop=h * TOPK + k == HEADS * TOPK - 1).then_inc(s["slot_free"], 1)

            with pe.Fori(0, NT - 1) as t:
                tile(t, False)
            tile(NT - 1, True)


PAIRS = HEADS // 2


def transposed_norm(c, tag, saved=None):
    nc = c.nc
    with ExitStack() as st:
        norm = RowStats(c, st, tag)
        rows = st.enter_context(nc.sbuf_tensor(tag + "rows", [P, D], F32))
        psT = st.enter_context(nc.psum_tensor(tag + "psT", [P, D], F32))
        s_rows, s_tr, s_out, s_saved = (c.sem(tag + n) for n in ("rows_ready", "turned", "stored", "saved"))
        block = st.enter_context(nc.Block())

        @block.sync
        def _(sp):
            if saved is not None:
                with sp.Fori(0, NT) as t:
                    sp.wait_ge(s_rows, t + 1)
                    sp.dma_start(saved[column(t), :], rows[:, :]).then_inc(s_saved, 16)
                sp.wait_ge(s_saved, 16 * NT)

        @block.vector
        def _(dve):
            norm.moments(dve)
            with dve.Fori(0, NT) as t:
                dve.wait_ge(s_tr, t)
                if saved is not None:
                    dve.wait_ge(s_saved, t * 16)
                norm.normalise(dve, t, rows[:, :]).then_inc(s_rows, 1)

        @block.tensor
        def _(pe):
            with pe.Fori(0, NT) as t:
                pe.wait_ge(s_rows, t + 1)
                pe.wait_ge(s_out, t)
                for k in range(KC):
                    mm = pe.transpose(psT[:, k * P:(k + 1) * P], rows[:, k * P:(k + 1) * P], c.ident[:, :])
                mm.then_inc(s_tr, 1)

        @block.scalar
        def _(act):
            norm.roots(act)
            with act.Fori(0, NT) as t:
                wait_alone(c, act, s_tr, t + 1)
                act.activation(c.xnT[:, :, column(t)], psT[:, :].rearrange("p (k n) -> p k n", k=KC),
                               ACT.Copy).then_inc(s_out, 1)


def stage_token_mix(c, mix):
    nc, ins = c.nc, c.ins
    with ExitStack() as st:
        sb = lambda n, s, d=F32: st.enter_context(nc.sbuf_tensor("t_" + n, s, d))
        ps = lambda n, s: st.enter_context(nc.psum_tensor("t_" + n, s, F32))
        wqk, wv, wo = sb("wqk", [P, KC, 2 * D]), sb("wv", [P, KC, D]), sb("wo", [P, KC, D])
        q, k_rows = sb("q", [P, NT, D]), sb("k_rows", [P, NT, P])
        kT = sb("kT", [P, NP])
        low, ksum, rk = sb("low", [P, PAIRS]), sb("ksum", [P, PAIRS]), sb("rk", [P, PAIRS])
        qmax, qsum, qr = sb("qmax", [P, HEADS]), sb("qsum", [P, HEADS]), sb("qr", [P, HEADS])
        qe, qs = sb("qe", [P, 2, D]), sb("qs", [P, 2, D])
        kq, z = sb("kq", [P, PAIRS, P]), sb("z", [P, PAIRS, D])
        psQ, psK, psR, psM = ps("psQ", [P, 2, D]), ps("psK", [P, 3 * D]), ps("psR", [P, 2, D]), ps("psM", [P, D])
        names = ("w", "q", "qd", "qexp", "qout", "kq0", "k", "low", "kexp", "tr", "krows", "kq", "kqout", "z", "zout", "y", "yout",
                 "rk", "pad")
        s = {n: c.sem("t_" + n) for n in names}
        block = st.enter_context(nc.Block())

        @block.sync
        def _(sp):
            sp.dma_start(wqk[:, :, :], ins["mix_qkT"].rearrange("(k p) n -> p k n", p=P)).then_inc(s["w"], 16)
            sp.dma_start(wv[:, :, :], ins["mix_v"].rearrange("(k p) n -> p k n", p=P)).then_inc(s["w"], 16)
            sp.dma_start(wo[:, :, :], ins["mix_outT"].rearrange("(k p) n -> p k n", p=P)).then_inc(s["w"], 16)

        @block.gpsimd
        def _(pool):
            pool.memset(kq[:, :, :], 0.0).then_inc(s["kq0"], 1)
            pool.memset(kT[:, N:NP], 0.0).then_inc(s["pad"], 1)

        @block.tensor
        def _(pe):
            pe.wait_ge(s["w"], 48)
            for t in range(NT):
                if t >= 2:
                    pe.wait_ge(s["qd"], t - 1)
                for k in range(KC):
                    mm = pe.matmul(psQ[:, t % 2, :], c.xnT[:, k, t * P:(t + 1) * P], wqk[:, k, 0:D], start=k == 0, stop=k == KC - 1)
                mm.then_inc(s["q"], 1)
            for m in range(PAIRS):
                if m:
                    pe.wait_ge(s["kexp"], m)
                for a, n in CHUNKS:
                    for k in range(KC):
                        mm = pe.matmul(psK[:, a:a + n], wqk[:, k, D + m * P:D + (m + 1) * P], c.xnT[:, k, a:a + n],
                                       start=k == 0, stop=k == KC - 1)
                mm.then_inc(s["k"], 1)
                pe.wait_ge(s["kexp"], m + 1)
                for g in range(3):
                    if 3 * m + g >= 2:
                        pe.wait_ge(s["krows"], 3 * m + g - 1)
                    for a in range(4 * g, min(4 * g + 4, NT)):
                        mm = pe.transpose(psR[:, (3 * m + g) % 2, a % 4 * P:(a % 4 + 1) * P], kT[:, a * P:(a + 1) * P], c.ident[:, :])
                    mm.then_inc(s["tr"], 1)
                pe.wait_ge(s["qout"], NT)
                pe.wait_ge(s["krows"], 3 * m + 3)
                if m:
                    pe.wait_ge(s["kqout"], 2 * m)
                for t in range(NT):
                    mm = pe.matmul(psM[:, 0:P], k_rows[:, t, :], q[:, t, m * P:(m + 1) * P], start=t == 0, stop=t == NT - 1)
                mm.then_inc(s["kq"], 1)
            pe.wait_ge(s["kqout"], 2 * PAIRS)
            for m in range(PAIRS):
                if m >= 2:
                    pe.wait_ge(s["zout"], m - 1)
                pe.transpose(psM[:, 0:P], kq[:, m, :], c.ident[:, :]).then_inc(s["z"], 1)
                pe.wait_ge(s["zout"], 2 * m + 1)
                pe.matmul(psQ[:, m % 2, :], kT[:, 0:P], wo[:, m, :], start=True, stop=True).then_inc(s["z"], 1)
                pe.wait_ge(s["zout"], 2 * m + 2)
            for m in range(KC):
                if m >= 2:
                    pe.wait_ge(s["yout"], m - 1)
                for k in range(KC):
                    mm = pe.matmul(psQ[:, m % 2, :], wv[:, k, m * P:(m + 1) * P], z[:, k, :], start=k == 0, stop=k == KC - 1)
                mm.then_inc(s["y"], 1)

        def heads(ap):
            return ap.rearrange("p (h e) -> p h e", h=HEADS)

        @block.vector
        def _(dve):
            dve.wait_ge(s["kq0"], 1)
            dve.wait_ge(s["pad"], 1)
            for t in range(NT):
                b = t % 2
                dve.wait_ge(s["q"], t + 1)
                dve.tensor_reduce(qmax[:, :], heads(psQ[:, b, :]), AX, ALU.max)
                dve.drain()
                dve.tensor_tensor(heads(qs[:, b, :]), heads(psQ[:, b, :]), qmax[:, :].unsqueeze(2).to_broadcast([P, HEADS, D // HEADS]),
                                  ALU.subtract).then_inc(s["qd"], 1)
                dve.wait_ge(s["qexp"], t + 1)
                dve.tensor_reduce(qsum[:, :], heads(qe[:, b, :]), AX, ALU.add)
                dve.drain()
                dve.reciprocal(qr[:, :], qsum[:, :])
                dve.drain()
                dve.tensor_tensor(heads(q[:, t, :]), heads(qe[:, b, :]), qr[:, :].unsqueeze(2).to_broadcast([P, HEADS, D // HEADS]),
                                  ALU.mult).then_inc(s["qout"], 1)
                dve.drain()
            for m in range(PAIRS):
                dve.wait_ge(s["k"], m + 1)
                dve.tensor_reduce(low[:, m:m + 1], psK[:, 0:N], AX, ALU.max)
                dve.drain()
                dve.tensor_scalar(low[:, m:m + 1], low[:, m:m + 1], -1.0, None, ALU.mult).then_inc(s["low"], 1)
                dve.wait_ge(s["kexp"], m + 1)
                dve.reciprocal(rk[:, m:m + 1], ksum[:, m:m + 1]).then_inc(s["rk"], 1)
                dve.wait_ge(s["kq"], m + 1)
                dve.drain()
                for i in range(2):
                    a = slice(64 * i, 64 * i + 64)
                    dve.tensor_scalar(kq[a, m, a], psM[a, a], rk[a, m:m + 1], None, ALU.mult).then_inc(s["kqout"], 1)

        @block.scalar
        def _(act):
            for t in range(NT):
                act.wait_ge(s["qd"], t + 1)
                act.activation(qe[:, t % 2, :], qs[:, t % 2, :], ACT.Exp).then_inc(s["qexp"], 1)
            for m in range(PAIRS):
                act.wait_ge(s["low"], m + 1)
                if m:
                    act.wait_ge(s["tr"], 3 * m)
                act.activation(kT[:, 0:N], psK[:, 0:N], ACT.Exp, bias=low[:, m:m + 1],
                               accum_out=ksum[:, m:m + 1]).then_inc(s["kexp"], 1)
                for g in range(3):
                    n = min(4, NT - 4 * g)
                    act.wait_ge(s["tr"], 3 * m + g + 1)
                    if m:
                        act.wait_ge(s["kq"], m)
                    act.activation(k_rows[:, 4 * g:4 * g + n, :], psR[:, (3 * m + g) % 2, 0:n * P].rearrange("p (a n) -> p a n", a=n),
                                   ACT.Copy).then_inc(s["krows"], 1)
            for m in range(PAIRS):
                act.wait_ge(s["z"], 2 * m + 1)
                act.activation(kT[:, 0:P], psM[:, 0:P], ACT.Copy).then_inc(s["zout"], 1)
                act.wait_ge(s["z"], 2 * m + 2)
                act.activation(z[:, m, :], psQ[:, m % 2, :], ACT.Copy).then_inc(s["zout"], 1)
            for m in range(KC):
                act.wait_ge(s["y"], m + 1)
                act.activation(mix[:, m, :], psQ[:, m % 2, :], ACT.Copy).then_inc(s["yout"], 1)
            act.wait_ge(s["yout"], KC)


def stage_edge_attention(c, msg):
    nc, ins = c.nc, c.ins
    with ExitStack() as st:
        sb = lambda n, s, d=F32: st.enter_context(nc.sbuf_tensor("a_" + n, s, d))
        ps = lambda n, s: st.enter_context(nc.psum_tensor("a_" + n, s, F32))
        cnt, mask = sb("cnt", [P, 2, NP], U16), sb("mask", [P, 2, NP], BF16)
        w, bqk, bq8, bv = sb("w", [P, KC, 3, P]), sb("bqk", [P, 2 * PAIRS]), sb("bq8", [P, PAIRS]), sb("bv", [P, D])
        qz, kT, v = sb("qz", [P, 2, NP]), sb("kT", [P, NP]), sb("v", [P, NT, P])
        qt = sb("qt", [P, 2, P])
        prob, pT = sb("prob", [P, 2, NP]), sb("pT", [P, 2, NT, P])
        low, den, rden = sb("low", [P, 2]), sb("den", [P, 2]), sb("rden", [P, 2])
        junk = sb("junk", [P, N], BF16)
        psS, psT, psV = ps("psS", [P, 3 * D]), ps("psT", [P, 3 * D]), ps("psV", [P, 2, D])
        names = ("cnt0", "cnt1", "b", "bq8", "zero", "w", "q", "qout", "v", "vout", "k", "kout", "staged", "score", "low", "exp",
                 "weighed", "turned", "pT", "sums", "msg", "rden", "pad")
        s = {n: c.sem("a_" + n) for n in names}
        U = 2 * NT
        block = st.enter_context(nc.Block())

        @block.sync
        def _(sp):
            sp.dma_start(bqk[:, :], ins["b_qkT"]).then_inc(s["b"], 16)
            sp.dma_start(bv[:, :], ins["b_v"].partition_broadcast(P)).then_inc(s["b"], 16)
            wt = ins["W_qkvT"].rearrange("(k p) (a n) -> p k a n", p=P, a=3)
            with sp.Fori(0, PAIRS) as m:
                sp.wait_ge(s["v"], m * 3)
                for i in range(3):
                    sp.dma_start(w[:, :, i, :], wt[:, :, i, bass.ds(m * P, P)]).then_inc(s["w"], 16)
                with sp.Fori(0, NT // 2) as j:
                    for b in range(2):
                        sp.wait_ge(s["weighed"], m * U + j * 4 + (2 * b + 2))
                        sp.dma_start(cnt[:, b, :], c.counts[bass.ds(j * 2 + b, 1), :, :].rearrange("a p n -> p (a n)"))\
                          .then_inc(s[f"cnt{b}"], 16)

        @block.gpsimd
        def _(pool):
            pool.memset(qz[:, :, :], 0.0).then_inc(s["zero"], 1)
            pool.memset(prob[:, :, N:NP], 0.0).then_inc(s["pad"], 1)
            with pool.Fori(0, PAIRS) as m:
                wait_alone(c, pool, s["qout"], m * 2 + 2)
                with pool.Fori(0, NT) as t:
                    for h in range(2):
                        wait_alone(c, pool, s["score"], m * U + t * 2 + (h + 1))
                        pool.tensor_copy(qt[:, h, :], qz[:, h, column(t)]).then_inc(s["staged"], 1)

        @block.tensor
        def _(pe):
            pe.sem_inc(s["score"], 2)
            pe.sem_inc(s["sums"], 1)

            def score(n, h):
                pe.wait_ge(s["staged"], n + 1)
                pe.wait_ge(s["exp"], n)
                for a, width in CHUNKS:
                    mm = pe.matmul(psS[:, a:a + width], qt[:, h, :], kT[:, a:a + width], start=True, stop=True)
                mm.then_inc(s["score"], 1)

            def turn(n, h):
                pe.wait_ge(s["weighed"], n + 5)
                pe.wait_ge(s["pT"], n)
                for a in range(NT):
                    mm = pe.transpose(psT[:, a * P:(a + 1) * P], prob[:, h, a * P:(a + 1) * P], c.ident[:, :])
                mm.then_inc(s["turned"], 1)

            def sums(n, h):
                pe.wait_ge(s["pT"], n + 1)
                pe.wait_ge(s["msg"], n)
                for a in range(NT):
                    mm = pe.matmul(psV[:, h, 0:P], pT[:, h, a, :], v[:, a, :], start=a == 0, stop=a == NT - 1)
                mm.then_inc(s["sums"], 1)

            with pe.Fori(0, PAIRS) as m:
                pe.wait_ge(s["w"], m * 48 + 48)
                pe.wait_ge(s["exp"], m * U)
                pe.wait_ge(s["pT"], m * U)
                pe.wait_ge(s["msg"], m * U + 1)
                for i, dst in enumerate((psS, psT)):
                    for a, width in CHUNKS:
                        for k in range(KC):
                            mm = pe.matmul(dst[:, a:a + width], w[:, k, i, :], c.xnT[:, k, a:a + width],
                                           start=k == 0, stop=k == KC - 1)
                    mm.then_inc(s["qk"[i]], 1)
                for t in range(NT):
                    if t == 8:
                        pe.wait_ge(s["vout"], m * 3 + 1)
                    for k in range(KC):
                        mm = pe.matmul(psV[:, t // 4 % 2, t % 4 * P:(t % 4 + 1) * P], c.xnT[:, k, t * P:(t + 1) * P],
                                       w[:, k, 2, :], start=k == 0, stop=k == KC - 1)
                    if t in (3, 7, NT - 1):
                        mm.then_inc(s["v"], 1)
                pe.wait_ge(s["kout"], m + 1)
                pe.wait_ge(s["qout"], m * 2 + 2)
                pe.wait_ge(s["vout"], m * 3 + 3)
                score(m * U, 0)

                def tiles(j, first, last):
                    for i in range(4):
                        n, h = m * U + j * 4 + i, i % 2
                        if not (last and i == 3):
                            score(n + 1, 1 - h)
                        turn(n, h)
                        if not (first and i == 0):
                            sums(m * U + j * 4 + i - 1 if i else m * U + (j * 4 - 1), 1 - h)

                tiles(0, True, False)
                with pe.Fori(1, NT // 2 - 1) as j:
                    tiles(j, False, False)
                tiles(NT // 2 - 1, False, True)
                sums(m * U + (U - 1), 1)

        @block.vector
        def _(dve):
            dve.sem_inc(s["weighed"], 4)
            dve.wait_ge(s["b"], 32)
            dve.tensor_scalar(bq8[:, :], bqk[:, 0:PAIRS], 64 ** -0.5, None, ALU.mult).then_inc(s["bq8"], 1)
            dve.wait_ge(s["pad"], 1)
            with dve.Fori(0, PAIRS) as m:
                for g in range(3):
                    n = min(4, NT - 4 * g)
                    dve.wait_ge(s["v"], m * 3 + (g + 1))
                    dve.tensor_tensor(v[:, 4 * g:4 * g + n, :], psV[:, g % 2, 0:n * P].rearrange("p (a n) -> p a n", a=n),
                                      bv[:, bass.ds(m * P, P)].unsqueeze(1).to_broadcast([P, n, P]), ALU.add).then_inc(s["vout"], 1)
                with dve.Fori(0, NT // 2) as j:
                    for i in range(4):
                        n, b, h = m * U + j * 4 + i, i // 2, i % 2
                        if h == 0:
                            dve.wait_ge(s[f"cnt{b}"], (m * (NT // 2) + j + 1) * 16)
                            dve.tensor_scalar(mask[:, b, 0:N], cnt[:, b, 0:N], 0.0, NEG, ALU.is_equal, ALU.mult)
                            dve.drain()
                        wait_alone(c, dve, s["score"], n + 3)
                        dve.tensor_tensor_reduce(junk[:, :], psS[:, 0:N], mask[:, b, 0:N], -1.0, 3e38, ALU.add, ALU.min,
                                                 low[:, h:h + 1])
                        dve.drain()
                        dve.scalar_tensor_tensor(out=low[:, h:h + 1], in0=low[:, h:h + 1], scalar=-0.1 * NEG, in1=low[:, h:h + 1],
                                                 op0=ALU.is_lt, op1=ALU.mult).then_inc(s["low"], 1)
                        dve.wait_ge(s["exp"], n + 1)
                        dve.scalar_tensor_tensor(out=prob[:, h, 0:N], in0=prob[:, h, 0:N], scalar=1.0, in1=cnt[:, b, 0:N],
                                                 op0=ALU.min, op1=ALU.mult, accum_out=den[:, h:h + 1]).then_inc(s["weighed"], 1)
                        dve.drain()
                        dve.tensor_scalar(den[:, h:h + 1], den[:, h:h + 1], 1e-30, None, ALU.max)
                        dve.drain()
                        dve.wait_ge(s["msg"], n)
                        dve.reciprocal(rden[:, h:h + 1], den[:, h:h + 1]).then_inc(s["rden"], 1)

        @block.scalar
        def _(act):
            act.sem_inc(s["msg"], 1)
            act.wait_ge(s["bq8"], 1)
            act.wait_ge(s["zero"], 1)

            def exponent(n, h):
                act.wait_ge(s["low"], n + 1)
                act.activation(prob[:, h, 0:N], psS[:, 0:N], ACT.Exp, bias=low[:, h:h + 1]).then_inc(s["exp"], 1)

            def message(m, t, n, h):
                act.wait_ge(s["sums"], n + 2)
                wait_alone(c, act, s["rden"], n + 1)
                act.activation(msg[:, bass.ds(t, 1), bass.ds(m * P + 64 * h, 64)].rearrange("p a n -> p (a n)"),
                               psV[:, h, 64 * h:64 * h + 64], ACT.Copy, scale=rden[:, h:h + 1]).then_inc(s["msg"], 1)

            def keep_turned(n, h):
                act.wait_ge(s["turned"], n + 1)
                act.wait_ge(s["sums"], n)
                act.activation(pT[:, h, :, :], psT[:, 0:NP].rearrange("p (a n) -> p a n", a=NT), ACT.Copy).then_inc(s["pT"], 1)

            with act.Fori(0, PAIRS) as m:
                wait_alone(c, act, s["q"], m + 1)
                for h in range(2):
                    a = slice(64 * h, 64 * h + 64)
                    act.activation(qz[a, h, :], psS[a, 0:NP], ACT.Identity, bias=bq8[a, bass.ds(m, 1)],
                                   scale=64 ** -0.5).then_inc(s["qout"], 1)
                wait_alone(c, act, s["k"], m + 1)
                act.activation(kT[:, :], psT[:, 0:NP], ACT.Identity, bias=bqk[:, bass.ds(m + PAIRS, 1)]).then_inc(s["kout"], 1)

                def tile(t, first):
                    for h in range(2):
                        n = m * U + t * 2 + h
                        exponent(n, h)
                        if not first:
                            message(m, t - 1, m * U + (t - 1) * 2 + h, h)
                        keep_turned(n, h)

                tile(0, True)
                with act.Fori(1, NT) as t:
                    tile(t, False)
                for h in range(2):
                    message(m, NT - 1, m * U + (U - 2 + h), h)


def stage_join(c, msg, mix):
    nc, ins = c.nc, c.ins
    with ExitStack() as st:
        sb = lambda n, s, d=F32: st.enter_context(nc.sbuf_tensor("j_" + n, s, d))
        ps = lambda n, s: st.enter_context(nc.psum_tensor("j_" + n, s, F32))
        wff, bff, bout = sb("wff", [P, KC, D]), sb("bff", [P, D]), sb("bout", [P, D])
        xt, mt, mT, y = sb("xt", [P, KC, P]), sb("mt", [P, D]), sb("mT", [P, KC, P]), sb("y", [P, D])
        psT, psO = ps("psT", [P, D]), ps("psO", [P, D])
        s = {n: c.sem("j_" + n) for n in ("w", "bias", "mt", "xt", "turned", "mT", "out", "x3")}
        block = st.enter_context(nc.Block())

        @block.sync
        def _(sp):
            sp.dma_start(wff[:, :, :], ins["W_ffT"].rearrange("(k p) n -> p k n", p=P)).then_inc(s["w"], 16)
            for dst, name in ((bff, "b_ff"), (bout, "b_out")):
                sp.dma_start(dst[:, :], ins[name].partition_broadcast(P)).then_inc(s["w"], 16)

        @block.gpsimd
        def _(pool):
            with pool.Fori(0, NT) as t:
                wait_alone(c, pool, s["turned"], t)
                pool.tensor_copy(mt[:, :], msg[:, bass.ds(t, 1), :].rearrange("p a n -> p (a n)")).then_inc(s["mt"], 1)

        @block.scalar
        def _(act):
            with act.Fori(0, NT) as t:
                wait_alone(c, act, s["out"], t)
                act.activation(xt[:, :, :], c.xnT[:, :, column(t)], ACT.Copy).then_inc(s["xt"], 1)
                act.wait_ge(s["turned"], t + 1)
                act.activation(mT[:, :, :], psT[:, :].rearrange("p (k n) -> p k n", k=KC), ACT.Copy).then_inc(s["mT"], 1)

        @block.tensor
        def _(pe):
            pe.wait_ge(s["w"], 48)
            with pe.Fori(0, NT) as t:
                pe.wait_ge(s["mt"], t + 1)
                pe.wait_ge(s["mT"], t)
                for k in range(KC):
                    mm = pe.transpose(psT[:, k * P:(k + 1) * P], mt[:, k * P:(k + 1) * P], c.ident[:, :])
                mm.then_inc(s["turned"], 1)
                pe.wait_ge(s["xt"], t + 1)
                pe.wait_ge(s["x3"], t)
                for k in range(KC):
                    pe.matmul(psO[:, :], xt[:, k, :], mix[:, k, :], start=k == 0, stop=False)
                pe.wait_ge(s["mT"], t + 1)
                for k in range(KC):
                    mm = pe.matmul(psO[:, :], mT[:, k, :], wff[:, k, :], start=False, stop=k == KC - 1)
                mm.then_inc(s["out"], 1)

        @block.vector
        def _(dve):
            dve.wait_ge(s["w"], 48)
            dve.tensor_tensor(bff[:, :], bff[:, :], bout[:, :], ALU.add)
            with dve.Fori(0, NT) as t:
                dve.drain()
                dve.wait_ge(s["out"], t + 1)
                dve.tensor_tensor(y[:, :], psO[:, :], bff[:, :], ALU.add)
                dve.drain()
                dve.tensor_tensor(c.x[:, bass.ds(t, 1), :], c.x[:, bass.ds(t, 1), :], y[:, :].unsqueeze(1),
                                  ALU.add).then_inc(s["x3"], 1)


def stage_attention(c):
    with ExitStack() as st:
        mix = st.enter_context(c.nc.sbuf_tensor("mix", [P, KC, D], F32))
        transposed_norm(c, "n3_")
        c.end_stage()
        stage_token_mix(c, mix)
        c.end_stage()
        msg = st.enter_context(c.nc.sbuf_tensor("msg", [P, NT, D], F32))
        stage_edge_attention(c, msg)
        c.end_stage()
        stage_join(c, msg, mix)
        c.end_stage()


CHOICES = 2
BLOCKS = (CHOICES * N + EXP * (P - 1)) // P


def rows_of(t):
    return P if t < NT - 1 else TAIL


def stage_gate(c, route):
    nc, ins = c.nc, c.ins
    share, slot_of, slots, owner = route
    with ExitStack() as st:
        sb = lambda n, s, d=F32: st.enter_context(nc.sbuf_tensor("r_" + n, s, d))
        ps = lambda n, s: st.enter_context(nc.psum_tensor("r_" + n, s, F32))
        gw1, gw2, gb1, gb2, be2 = sb("gw1", [P, KC, 2 * P]), sb("gw2", [P, 2, EXP]), sb("gb1", [P, 2]), sb("gb2", [P, EXP]), sb("be2", [EXP, D])
        gT = sb("gT", [P, 2, NP])
        logit, expo, gate = sb("logit", [P, NT, EXP]), sb("expo", [P, NT, EXP]), sb("gate", [P, NT, EXP])
        peak, total, top, top_at = sb("peak", [P, NT]), sb("total", [P, NT]), sb("top", [P, NT, 8]), sb("top_at", [P, NT, 8], U32)
        at, expert_i, expert = sb("at", [P, NT, 8]), sb("expert_i", [P, EXP], I32), sb("expert", [P, EXP])
        gap, second, first, hit = sb("gap", [P, NT]), sb("second", [P, NT]), sb("first", [P, NT]), sb("hit", [P, 2, NT, EXP])
        part, comb = sb("part", [P, 2, NT, EXP]), sb("comb", [P, NT, EXP])
        member, below, ones = sb("member", [P, NT, EXP]), sb("below", [P, P]), sb("ones", [P, P])
        rank, tally, before = sb("rank", [P, NT, EXP]), sb("tally", [P, NT, EXP]), sb("before", [P, NT + 1, EXP])
        filled_f, filled, blocks = sb("filled_f", [P, EXP]), sb("filled", [P, EXP], I32), sb("blocks", [P, EXP])
        start, base = sb("start", [P, EXP + 1]), sb("base", [P, EXP])
        block_i, block_id, past = sb("block_i", [P, BLOCKS], I32), sb("block_id", [P, BLOCKS]), sb("past", [P, BLOCKS, EXP])
        owner_f, slot_f = sb("owner_f", [P, BLOCKS]), sb("slot_f", [P, 2, NT])
        row_id, spare = sb("row_id", [P, NT], U32), sb("spare", [P, BLOCKS], U32)
        combT = sb("combT", [EXP, NT, P])
        psG, psL, psC, psB = ps("psG", [P, 2, D]), ps("psL", [P, 3, NT, EXP]), ps("psC", [EXP, 3, D]), ps("psB", [P, 2, D])
        s = {n: c.sem("r_" + n) for n in ("w", "iota", "expert", "hidden", "relu", "logits", "shifted", "exp", "gap", "exp2", "comb",
                                          "turned", "combT", "bias", "x", "tri", "both", "member", "ranked", "slot", "list0",
                                          "listed", "slots")}
        block = st.enter_context(nc.Block())

        def wide(ap):
            return ap.unsqueeze(2).to_broadcast([P, NT, EXP])

        @block.sync
        def _(sp):
            sp.dma_start(gw1[:, :, :], ins["gw1"].rearrange("(k p) n -> p k n", p=P)).then_inc(s["w"], 16)
            sp.dma_start(gw2[:, :, :], ins["gw2"].rearrange("(k p) n -> p k n", p=P)).then_inc(s["w"], 16)
            sp.dma_start(gb1[:, :], ins["gb1T"]).then_inc(s["w"], 16)
            sp.dma_start(gb2[:, :], ins["gb2"].partition_broadcast(P)).then_inc(s["w"], 16)
            sp.dma_start(be2[:, :], ins["be2"]).then_inc(s["w"], 16)
            sp.wait_ge(s["iota"], 8)
            sp.dma_start(c.slot_list.rearrange("(p b) a -> p (b a)", p=P), spare[:, :]).then_inc(s["list0"], 16)
            sp.wait_ge(s["listed"], 16 * CHOICES * NT)
            sp.dma_start(slots[:, :], c.slot_list.rearrange("(b p) a -> p (b a)", p=P), allow_slow_non_contiguous=True).then_inc(s["slots"], 16)
            sp.wait_ge(s["slots"], 16)

        @block.gpsimd
        def _(pool):
            pool.iota(expert_i[:, :], pattern=[[1, EXP]], base=0, channel_multiplier=0).then_inc(s["iota"], 1)
            pool.iota(block_i[:, :], pattern=[[1, BLOCKS]], base=0, channel_multiplier=0).then_inc(s["iota"], 1)
            pool.iota(row_id[:, :], pattern=[[P, NT]], base=0, channel_multiplier=1).then_inc(s["iota"], 1)
            pool.iota(spare[:, :], pattern=[[0, BLOCKS]], base=NP - 1, channel_multiplier=0).then_inc(s["iota"], 1)
            pool.memset(below[:, :], 1.0).then_inc(s["iota"], 1)
            pool.memset(ones[:, :], 1.0).then_inc(s["iota"], 1)
            pool.wait_ge(s["iota"], 6)
            pool.tensor_copy(expert[:, :], expert_i[:, :]).then_inc(s["iota"], 1)
            pool.tensor_copy(block_id[:, :], block_i[:, :]).then_inc(s["iota"], 1)
            pool.affine_select(out=below[:, :], in_=below[:, :], compare_op=ALU.is_gt, fill=0.0, base=0,
                               pattern=[[1, P]], channel_multiplier=-1).then_inc(s["tri"], 1)
            pool.wait_ge(s["both"], 1)
            pool.affine_select(out=member[:, NT - 1, :], in_=member[:, NT - 1, :], compare_op=ALU.is_ge, fill=0.0,
                               base=TAIL - 1, pattern=[[0, EXP]], channel_multiplier=-1).then_inc(s["member"], 1)
            pool.wait_ge(s["slot"], 1)
            pool.wait_ge(s["list0"], 16)
            for i in range(CHOICES):
                for t in range(NT):
                    r = rows_of(t)
                    pool.indirect_dma_start(c.slot_list, bass.IndirectOffsetOnAxis(slot_of[0:r, i, t:t + 1], 0),
                                            row_id[0:r, t:t + 1], None).then_inc(s["listed"], 16)

        @block.tensor
        def _(pe):
            pe.wait_ge(s["w"], 80)
            for m in range(2):
                for i, (a, n) in enumerate(CHUNKS):
                    u = 3 * m + i
                    if u >= 2:
                        pe.wait_ge(s["relu"], u - 1)
                    for k in range(KC):
                        mm = pe.matmul(psG[:, u % 2, 0:n], gw1[:, k, m * P:(m + 1) * P], c.xnT[:, k, a:a + n],
                                       start=k == 0, stop=k == KC - 1)
                    mm.then_inc(s["hidden"], 1)
            pe.wait_ge(s["relu"], 6)
            for t in range(NT):
                for m in range(2):
                    mm = pe.matmul(psL[:, 0, t, :], gT[:, m, t * P:(t + 1) * P], gw2[:, m, :], start=m == 0, stop=m == 1)
            mm.then_inc(s["logits"], 1)
            pe.wait_ge(s["tri"], 1)
            pe.wait_ge(s["member"], 1)
            pe.matmul(psL[:, 1, :, :], below[:, :], member[:, :, :], start=True, stop=True)
            pe.matmul(psL[:, 2, :, :], ones[:, :], member[:, :, :], start=True, stop=True).then_inc(s["ranked"], 1)
            pe.wait_ge(s["comb"], 1)
            for t in range(NT):
                mm = pe.transpose(psC[:, t // 4, t % 4 * P:(t % 4 + 1) * P], comb[:, t, :], c.ident[:, :])
            mm.then_inc(s["turned"], 1)
            pe.wait_ge(s["combT"], 1)
            for t in range(NT):
                if t >= 2:
                    pe.wait_ge(s["x"], t - 1)
                pe.matmul(psB[:, t % 2, :], combT[:, t, :], be2[:, :], start=True, stop=True).then_inc(s["bias"], 1)

        @block.scalar
        def _(act):
            act.wait_ge(s["w"], 80)
            for m in range(2):
                for i, (a, n) in enumerate(CHUNKS):
                    u = 3 * m + i
                    act.wait_ge(s["hidden"], u + 1)
                    act.activation(gT[:, m, a:a + n], psG[:, u % 2, 0:n], ACT.Relu, bias=gb1[:, m:m + 1]).then_inc(s["relu"], 1)
            act.wait_ge(s["shifted"], 1)
            act.activation(expo[:, :, :], logit[:, :, :], ACT.Exp).then_inc(s["exp"], 1)
            act.wait_ge(s["gap"], 1)
            act.activation(second[:, :], gap[:, :], ACT.Exp).then_inc(s["exp2"], 1)
            act.wait_ge(s["turned"], 1)
            act.activation(combT[:, :, :], psC[:, :, :].rearrange("p a (b n) -> p (a b) n", n=P)[:, 0:NT, :],
                           ACT.Copy).then_inc(s["combT"], 1)

        @block.vector
        def _(dve):
            dve.wait_ge(s["w"], 80)
            dve.wait_ge(s["logits"], 1)
            dve.tensor_tensor(logit[:, :, :], psL[:, 0, :, :], gb2[:, :].unsqueeze(1).to_broadcast([P, NT, EXP]), ALU.add)
            dve.drain()
            dve.tensor_reduce(peak[:, :], logit[:, :, :], AX, ALU.max)
            dve.drain()
            dve.tensor_tensor(logit[:, :, :], logit[:, :, :], wide(peak[:, :]), ALU.subtract).then_inc(s["shifted"], 1)
            dve.wait_ge(s["exp"], 1)
            dve.tensor_reduce(total[:, :], expo[:, :, :], AX, ALU.add)
            dve.drain()
            dve.reciprocal(peak[:, :], total[:, :])
            dve.drain()
            dve.tensor_tensor(gate[:, :, :], expo[:, :, :], wide(peak[:, :]), ALU.mult)
            dve.drain()
            for t in range(NT):
                dve.max(top[:, t, :], gate[:, t, :])
            dve.drain()
            for t in range(NT):
                dve.max_index(top_at[:, t, :], top[:, t, :], gate[:, t, :])
            dve.tensor_tensor(gap[:, :], top[:, :, 1], top[:, :, 0], ALU.subtract).then_inc(s["gap"], 1)
            dve.drain()
            dve.tensor_copy(at[:, :, :], top_at[:, :, :])
            dve.wait_ge(s["exp2"], 1)
            dve.tensor_scalar(first[:, :], second[:, :], 1.0, None, ALU.add)
            dve.drain()
            dve.reciprocal(gap[:, :], first[:, :])
            dve.drain()
            dve.tensor_tensor(share[:, 1, :], second[:, :], gap[:, :], ALU.mult)
            dve.tensor_copy(share[:, 0, :], gap[:, :])
            dve.wait_ge(s["iota"], 8)
            ids = expert[:, :].unsqueeze(1).to_broadcast([P, NT, EXP])
            for i in range(CHOICES):
                dve.tensor_tensor(hit[:, i, :, :], wide(at[:, :, i]), ids, ALU.is_equal)
            dve.drain()
            dve.tensor_tensor(member[:, :, :], hit[:, 0, :, :], hit[:, 1, :, :], ALU.add).then_inc(s["both"], 1)
            for i in range(CHOICES):
                dve.tensor_tensor(part[:, i, :, :], hit[:, i, :, :], wide(share[:, i, :]), ALU.mult)
            dve.drain()
            dve.tensor_tensor(comb[:, :, :], part[:, 0, :, :], part[:, 1, :, :], ALU.add).then_inc(s["comb"], 1)
            dve.wait_ge(s["ranked"], 1)
            dve.tensor_copy(tally[:, :, :], psL[:, 2, :, :])
            dve.memset(before[:, 0, :], 0.0)
            dve.memset(start[:, 0:1], 0.0)
            dve.drain()
            for t in range(NT):
                dve.tensor_tensor(before[:, t + 1, :], before[:, t, :], tally[:, t, :], ALU.add)
                dve.drain()
            dve.tensor_scalar(filled_f[:, :], before[:, NT, :], float(P - 1), None, ALU.add)
            dve.drain()
            dve.tensor_copy(filled[:, :], filled_f[:, :])
            dve.drain()
            dve.tensor_scalar(filled[:, :], filled[:, :], 7, None, ALU.arith_shift_right)
            dve.drain()
            dve.tensor_copy(blocks[:, :], filled[:, :])
            dve.drain()
            for e in range(EXP):
                dve.tensor_tensor(start[:, e + 1:e + 2], start[:, e:e + 1], blocks[:, e:e + 1], ALU.add)
                dve.drain()
            dve.tensor_scalar(base[:, :], start[:, 0:EXP], float(P), None, ALU.mult)
            dve.tensor_tensor(rank[:, :, :], psL[:, 1, :, :], before[:, 0:NT, :], ALU.add)
            dve.drain()
            dve.tensor_tensor(rank[:, :, :], rank[:, :, :], base[:, :].unsqueeze(1).to_broadcast([P, NT, EXP]), ALU.add)
            dve.drain()
            for i in range(CHOICES):
                dve.tensor_tensor(part[:, i, :, :], hit[:, i, :, :], rank[:, :, :], ALU.mult)
            dve.drain()
            dve.tensor_reduce(slot_f[:, :, :], part[:, :, :, :], AX, ALU.add)
            dve.drain()
            dve.tensor_copy(slot_of[:, :, :], slot_f[:, :, :]).then_inc(s["slot"], 1)
            dve.tensor_tensor(past[:, :, :], block_id[:, :].unsqueeze(2).to_broadcast([P, BLOCKS, EXP]),
                              start[:, 1:EXP + 1].unsqueeze(1).to_broadcast([P, BLOCKS, EXP]), ALU.is_ge)
            dve.drain()
            dve.tensor_reduce(owner_f[:, :], past[:, :, :], AX, ALU.add)
            dve.drain()
            dve.tensor_scalar(owner[:, :], owner_f[:, :], float(EXP - 1), None, ALU.min)
            for t in range(NT):
                dve.wait_ge(s["bias"], t + 1)
                dve.tensor_tensor(c.x[:, t, :], c.x[:, t, :], psB[:, t % 2, :], ALU.add).then_inc(s["x"], 1)


def stage_expert_layers(c, route):
    nc, ins = c.nc, c.ins
    share, slot_of, slots, owner = route
    with ExitStack() as st:
        sb = lambda n, s, d=F32: st.enter_context(nc.sbuf_tensor("e_" + n, s, d))
        ps = lambda n, s: st.enter_context(nc.psum_tensor("e_" + n, s, F32))
        w1, w2, be1 = sb("w1", [P, 2, KC, HID]), sb("w2", [P, 2, HC, D]), sb("be1", [P, EXP * HC])
        rows, rowsT, hT, y = sb("rows", [P, 2, D]), sb("rowsT", [P, KC, P]), sb("hT", [P, 2, HC, P]), sb("y", [P, 2, D])
        psT, psU, psY = ps("psT", [P, D]), ps("psU", [P, 2, HC, P]), ps("psY", [P, 2, D])
        s = {n: c.sem("e_" + n) for n in ("b", "w1_0", "w1_1", "w2_0", "w2_1", "rows_0", "rows_1", "turned", "rowsT", "up",
                                          "hidden", "gelu", "down", "y", "stored_0", "stored_1")}
        block = st.enter_context(nc.Block())
        pairs = BLOCKS // 2

        @block.sync
        def _(sp):
            sp.dma_start(be1[:, :], ins["be1T"]).then_inc(s["b"], 16)

            def load(name, buffer, src, i, b, user, count):
                e = sp.value_load(owner[0:1, bass.ds(i, 1)], min_val=0, max_val=EXP - 1)
                if user:
                    sp.wait_ge(s[user], count)
                sp.dma_start(buffer[:, b, :, :], ins[src][bass.ds(e, 1), :, :].rearrange("e (k p) n -> p (e k) n", p=P))\
                  .then_inc(s[f"{name}_{b}"], 16)

            def step(i, b):
                if not isinstance(i, int) or i + 3 < BLOCKS:
                    load("w1", w1, "we1", i + 3, 1 - b, "hidden", i + 2)
                if not isinstance(i, int) or i + 2 < BLOCKS:
                    load("w2", w2, "we2", i + 2, b, "down", i + 2)
                sp.wait_ge(s["y"], i + 2)
                sp.dma_start(c.slot_rows[bass.ds(i * P, P), :], y[:, b, :]).then_inc(s[f"stored_{b}"], 16)

            for b in range(2):
                load("w1", w1, "we1", b, b, None, 0)
                load("w2", w2, "we2", b, b, None, 0)
            load("w1", w1, "we1", 2, 0, "hidden", 1)
            with sp.Fori(0, pairs - 1) as j:
                for b in range(2):
                    step(j * 2 + b, b)
            for i in range(2 * (pairs - 1), BLOCKS):
                step(i, i % 2)
            for b in range(2):
                sp.wait_ge(s[f"stored_{b}"], 16 * ((BLOCKS + 1 - b) // 2))

        @block.gpsimd
        def _(pool):
            for i in range(BLOCKS):
                if i >= 2:
                    pool.wait_ge(s["turned"], i - 1)
                pool.indirect_dma_start(rows[:, i % 2, :], None, c.norm_rows, bass.IndirectOffsetOnAxis(slots[:, i:i + 1], 0))\
                    .then_inc(s[f"rows_{i % 2}"], 16)

        @block.tensor
        def _(pe):
            pe.sem_inc(s["down"], 1)

            def turn(i, j, b):
                pe.wait_ge(s[f"rows_{b}"], j * 16 + 16)
                pe.wait_ge(s["rowsT"], i)
                for k in range(KC):
                    mm = pe.transpose(psT[:, k * P:(k + 1) * P], rows[:, b, k * P:(k + 1) * P], c.ident[:, :])
                mm.then_inc(s["turned"], 1)

            def hidden(i, j, b):
                pe.wait_ge(s[f"w1_{b}"], j * 16 + 16)
                pe.wait_ge(s["rowsT"], i + 1)
                pe.wait_ge(s["gelu"], (i - 1) * HC if not isinstance(i, int) or i else 0)
                for m in range(HC):
                    for k in range(KC):
                        mm = pe.matmul(psU[:, b, m, :], w1[:, b, k, m * P:(m + 1) * P], rowsT[:, k, :],
                                       start=k == 0, stop=k == KC - 1)
                    if m % (HC // 2) == HC // 2 - 1:
                        mm.then_inc(s["up" if m < HC // 2 else "hidden"], 1)

            def output(i, j, b):
                pe.wait_ge(s[f"w2_{b}"], j * 16 + 16)
                pe.wait_ge(s["gelu"], i * HC + HC)
                pe.wait_ge(s["y"], i)
                for m in range(HC):
                    mm = pe.matmul(psY[:, b, :], hT[:, b, m, :], w2[:, b, m, :], start=m == 0, stop=m == HC - 1)
                mm.then_inc(s["down"], 1)

            turn(0, 0, 0)
            hidden(0, 0, 0)
            turn(1, 0, 1)
            with pe.Fori(0, pairs - 1) as j:
                hidden(j * 2 + 1, j, 1)
                turn(j * 2 + 2, j + 1, 0)
                output(j * 2, j, 0)
                hidden(j * 2 + 2, j + 1, 0)
                turn(j * 2 + 3, j + 1, 1)
                output(j * 2 + 1, j, 1)
            for i in range(2 * (pairs - 1), BLOCKS):
                if i + 1 < BLOCKS:
                    hidden(i + 1, (i + 1) // 2, (i + 1) % 2)
                if i + 2 < BLOCKS:
                    turn(i + 2, (i + 2) // 2, i % 2)
                output(i, i // 2, i % 2)

        @block.scalar
        def _(act):
            act.wait_ge(s["b"], 16)

            def block_gelu(i, b):
                e = act.value_load(owner[0:1, bass.ds(i, 1)], min_val=0, max_val=EXP - 1)
                wait_alone(c, act, s["down"], i)
                for m in range(HC):
                    if m % (HC // 2) == 0:
                        wait_alone(c, act, s["hidden" if m else "up"], i + 1)
                    act.activation(hT[:, b, m, :], psU[:, b, m, :], ACT.Gelu,
                                   bias=be1[:, bass.ds(e * HC + m, 1)]).then_inc(s["gelu"], 1)

            with act.Fori(0, pairs) as j:
                for b in range(2):
                    block_gelu(j * 2 + b, b)
            for i in range(2 * pairs, BLOCKS):
                block_gelu(i, i % 2)

        @block.vector
        def _(dve):
            dve.sem_inc(s["y"], 1)

            dve.wait_ge(s["turned"], 1)
            dve.tensor_copy(rowsT[:, :, :], psT[:, :].rearrange("p (k n) -> p k n", k=KC)).then_inc(s["rowsT"], 1)
            dve.wait_ge(s["hidden"], 1)
            dve.wait_ge(s["turned"], 2)
            dve.tensor_copy(rowsT[:, :, :], psT[:, :].rearrange("p (k n) -> p k n", k=KC)).then_inc(s["rowsT"], 1)

            def later(i, j, b, ahead):
                if ahead:
                    dve.wait_ge(s["hidden"], i + 2)
                    dve.wait_ge(s["turned"], i + 3)
                    dve.tensor_copy(rowsT[:, :, :], psT[:, :].rearrange("p (k n) -> p k n", k=KC)).then_inc(s["rowsT"], 1)
                dve.wait_ge(s["down"], i + 2)
                dve.wait_ge(s[f"stored_{b}"], j * 16)
                dve.tensor_copy(y[:, b, :], psY[:, b, :]).then_inc(s["y"], 1)

            with dve.Fori(0, pairs - 1) as j:
                for b in range(2):
                    later(j * 2 + b, j, b, True)
            for i in range(2 * (pairs - 1), BLOCKS):
                later(i, i // 2, i % 2, i + 2 < BLOCKS)


def stage_combine(c, route):
    nc = c.nc
    share, slot_of, slots, owner = route
    depth = 8
    with ExitStack() as st:
        got = st.enter_context(nc.sbuf_tensor("c_got", [P, depth, D], F32))
        s_got = [c.sem(f"c_got{i}") for i in range(depth)]
        s_used, s_out = c.sem("c_used"), c.sem("c_out")
        block = st.enter_context(nc.Block())

        @block.gpsimd
        def _(pool):
            for t in range(NT):
                for i in range(CHOICES):
                    n, r = t * CHOICES + i, rows_of(t)
                    if n >= depth:
                        pool.wait_ge(s_used, n - depth + 1)
                    pool.indirect_dma_start(got[0:r, n % depth, :], None, c.slot_rows,
                                            bass.IndirectOffsetOnAxis(slot_of[0:r, i, t:t + 1], 0)).then_inc(s_got[n % depth], 16)

        @block.vector
        def _(dve):
            for t in range(NT):
                for i in range(CHOICES):
                    n, r = t * CHOICES + i, rows_of(t)
                    dve.wait_ge(s_got[n % depth], 16 * (n // depth + 1))
                    dve.drain()
                    dve.scalar_tensor_tensor(out=c.x[0:r, t, :], in0=got[0:r, n % depth, :], scalar=share[0:r, i, t:t + 1],
                                             in1=c.x[0:r, t, :], op0=ALU.mult, op1=ALU.add).then_inc(s_used, 1)

        @block.sync
        def _(sp):
            for t in range(NT):
                r = rows_of(t)
                sp.wait_ge(s_used, CHOICES * (t + 1))
                sp.dma_start(c.out[t * P:t * P + r, :], c.x[0:r, t, :]).then_inc(s_out, 16)
            sp.wait_ge(s_out, 16 * NT)


def stage_experts(c):
    with ExitStack() as st:
        sb = lambda n, s, d: st.enter_context(c.nc.sbuf_tensor("x_" + n, s, d))
        route = (sb("share", [P, CHOICES, NT], F32), sb("slot_of", [P, CHOICES, NT], U32), sb("slots", [P, BLOCKS], U32),
                 sb("owner", [P, BLOCKS], I32))
        transposed_norm(c, "n4_", c.norm_rows)
        c.end_stage()
        stage_gate(c, route)
        c.end_stage()
        stage_expert_layers(c, route)
        c.end_stage()
        stage_combine(c, route)
        c.end_stage()


def build(nc, ins, out):
    with ExitStack() as ctx:
        c = Core(nc, ctx, ins, out)
        with ExitStack() as first:
            keep = tuple(first.enter_context(nc.sbuf_tensor(n, sh, F32)) for n, sh in
                         (("xn", [P, NT, D]), ("kv", [P, KC, D]), ("mean_row", [P, D])))
            stage_prepare(c, keep)
            c.end_stage()
            stage_graph(c, keep)
            c.end_stage()
        stage_memory(c)
        c.end_stage()
        stage_attention(c)
        stage_experts(c)


def host_layout(a):
    import numpy as np

    def cc(v):
        return np.ascontiguousarray(v)

    def T(v):
        return cc(np.asarray(v).T)

    return {
        "x": cc(a["x"]), "src": cc(a["src"]), "dst": cc(a["dst"]),
        "W_selfT": T(a["L0_gnn_W_self"]), "W_neighT": T(a["L0_gnn_W_neigh"]),
        "bias": cc(a["L0_gnn_bias"]), "gamma": cc(a["L0_gnn_gamma"]), "beta": cc(a["L0_gnn_beta"]),
        "W_vT": T(a["L0_mix_W_v"]), "W_thetaT": T(a["L0_mix_W_theta"]),
        "Wq": cc(a["L0_ffn_Wq"]), "bqT": T(np.asarray(a["L0_ffn_bq"]).reshape(HEADS, P)),
        "keysT": cc(np.asarray(a["L0_ffn_keys"]).transpose(1, 3, 0, 2)),
        "mix_qkT": T(np.asarray(a["L1_mix_w_qkv"])[0:2 * D]), "mix_v": cc(np.asarray(a["L1_mix_w_qkv"])[2 * D:]),
        "mix_outT": T(a["L1_mix_w_out"]), "b_out": cc(a["L1_mix_b_out"]),
        "W_qkvT": T(a["L1_gnn_W_qkv"]), "W_ffT": T(a["L1_gnn_W_ff"]), "b_ff": cc(a["L1_gnn_b_ff"]),
        "b_qkT": T(np.asarray(a["L1_gnn_b_qkv"])[0:2 * D].reshape(2 * PAIRS, P)), "b_v": cc(np.asarray(a["L1_gnn_b_qkv"])[2 * D:]),
        "gw1": cc(a["L1_ffn_gw1"]), "gb1T": T(np.asarray(a["L1_ffn_gb1"]).reshape(2, P)), "gw2": cc(a["L1_ffn_gw2"]),
        "gb2": cc(a["L1_ffn_gb2"]), "we1": cc(a["L1_ffn_we1"]), "we2": cc(a["L1_ffn_we2"]), "be2": cc(a["L1_ffn_be2"]),
        "be1T": T(np.asarray(a["L1_ffn_be1"]).reshape(EXP * HC, P)),
        "table": np.concatenate([np.asarray(a["L0_ffn_w_down"]), np.asarray(a["L0_ffn_w_up"])], axis=1),
    }


def kernel(**inputs):
    import concourse.bacc as bacc
    from concourse.bass_utils import run_bass_kernel_spmd

    arrays = host_layout(inputs)
    nc = bacc.Bacc("TRN2", target_bir_lowering=False, num_devices=1)
    ins = {name: nc.dram_tensor("in_" + name, a.shape, mybir.dt.from_np(a.dtype), kind="ExternalInput").ap()
           for name, a in arrays.items()}
    out = nc.dram_tensor("out", (N, D), F32, kind="ExternalOutput").ap()
    build(nc, ins, out)
    return run_bass_kernel_spmd(nc, [{"in_" + name: a for name, a in arrays.items()}], core_ids=[0]).results[0]["out"]
```

```python
from contextlib import ExitStack

import concourse.bass as bass
from concourse import mybir

F32 = mybir.dt.float32
F32R = mybir.dt.float32r
BF16 = mybir.dt.bfloat16
F16 = mybir.dt.float16
I32 = mybir.dt.int32
U32 = mybir.dt.uint32
U16 = mybir.dt.uint16
ALU = mybir.AluOpType
ACT = mybir.ActivationFunctionType
AX = mybir.AxisListType.X

P = 128
N = 1250
NT = -(-N // P)
NP = NT * P
TAIL = N - (NT - 1) * P
D = 512
KC = D // P
E = 20000
EPAIR = 250
EC = EPAIR // 2
NG = E // EPAIR
HEADS = 8
NKEYS = 256
TOPK = 8
EXP = 8
HID = 1024
HC = HID // P
SPLIT = 4
EPS = 1e-5
NEG = -1e30
CHUNKS = [(0, 512), (512, 512), (1024, 256)]


class Core:

    def __init__(self, nc, ctx, ins, out):
        self.nc, self.ctx, self.ins, self.out = nc, ctx, ins, out
        self.x = ctx.enter_context(nc.sbuf_tensor("x_rows", [P, NT, D], F32))
        self.xnT = ctx.enter_context(nc.sbuf_tensor("xnT", [P, KC, NP], F32))
        self.ident = ctx.enter_context(nc.sbuf_tensor("ident", [P, P], F32))
        self.shares = nc.dram_tensor("edge_shares", (NT, P, NT, P), F32, kind="Internal").ap()
        self.qk_parts = nc.dram_tensor("qk_parts", (2 * HEADS, 2, D // HEADS, NP), F32, kind="Internal").ap()
        self.masks = nc.dram_tensor("edge_masks", (NT, P, NP), BF16, kind="Internal").ap()
        self.counts = nc.dram_tensor("edge_counts", (NT, P, NP), U16, kind="Internal").ap()

        self.norm_rows = nc.dram_tensor("norm_rows", (NP, D), F32, kind="Internal").ap()
        self.slot_list = nc.dram_tensor("slot_list", (BLOCKS * P, 1), U32, kind="Internal").ap()
        self.slot_rows = nc.dram_tensor("slot_rows", (BLOCKS * P, D), F32, kind="Internal").ap()
        self.live = []
        self.stage, self.passed = 0, None

    def sem(self, name):
        self.live.append(self.nc.alloc_semaphore(name=name))
        return self.live[-1]

    def end_stage(self):
        self.nc.clear_and_free_semaphores(self.live)
        self.live, self.passed = [], None
        self.nc.all_engine_barrier()


class RowStats:

    def __init__(self, c, st, tag):
        sb = lambda n, s: st.enter_context(c.nc.sbuf_tensor(tag + n, s, F32))
        self.c, self.stats, self.mv, self.rstd = c, sb("stats", [P, NT, 6]), sb("mv", [P, NT, 2]), sb("rstd", [P, NT])
        self.root = sb("root", [P, NT])
        self.s_mv, self.s_root = c.sem(tag + "moments"), c.sem(tag + "root")

    def moments(self, dve, part):
        lo, hi = ((0, SPLIT), (SPLIT, NT))[part]
        for t in range(lo, hi):
            dve.bn_stats(self.stats[:, t, :], self.c.x[:, t, :])
        dve.drain()
        for t in range(lo, hi):
            dve.bn_aggr(self.mv[:, t, :], self.stats[:, t, :])
        dve.drain()
        dve.tensor_scalar(self.rstd[:, lo:hi], self.mv[:, lo:hi, 1], EPS, None, ALU.add).then_inc(self.s_mv, 1)
        dve.wait_ge(self.s_root, part + 1)
        dve.reciprocal(self.rstd[:, lo:hi], self.root[:, lo:hi])
        dve.drain()

    def roots(self, act):
        for part, (lo, hi) in enumerate(((0, SPLIT), (SPLIT, NT))):
            act.wait_ge(self.s_mv, part + 1)
            act.activation(self.root[:, lo:hi], self.rstd[:, lo:hi], ACT.Sqrt).then_inc(self.s_root, 1)

    def normalise(self, dve, t, dst):
        one = bass.ds(t, 1)
        return dve.tensor_scalar(dst, self.c.x[:, one, :], self.mv[:, one, 0], self.rstd[:, one], ALU.subtract, ALU.mult)


def wait_alone(c, eng, sem, value):
    eng.wait_ge(sem, value)
    if c.passed is None:
        c.stage += 1
        c.passed = c.sem(f"passed{c.stage}")
    eng.sem_inc(c.passed, 1)


def column(t):
    return bass.ds(t * P, P)


def stage_prepare(c, keep, ahead):
    nc, ins = c.nc, c.ins
    neigh, kv = keep
    ws, keys, bias, gamma = ahead
    with ExitStack() as st:
        sb = lambda n, s, d=F32: st.enter_context(nc.sbuf_tensor(n, s, d))
        ps = lambda n, s: st.enter_context(nc.psum_tensor(n, s, F32))
        wv, wth, wn = sb("wv", [P, KC, D]), sb("wth", [P, KC, D]), sb("wn", [P, KC, D])
        rows, beta = sb("rows", [P, 2, D]), sb("beta", [P, D])
        norm = RowStats(c, st, "p_")
        gram, m1 = sb("gram", [P, KC, D]), sb("m1", [P, KC, D])
        xsum, xbar, ones = sb("xsum", [P, KC]), sb("xbar", [P, KC, P]), sb("ones", [P, P])
        edge_i, edge_f = sb("edge_i", [NG, 2, EPAIR], I32), sb("edge_f", [NG, 2, EPAIR])
        ends = sb("ends", [NG, 2])
        edges = sb("edges", [EC, 4, 2 * NG])
        shifted = sb("shifted", [EC, 2, 2 * NG])
        row = sb("row", [1, 6, NT * NG], F16)
        group_i, group_id = sb("group_i", [1, NG], I32), sb("group_id", [1, NG])
        tile_i, tile_lo, tile_hi = sb("tile_i", [P, NT], I32), sb("tile_lo", [P, NT]), sb("tile_hi", [P, NT])
        bounds_f, bounds, many_u = sb("bounds_f", [1, 5, NT]), sb("bounds", [1, 2 * NT], U32), sb("many", [1, NT], U32)
        node_i, node_id = sb("node_i", [P, NP], I32), sb("node_id", [P, NP], F16)
        zero = sb("zero", [P, D], BF16)
        hot_dst, hot_src = sb("hot_dst", [EC, 4, P], BF16), sb("hot_src", [EC, 4, NP], BF16)
        cnt, cnt16, mask, share, shareT = sb("cnt", [P, 2, NP]), sb("cnt16", [P, NP], U16), sb("mask", [P, NP], BF16), sb("share", [P, NP]), sb("shareT", [P, NT, P])
        deg, rdeg = sb("deg", [P, 2]), sb("rdeg", [P, 2])
        psB, psT = ps("psB", [P, 6, D]), ps("psT", [P, 2, D])
        names = ("tail", "x0", "x", "edges_in", "w", "ahead", "id0", "id", "ones", "zero", "const", "edge_f", "ends", "edge_tr",
                 "edges", "bounds", "rows", "tr", "tdone", "gram", "gdone", "gout", "bar", "mm", "ev", "mean", "near", "nout",
                 "hot", "hot_free", "cnt", "cnt_out", "cnt16", "deg", "share", "turned", "turned_out", "stored", "kept")
        s = {n: c.sem("p_" + n) for n in names}
        block = st.enter_context(nc.Block())
        C2 = [psB[:, 3 * b:3 * b + 3, :].rearrange("p a n -> p (a n)") for b in range(2)]

        @block.sync
        def _(sp):
            sp.dma_start(edge_i[:, 0, :], ins["src"].rearrange("(g e) -> g e", g=NG)).then_inc(s["edges_in"], 16)
            sp.dma_start(edge_i[:, 1, :], ins["dst"].rearrange("(g e) -> g e", g=NG)).then_inc(s["edges_in"], 16)
            for name, lo, hi in (("x0", 0, SPLIT), ("x", SPLIT, NT - 1)):
                sp.dma_start(c.x[:, lo:hi, :], ins["x"][lo * P:hi * P, :].rearrange("(t p) d -> p t d", p=P)).then_inc(s[name], 16)
            sp.wait_ge(s["tail"], 1)
            sp.dma_start(c.x[0:TAIL, NT - 1, :], ins["x"][(NT - 1) * P:N, :]).then_inc(s["x"], 16)
            for w, name in ((wv, "W_vT"), (wth, "W_thetaT"), (wn, "W_neighT")):
                sp.dma_start(w[:, :, :], ins[name].rearrange("(k p) n -> p k n", p=P)).then_inc(s["w"], 16)
            sp.dma_start(beta[:, :], ins["beta"].partition_broadcast(P)).then_inc(s["w"], 16)
            sp.dma_start(ws[:, :, :], ins["W_selfT"].rearrange("(k p) n -> p k n", p=P)).then_inc(s["ahead"], 16)
            for dst, name in ((bias, "bias"), (gamma, "gamma")):
                sp.dma_start(dst[:, :], ins[name].partition_broadcast(P)).then_inc(s["ahead"], 16)
            for i in range(2):
                sp.dma_start(keys[64 * i:64 * i + 64, :, :], ins["keysT"][i]).then_inc(s["ahead"], 16)
            with sp.Fori(0, NT) as t:
                sp.wait_ge(s["cnt16"], t * 2 + 1)
                sp.dma_start(c.counts[bass.ds(t, 1), :, :].rearrange("a p n -> p (a n)"), cnt16[:, :]).then_inc(s["stored"], 16)
                sp.wait_ge(s["cnt16"], t * 2 + 2)
                sp.dma_start(c.masks[bass.ds(t, 1), :, :].rearrange("a p n -> p (a n)"), mask[:, :]).then_inc(s["stored"], 16)
                wait_alone(c, sp, s["turned_out"], t * 3 + 3)
                sp.dma_start(c.shares[bass.ds(t, 1), :, :, :].rearrange("u p a n -> p (u a) n"), shareT[:, :, :]).then_inc(s["kept"], 16)
            sp.wait_ge(s["stored"], 32 * NT)
            sp.wait_ge(s["kept"], 16 * NT)
            sp.wait_ge(s["ahead"], 80)

        @block.gpsimd
        def _(pool):
            pool.memset(c.x[96:P, NT - 1, :], 0.0).then_inc(s["tail"], 1)
            pool.wait_ge(s["tail"], 1)
            pool.memset(c.ident[:, :], 0.0).then_inc(s["id0"], 1)
            pool.wait_ge(s["id0"], 1)
            pool.affine_select(out=c.ident[:, :], in_=c.ident[:, :], compare_op=ALU.not_equal, fill=1.0,
                               base=0, pattern=[[-1, P]], channel_multiplier=1).then_inc(s["id"], 1)
            pool.memset(ones[:, :], 1.0).then_inc(s["ones"], 1)
            pool.memset(zero[:, :], 0.0).then_inc(s["zero"], 1)
            pool.iota(group_i[:, :], pattern=[[1, NG]], base=0, channel_multiplier=0).then_inc(s["const"], 1)
            pool.iota(tile_i[:, :], pattern=[[P, NT]], base=0, channel_multiplier=0).then_inc(s["const"], 1)
            pool.iota(node_i[:, :], pattern=[[1, NP]], base=0, channel_multiplier=0).then_inc(s["const"], 1)
            pool.wait_ge(s["const"], 3)
            pool.tensor_copy(group_id[:, :], group_i[:, :]).then_inc(s["const"], 1)
            pool.tensor_copy(tile_lo[:, :], tile_i[:, :]).then_inc(s["const"], 1)
            pool.tensor_copy(node_id[:, :], node_i[:, :]).then_inc(s["const"], 1)
            with pool.Fori(0, NT // 2) as j:
                for b in range(2):
                    t = j * 2 + b
                    pool.wait_ge(s["cnt_out"], t + 1)
                    wait_alone(c, pool, s["stored"], t * 32)
                    pool.tensor_copy(cnt16[:, :], cnt[:, b, :]).then_inc(s["cnt16"], 1)
                    pool.tensor_scalar(mask[:, :], cnt[:, b, :], 0.0, NEG, ALU.is_equal, ALU.mult).then_inc(s["cnt16"], 1)

        @block.vector
        def _(dve):
            dve.wait_ge(s["edges_in"], 32)
            dve.tensor_copy(edge_f[:, :, :], edge_i[:, :, :]).then_inc(s["edge_f"], 1)
            dve.drain()
            dve.tensor_reduce(ends[:, 0:1], edge_f[:, 1, :], AX, ALU.min)
            dve.tensor_reduce(ends[:, 1:2], edge_f[:, 1, :], AX, ALU.max).then_inc(s["ends"], 1)
            dve.wait_ge(s["edge_tr"], 1)
            dve.memset(edges[:, :, NG:2 * NG], -2.0 * NP)
            dve.tensor_copy(edges[:, :, 0:NG], psT[0:EC, 0, 0:4 * NG].rearrange("p (a g) -> p a g", a=4)).then_inc(s["edges"], 1)
            r = [row[0:1, i, :].rearrange("p (t g) -> p t g", t=NT) for i in range(6)]
            lowest = row[0:1, 4, 0:NG].unsqueeze(1).to_broadcast([1, NT, NG])
            highest = row[0:1, 5, 0:NG].unsqueeze(1).to_broadcast([1, NT, NG])
            gid = group_id[0:1, :].unsqueeze(1).to_broadcast([1, NT, NG])
            dve.tensor_copy(row[0:1, 4, 0:NG], psT[0:1, 1, 0:NG])
            dve.tensor_copy(row[0:1, 5, 0:NG], psT[0:1, 1, NG:2 * NG]).then_inc(s["edges"], 1)
            dve.wait_ge(s["x0"], 16)
            norm.moments(dve, 0)
            for b in range(2):
                norm.normalise(dve, b, rows[:, b, :]).then_inc(s["rows"], 1)
            dve.wait_ge(s["x"], 32)
            norm.moments(dve, 1)
            with dve.Fori(1, NT // 2) as j:
                for b in range(2):
                    dve.wait_ge(s["gram"], j * 2 + b)
                    norm.normalise(dve, j * 2 + b, rows[:, b, :]).then_inc(s["rows"], 1)
            dve.wait_ge(s["const"], 6)
            dve.tensor_scalar(tile_hi[:, :], tile_lo[:, :], float(P - 1), None, ALU.add)
            dve.drain()
            dve.tensor_tensor(r[0], highest, tile_lo[0:1, :].unsqueeze(2).to_broadcast([1, NT, NG]), ALU.is_ge)
            dve.tensor_tensor(r[1], tile_hi[0:1, :].unsqueeze(2).to_broadcast([1, NT, NG]), lowest, ALU.is_ge)
            dve.drain()
            dve.tensor_tensor(r[2], r[0], r[1], ALU.mult)
            dve.drain()
            dve.scalar_tensor_tensor(out=r[0], in0=r[2], scalar=-1000.0, in1=gid, op0=ALU.mult, op1=ALU.add)
            dve.scalar_tensor_tensor(out=r[1], in0=gid, scalar=1.0, in1=r[2], op0=ALU.add, op1=ALU.mult)
            dve.drain()
            dve.tensor_reduce(bounds_f[:, 0, :], r[0], AX, ALU.min)
            dve.tensor_reduce(bounds_f[:, 1, :], r[1], AX, ALU.max)
            dve.drain()
            dve.tensor_scalar(bounds_f[:, 2, :], bounds_f[:, 0, :], 0.0, 1000.0, ALU.is_lt, ALU.mult)
            dve.drain()
            dve.tensor_tensor(bounds_f[:, 0, :], bounds_f[:, 0, :], bounds_f[:, 2, :], ALU.add)
            dve.drain()
            dve.tensor_tensor(bounds_f[:, 3, :], bounds_f[:, 1, :], bounds_f[:, 0, :], ALU.subtract)
            dve.drain()
            dve.tensor_scalar(many_u[:, :], bounds_f[:, 3, :], 1.0, 1.0, ALU.max, ALU.add)
            dve.drain()
            dve.tensor_scalar(bounds[:, NT:2 * NT], many_u[:, :], 1, None, ALU.logical_shift_right)
            dve.tensor_copy(bounds[:, 0:NT], bounds_f[:, 0, :]).then_inc(s["bounds"], 1)
            dve.wait_ge(s["tdone"], NT)
            dve.tensor_reduce(xsum[:, :], c.xnT[:, :, :], AX, ALU.add)
            dve.wait_ge(s["ones"], 1)
            dve.drain()
            for k in range(KC):
                bar = dve.tensor_scalar(xbar[:, k, :], ones[:, :], xsum[:, k:k + 1], 1.0 / N, ALU.mult, ALU.mult)
            bar.then_inc(s["bar"], 1)
            dve.wait_ge(s["bounds"], 1)
            done = dve.alloc_register("groups_done")
            dve.reg_mov(done, 0)
            def one_hots(t):
                first = dve.value_load(bounds[0:1, bass.ds(t, 1)], min_val=0, max_val=NG - 1)
                many = dve.value_load(bounds[0:1, bass.ds(t + NT, 1)], min_val=1, max_val=NG // 2)
                before = dve.snap(done)
                dve.drain()
                dve.tensor_scalar(shifted[:, :, :], edges[:, 2:4, :], tile_lo[0:EC, bass.ds(t, 1)], None, ALU.subtract)
                dve.drain()
                with dve.Fori(0, many) as i:
                    for j in range(4):
                        at = bass.ds(first + i * 2 + j // 2, 1)
                        dve.wait_ge(s["hot_free"], (before + i) * 4 + (j + 1))
                        dve.tensor_scalar(hot_dst[:, j, :], node_id[0:EC, 0:P], shifted[:, j % 2, at], None, ALU.is_equal)
                        dve.tensor_scalar(hot_src[:, j, :], node_id[0:EC, :], edges[:, j % 2, at], None,
                                          ALU.is_equal).then_inc(s["hot"], 1)
                dve.reg_add(done, done, many)

            def degrees(t, b):
                dve.wait_ge(s["cnt_out"], t + 1)
                dve.tensor_scalar(rdeg[:, b:b + 1], deg[:, b:b + 1], 1.0, None, ALU.max)
                dve.drain()
                dve.reciprocal(rdeg[:, b:b + 1], rdeg[:, b:b + 1]).then_inc(s["deg"], 1)

            one_hots(0)
            one_hots(1)
            degrees(0, 0)
            with dve.Fori(1, NT // 2) as k:
                for b in range(2):
                    one_hots(k * 2 + b)
                    degrees(k * 2 + (b - 1), 1 - b)
            degrees(NT - 1, 1)
            dve.wait_ge(s["mm"], 2 * KC + 1)
            dve.wait_ge(s["w"], 64)
            dve.tensor_tensor(beta[:, :], beta[:, :], psT[:, 1, :], ALU.add).then_inc(s["mean"], 1)
            dve.drain()
            dve.tensor_tensor(c.x[:, :, :], c.x[:, :, :], beta[:, :].unsqueeze(1).to_broadcast([P, NT, D]), ALU.add)

        @block.scalar
        def _(act):
            norm.roots(act)
            with act.Fori(0, NT // 2) as j:
                for b in range(2):
                    wait_alone(c, act, s["tr"], j * 2 + (b + 1))
                    act.activation(c.xnT[:, :, column(j * 2 + b)], psT[:, b, :].rearrange("p (k n) -> p k n", k=KC),
                                   ACT.Copy).then_inc(s["tdone"], 1)
            act.wait_ge(s["gdone"], 1)
            for m in range(KC):
                act.activation(gram[:, m, :], psB[:, m, :], ACT.Copy).then_inc(s["gout"], 1)
            for m in range(2 * KC):
                act.wait_ge(s["mm"], m + 1)
                dst, scale = (m1, 1.0) if m < KC else (kv, 1.0 / (N * D ** 0.5))
                act.activation(dst[:, m % KC, :], psB[:, 4 + m % 2, :], ACT.Copy, scale=scale).then_inc(s["ev"], 1)

            def turned(t):
                wait_alone(c, act, s["kept"], t * 16)
                for g in range(3):
                    n = min(4, NT - 4 * g)
                    act.wait_ge(s["turned"], t * 3 + (g + 1))
                    act.activation(shareT[:, 4 * g:4 * g + n, :], psT[:, g % 2, 0:n * P].rearrange("p (a n) -> p a n", a=n),
                                   ACT.Copy).then_inc(s["turned_out"], 1)

            def counts(t, b):
                act.wait_ge(s["cnt"], t + 1)
                if not isinstance(t, int):
                    act.wait_ge(s["cnt16"], t * 2 - 2)
                    act.wait_ge(s["share"], t - 1)
                act.activation(cnt[:, b, :], C2[b][:, 0:NP], ACT.Copy, accum_out=deg[:, b:b + 1]).then_inc(s["cnt_out"], 1)

            def shares(t, b):
                act.wait_ge(s["deg"], t + 1)
                act.activation(share[:, :], cnt[:, b, :], ACT.Copy, scale=rdeg[:, b:b + 1]).then_inc(s["share"], 1)

            counts(0, 0)
            counts(1, 1)
            shares(0, 0)
            with act.Fori(1, NT // 2) as j:
                for b in range(2):
                    counts(j * 2 + b, b)
                    turned(j * 2 + (b - 2))
                    shares(j * 2 + (b - 1), 1 - b)
            turned(NT - 2)
            shares(NT - 1, 1)
            turned(NT - 1)
            for t in range(NT):
                act.wait_ge(s["near"], t + 1)
                act.activation(neigh[:, t, :], psB[:, t % 2, :], ACT.Copy).then_inc(s["nout"], 1)
            act.wait_ge(s["nout"], NT)

        @block.tensor
        def _(pe):
            pe.wait_ge(s["id"], 1)
            pe.wait_ge(s["edge_f"], 1)
            for a in range(4):
                pe.transpose(psT[0:EC, 0, a * NG:(a + 1) * NG], edge_f[:, a // 2, a % 2 * EC:(a % 2 + 1) * EC],
                             c.ident[0:NG, 0:NG])
            pe.wait_ge(s["ends"], 1)
            for a in range(2):
                mm = pe.matmul(psT[0:1, 1, a * NG:(a + 1) * NG], ends[:, a:a + 1], c.ident[0:NG, 0:NG], start=True, stop=True)
            mm.then_inc(s["edge_tr"], 1)
            pe.wait_ge(s["edges"], 2)
            pe.sem_inc(s["gram"], 1)

            def tile(t, b, first):
                pe.wait_ge(s["rows"], t + 1)
                if not first:
                    pe.wait_ge(s["tdone"], t - 1)
                for k in range(KC):
                    mm = pe.transpose(psT[:, b, k * P:(k + 1) * P], rows[:, b, k * P:(k + 1) * P], c.ident[:, :])
                mm.then_inc(s["tr"], 1)
                for m in range(KC):
                    mm = pe.matmul(psB[:, m, :], rows[:, b, m * P:(m + 1) * P], rows[:, b, :], start=first and b == 0,
                                   stop=True, skip_group_check=True)
                mm.then_inc(s["gram"], 1)

            for b in range(2):
                tile(b, b, True)
            with pe.Fori(1, NT // 2) as j:
                for b in range(2):
                    tile(j * 2 + b, b, False)
            pe.wait_ge(s["w"], 64)
            pe.matmul(psB[:, 4, 0:P], c.ident[:, :], c.ident[:, :], start=True, stop=True).then_inc(s["gdone"], 1)
            for m in range(2 * KC):
                left, right = (gram, wv) if m < KC else (wth, m1)
                if m < KC:
                    pe.wait_ge(s["gout"], KC)
                if m >= 2:
                    pe.wait_ge(s["ev"], m - 1)
                if m == KC:
                    pe.wait_ge(s["ev"], KC)
                for k in range(KC):
                    mm = pe.matmul(psB[:, 4 + m % 2, :], left[:, k, m % KC * P:(m % KC + 1) * P], right[:, k, :],
                                   start=k == 0, stop=k == KC - 1)
                mm.then_inc(s["mm"], 1)
            pe.wait_ge(s["ev"], 2 * KC)
            pe.wait_ge(s["tdone"], NT)
            pe.wait_ge(s["zero"], 1)
            pe.sem_inc(s["hot_free"], 4)
            pe.wait_ge(s["bounds"], 1)
            done = pe.alloc_register("groups_done")
            pe.reg_mov(done, 0)

            def count(t, b):
                many = pe.value_load(bounds[0:1, bass.ds(t + NT, 1)], min_val=1, max_val=NG // 2)
                before = pe.snap(done)
                if not isinstance(t, int):
                    pe.wait_ge(s["cnt_out"], t - 1)
                for a, n in CHUNKS:
                    pe.matmul(C2[b][:, a:a + n], zero[:, 0:P], zero[:, 0:n], start=True, stop=True, skip_group_check=True)
                with pe.Fori(0, many) as i:
                    for j in range(4):
                        pe.wait_ge(s["hot"], (before + i) * 4 + (j + 1))
                        for a, n in CHUNKS:
                            mm = pe.matmul(C2[b][:, a:a + n], hot_dst[:, j, :], hot_src[:, j, a:a + n], start=False,
                                           stop=True, skip_group_check=True)
                        mm.then_inc(s["hot_free"], 1)
                pe.reg_add(done, done, many)
                pe.matmul(C2[b][:, 0:P], zero[:, 0:P], zero[:, 0:P], start=False, stop=True,
                          skip_group_check=True).then_inc(s["cnt"], 1)

            def turn(t):
                pe.wait_ge(s["share"], t + 1)
                for g in range(3):
                    pe.wait_ge(s["turned_out"], t * 3 + (g - 1) if g else t * 3)
                    for a in range(4 * g, min(4 * g + 4, NT)):
                        mm = pe.transpose(psT[:, g % 2, a % 4 * P:(a % 4 + 1) * P], share[:, a * P:(a + 1) * P], c.ident[:, :])
                    mm.then_inc(s["turned"], 1)

            count(0, 0)
            count(1, 1)
            with pe.Fori(1, NT // 2) as j:
                for b in range(2):
                    count(j * 2 + b, b)
                    turn(j * 2 + (b - 2))
            turn(NT - 2)
            turn(NT - 1)
            pe.wait_ge(s["cnt_out"], NT)
            pe.wait_ge(s["turned_out"], 3 * NT)
            pe.wait_ge(s["bar"], 1)
            for k in range(KC):
                mm = pe.matmul(psT[:, 1, :], xbar[:, k, :], wv[:, k, :], start=k == 0, stop=k == KC - 1)
            mm.then_inc(s["mm"], 1)
            for t in range(NT):
                if t >= 2:
                    pe.wait_ge(s["nout"], t - 1)
                for k in range(KC):
                    mm = pe.matmul(psB[:, t % 2, :], c.xnT[:, k, t * P:(t + 1) * P], wn[:, k, :], start=k == 0, stop=k == KC - 1)
                mm.then_inc(s["near"], 1)


RING = 16
AHEAD = RING // TOPK
LEAD = 3
PRODUCTS = 2 * KC + NT
EACH = 3
EARLY = HEADS - PRODUCTS // EACH


def stage_layer0(c, keep, ahead):
    nc, ins = c.nc, c.ins
    neigh, kv = keep
    ws, keys, bias, gamma = ahead
    with ExitStack() as st:
        sb = lambda n, s, d=F32: st.enter_context(nc.sbuf_tensor("m_" + n, s, d))
        ps = lambda n, s: st.enter_context(nc.psum_tensor("m_" + n, s, F32))
        ring = sb("ring", [P, RING, 2 * D])
        wq, bq = sb("wq", [P, KC, HEADS * P]), sb("bq", [P, HEADS])
        xt, share, h_sum = sb("xt", [P, KC, P]), sb("share", [P, NT, P]), sb("h_sum", [P, D])
        stats, mv, rstd, root = sb("stats", [P, 6]), sb("mv", [P, 2]), sb("rstd", [P, 1]), sb("root", [P, 1])
        stats1, mv1, rstd1, root1 = sb("stats1", [P, 6]), sb("mv1", [P, 2]), sb("rstd1", [P, 1]), sb("root1", [P, 1])
        coming, current, xT = sb("coming", [P, D]), sb("current", [P, D]), sb("xT", [P, KC, P])
        qz = sb("qz", [P, 2, 2, P])
        product = sb("product", [P, D])
        diag = sb("diag", [P, AHEAD * TOPK, P])
        top, top_at, top_id = sb("top", [P, 2, TOPK]), sb("top_at", [P, 2, TOPK], U32), sb("top_id", [P, 2, TOPK])
        pairs, best = sb("pairs", [P, TOPK, TOPK]), sb("best", [P, HEADS, TOPK])
        best_at, side, side_f = sb("best_at", [P, TOPK], U32), sb("side", [P, 2, TOPK], U32), sb("side_f", [P, 2, TOPK])
        pick, chosen = sb("pick", [P, 2, TOPK, TOPK]), sb("chosen", [P, 2, TOPK])
        number_i, number = sb("number_i", [P, TOPK], I32), sb("number", [P, TOPK])
        rows_at = sb("rows_at", [P, HEADS, TOPK], U32)
        lowest, expo, total = sb("lowest", [P, HEADS]), sb("expo", [P, HEADS, TOPK]), sb("total", [P, HEADS])
        inner, part, rtotal = sb("inner", [P, TOPK]), sb("part", [P, TOPK]), sb("rtotal", [P, 1])
        weight = sb("weight", [P, AHEAD, TOPK])
        psT, psQ, psS, acc, psH = ps("psT", [P, D]), ps("psQ", [P, 2, D]), ps("psS", [P, 2, D]), ps("acc", [P, D]), ps("psH", [P, 2, D])
        names = ("w", "qz0", "number0", "number", "xt", "share_in", "layer", "moments", "root", "x1", "moments1", "root1",
                 "coming", "tr", "xT", "q", "qT", "score", "found", "soft", "weight", "diag", "slot_free", "x2")
        s = {n: c.sem("m_" + n) for n in names}
        s_land = [c.sem(f"m_landed{i}") for i in range(RING)]
        block = st.enter_context(nc.Block())

        def wait(eng, name, value):
            if not isinstance(value, int) or value > 0:
                eng.wait_ge(s[name], value)

        @block.sync
        def _(sp):
            sp.dma_start(wq[:, :, :], ins["Wq"].rearrange("(k p) n -> p k n", p=P)).then_inc(s["w"], 16)
            sp.dma_start(bq[:, :], ins["bqT"]).then_inc(s["w"], 16)
            with sp.Fori(0, NT) as t:
                sp.wait_ge(s["layer"], t)
                sp.dma_start(share[:, :, :], c.shares[bass.ds(t, 1), :, :, :].rearrange("u p a n -> p (u a) n")).then_inc(s["share_in"], 16)

        @block.gpsimd
        def _(pool):
            pool.memset(qz[:, :, :, :], 0.0).then_inc(s["qz0"], 1)
            pool.iota(number_i[:, :], pattern=[[1, TOPK]], base=0, channel_multiplier=0).then_inc(s["number0"], 1)
            pool.wait_ge(s["number0"], 1)
            pool.tensor_copy(number[:, :], number_i[:, :]).then_inc(s["number"], 1)
            with pool.Fori(0, NT) as t:
                for h in range(HEADS):
                    pool.wait_ge(s["found"], t * HEADS + (h + 1))
                    for k in range(TOPK):
                        slot = (h * TOPK + k) % RING
                        wait_alone(c, pool, s["slot_free"], t * (HEADS * TOPK) + (h * TOPK + k + 1))
                        pool.indirect_dma_start(ring[:, slot, :], None, ins["table"],
                                                bass.IndirectOffsetOnAxis(rows_at[:, h, k:k + 1], 0)).then_inc(s_land[slot], 16)

        def search(dve, h, nth):
            wait_alone(c, dve, s["score"], nth + 1)
            b = h % 2
            for i in range(2):
                dve.max(top[:, i, :], psS[:, b, NKEYS * i:NKEYS * (i + 1)])
            dve.drain()
            for i in range(2):
                dve.max_index(top_at[:, i, :], top[:, i, :], psS[:, b, NKEYS * i:NKEYS * (i + 1)])
            dve.tensor_tensor(pairs[:, :, :], top[:, 0, :].unsqueeze(2).to_broadcast([P, TOPK, TOPK]),
                              top[:, 1, :].unsqueeze(1).to_broadcast([P, TOPK, TOPK]), ALU.add)
            dve.drain()
            dve.tensor_copy(top_id[:, :, :], top_at[:, :, :])
            dve.max(best[:, h, :], pairs[:, :, :].rearrange("p a b -> p (a b)"))
            dve.drain()
            dve.max_index(best_at[:, :], best[:, h, :], pairs[:, :, :].rearrange("p a b -> p (a b)"))
            dve.tensor_scalar(lowest[:, h:h + 1], best[:, h, 0:1], -1.0, None, ALU.mult)
            dve.drain()
            dve.tensor_scalar(side[:, 0, :], best_at[:, :], 3, None, ALU.logical_shift_right)
            dve.tensor_scalar(side[:, 1, :], best_at[:, :], TOPK - 1, None, ALU.bitwise_and)
            dve.drain()
            dve.tensor_copy(side_f[:, :, :], side[:, :, :])
            dve.drain()
            dve.tensor_tensor(pick[:, :, :, :], side_f[:, :, :].unsqueeze(3).to_broadcast([P, 2, TOPK, TOPK]),
                              number[:, :].unsqueeze(1).unsqueeze(1).to_broadcast([P, 2, TOPK, TOPK]), ALU.is_equal)
            dve.drain()
            dve.tensor_tensor(pick[:, :, :, :], pick[:, :, :, :],
                              top_id[:, :, :].unsqueeze(2).to_broadcast([P, 2, TOPK, TOPK]), ALU.mult)
            dve.drain()
            dve.tensor_reduce(chosen[:, :, :], pick[:, :, :, :], AX, ALU.add)
            dve.drain()
            dve.scalar_tensor_tensor(out=rows_at[:, h, :], in0=chosen[:, 0, :], scalar=float(NKEYS), in1=chosen[:, 1, :],
                                     op0=ALU.mult, op1=ALU.add).then_inc(s["found"], 1)

        def use(dve, h, nth, t, before):
            dve.wait_ge(s["soft"], nth + 1)
            dve.reciprocal(rtotal[:, :], total[:, h:h + 1])
            for k in range(TOPK):
                slot = (h * TOPK + k) % RING
                dve.wait_ge(s_land[slot], (t * (HEADS // AHEAD) + (h // AHEAD + 1)) * 16)
                dve.tensor_tensor_reduce(ring[:, slot, 0:D], ring[:, slot, 0:D], current[:, :], 1.0, 0.0, ALU.mult, ALU.add,
                                         inner[:, k:k + 1])
            if before is not None:
                add_memory(dve, before)
            dve.drain()
            dve.tensor_scalar(part[:, :], expo[:, h, :], rtotal[:, 0:1], None, ALU.mult)
            dve.drain()
            dve.scalar_tensor_tensor(out=weight[:, h % AHEAD, :], in0=inner[:, :], scalar=0.0, in1=part[:, :],
                                     op0=ALU.max, op1=ALU.mult).then_inc(s["weight"], 1)
            dve.drain()

        def add_memory(dve, t):
            dve.wait_ge(s["slot_free"], (t + 1) * (HEADS * TOPK) + RING)
            dve.tensor_tensor(c.x[:, bass.ds(t, 1), :], c.x[:, bass.ds(t, 1), :], acc[:, :].unsqueeze(1),
                              ALU.add).then_inc(s["x2"], 1)

        def layer_sum(dve, u):
            dve.wait_ge(s["layer"], u + 1)
            dve.tensor_tensor(h_sum[:, :], psH[:, 1, :], bias[:, :], ALU.add)
            dve.drain()
            dve.bn_stats(stats[:, :], h_sum[:, :])
            dve.drain()
            dve.bn_aggr(mv[:, :], stats[:, :])
            dve.drain()
            dve.tensor_scalar(rstd[:, :], mv[:, 1:2], EPS, None, ALU.add).then_inc(s["moments"], 1)

        def layer_norm(dve, u):
            one = bass.ds(u, 1)
            dve.wait_ge(s["root"], u + 1)
            dve.reciprocal(rstd[:, :], root[:, :])
            dve.drain()
            dve.tensor_scalar(product[:, :], h_sum[:, :], mv[:, 0:1], rstd[:, 0:1], ALU.subtract, ALU.mult)
            dve.tensor_tensor(c.x[:, one, :], c.x[:, one, :], psH[:, 0, :].unsqueeze(1), ALU.add).then_inc(s["x1"], 1)
            dve.drain()
            dve.tensor_tensor(h_sum[:, :], product[:, :], gamma[:, :], ALU.mult)

        def layer_add(dve, u):
            one = bass.ds(u, 1)
            dve.drain()
            dve.tensor_tensor(c.x[:, one, :], c.x[:, one, :], h_sum[:, :].unsqueeze(1), ALU.add)
            dve.drain()
            dve.bn_stats(stats1[:, :], c.x[:, one, :])
            dve.drain()
            dve.bn_aggr(mv1[:, :], stats1[:, :])
            dve.drain()
            dve.tensor_scalar(rstd1[:, :], mv1[:, 1:2], EPS, None, ALU.add).then_inc(s["moments1"], 1)

        def next_rows(dve, n):
            dve.wait_ge(s["root1"], n + 1)
            dve.reciprocal(rstd1[:, :], root1[:, :])
            dve.drain()
            dve.tensor_scalar(coming[:, :], c.x[:, bass.ds(n, 1), :], mv1[:, 0:1], rstd1[:, 0:1],
                              ALU.subtract, ALU.mult).then_inc(s["coming"], 1)

        @block.vector
        def _(dve):
            def tile(t, before, more, last):
                dve.drain()
                dve.tensor_copy(current[:, :], coming[:, :])
                dve.drain()
                for h in range(HEADS):
                    use(dve, h, t * HEADS + h, t, before if h == 0 else None)
                    if not (last and h + LEAD >= HEADS):
                        search(dve, (h + LEAD) % HEADS, t * HEADS + (h + LEAD))
                    if not last and 1 <= h <= 3:
                        (layer_norm, layer_add, next_rows)[h - 1](dve, t + 1)
                    if h == HEADS - 1 and more:
                        layer_sum(dve, t + 2)

            layer_sum(dve, 0)
            layer_norm(dve, 0)
            layer_add(dve, 0)
            next_rows(dve, 0)
            dve.wait_ge(s["number"], 1)
            for h in range(LEAD):
                search(dve, h, h)
            layer_sum(dve, 1)
            tile(0, None, True, False)
            with dve.Fori(1, NT - 2) as t:
                tile(t, t - 1, True, False)
            tile(NT - 2, NT - 3, False, False)
            tile(NT - 1, NT - 2, False, True)
            add_memory(dve, NT - 1)

        @block.scalar
        def _(act):
            def queries(h, nth):
                act.wait_ge(s["q"], nth + 1)
                wait(act, "score", nth - 1)
                for i in range(2):
                    a = slice(64 * i, 64 * i + 64)
                    act.activation(qz[a, h % 2, i, :], psQ[a, h % 2, 0:P], ACT.Identity, bias=bq[a, h:h + 1]).then_inc(s["qT"], 1)

            def soften(h, nth):
                act.wait_ge(s["found"], nth + 1)
                act.activation(expo[:, h, :], best[:, h, :], ACT.Exp, bias=lowest[:, h:h + 1],
                               accum_out=total[:, h:h + 1]).then_inc(s["soft"], 1)

            def stage_x(u):
                if not isinstance(u, int) or u > 0:
                    wait_alone(c, act, s["layer"], u)
                act.activation(xt[:, :, :], c.xnT[:, :, column(u)], ACT.Copy).then_inc(s["xt"], 1)

            def layer_root(u):
                act.wait_ge(s["moments"], u + 1)
                act.activation(root[:, :], rstd[:, :], ACT.Sqrt).then_inc(s["root"], 1)

            def x1_root(u):
                act.wait_ge(s["moments1"], u + 1)
                act.activation(root1[:, :], rstd1[:, :], ACT.Sqrt).then_inc(s["root1"], 1)

            def turned_rows(n):
                act.wait_ge(s["tr"], n + 1)
                act.activation(xT[:, :, :], psT[:, :].rearrange("p (k n) -> p k n", k=KC), ACT.Copy).then_inc(s["xT"], 1)

            def tile(t, more, last):
                for h in range(HEADS):
                    if h == 0 and not last:
                        layer_root(t + 1)
                    if h == 1 and more:
                        stage_x(t + 2)
                    if h == 4 and not last:
                        turned_rows(t + 1)
                    if not (last and h + LEAD + 1 >= HEADS):
                        queries((h + LEAD + 1) % HEADS, t * HEADS + (h + LEAD + 1))
                    act.wait_ge(s["weight"], t * HEADS + (h + 1))
                    act.wait_ge(s["slot_free"], t * (HEADS * TOPK) + (h + 1) * TOPK)
                    for k in range(TOPK):
                        act.activation(diag[:, h % AHEAD * TOPK + k, :], c.ident[:, :], ACT.Copy,
                                       scale=weight[:, h % AHEAD, k:k + 1]).then_inc(s["diag"], 1)
                    if not (last and h + LEAD >= HEADS):
                        soften((h + LEAD) % HEADS, t * HEADS + (h + LEAD))
                    if h == 2 and not last:
                        x1_root(t + 1)

            stage_x(0)
            layer_root(0)
            x1_root(0)
            act.wait_ge(s["w"], 32)
            act.wait_ge(s["qz0"], 1)
            stage_x(1)
            turned_rows(0)
            queries(0, 0)
            for h in range(LEAD):
                queries(h + 1, h + 1)
                soften(h, h)
            tile(0, True, False)
            with act.Fori(1, NT - 2) as t:
                tile(t, True, False)
            tile(NT - 2, False, False)
            tile(NT - 1, False, True)

        def layer(pe, u, lo, hi):
            if lo == 0:
                pe.wait_ge(s["xt"], u + 1)
                wait(pe, "x1", u)
            for i in range(lo, hi):
                if i < KC:
                    mm = pe.matmul(psH[:, 0, :], xt[:, i, :], kv[:, i, :], start=i == 0, stop=i == KC - 1)
                elif i < 2 * KC:
                    mm = pe.matmul(psH[:, 1, :], xt[:, i - KC, :], ws[:, i - KC, :], start=i == KC, stop=False)
                else:
                    a = i - 2 * KC
                    if a == 0:
                        pe.wait_ge(s["share_in"], u * 16 + 16)
                    mm = pe.matmul(psH[:, 1, :], share[:, a, :], neigh[:, a, :], start=False, stop=a == NT - 1)
            if hi == 2 * KC + NT:
                mm.then_inc(s["layer"], 1)

        def project(pe, h, nth):
            wait(pe, "qT", (nth - 1) * 2)
            for k in range(KC):
                mm = pe.matmul(psQ[:, h % 2, 0:P], wq[:, k, h * P:(h + 1) * P], xT[:, k, :], start=k == 0, stop=k == KC - 1)
            mm.then_inc(s["q"], 1)

        def scores(pe, h, nth):
            pe.wait_ge(s["qT"], (nth + 1) * 2)
            wait(pe, "found", nth - 1)
            for i in range(2):
                mm = pe.matmul(psS[:, h % 2, NKEYS * i:NKEYS * (i + 1)], qz[:, h % 2, i, :], keys[:, h, :], start=True, stop=True)
            mm.then_inc(s["score"], 1)

        def turn_rows(pe, n):
            pe.wait_ge(s["coming"], n + 1)
            for k in range(KC):
                mm = pe.transpose(psT[:, k * P:(k + 1) * P], coming[:, k * P:(k + 1) * P], c.ident[:, :])
            mm.then_inc(s["tr"], 1)

        @block.tensor
        def _(pe):
            def tile(t, more, last):
                for h in range(HEADS):
                    if h >= EARLY and more:
                        layer(pe, t + 2, (h - EARLY) * EACH, (h - EARLY + 1) * EACH)
                    if h == 4 and not last:
                        turn_rows(pe, t + 1)
                        pe.wait_ge(s["xT"], t + 2)
                    if not (last and h + LEAD + 1 >= HEADS):
                        project(pe, (h + LEAD + 1) % HEADS, t * HEADS + (h + LEAD + 1))
                    if not (last and h + LEAD >= HEADS):
                        scores(pe, (h + LEAD) % HEADS, t * HEADS + (h + LEAD))
                    if h == 0:
                        wait(pe, "x2", t)
                    for k in range(TOPK):
                        pe.wait_ge(s["diag"], t * (HEADS * TOPK) + (h * TOPK + k + 1))
                        pe.matmul(acc[:, :], diag[:, h % AHEAD * TOPK + k, :], ring[:, (h * TOPK + k) % RING, D:2 * D],
                                  start=h + k == 0, stop=h * TOPK + k == HEADS * TOPK - 1).then_inc(s["slot_free"], 1)

            pe.sem_inc(s["slot_free"], RING)
            layer(pe, 0, 0, PRODUCTS)
            pe.wait_ge(s["w"], 32)
            turn_rows(pe, 0)
            pe.wait_ge(s["xT"], 1)
            project(pe, 0, 0)
            for h in range(LEAD):
                project(pe, h + 1, h + 1)
                scores(pe, h, h)
            layer(pe, 1, 0, PRODUCTS)
            tile(0, True, False)
            with pe.Fori(1, NT - 2) as t:
                tile(t, True, False)
            tile(NT - 2, False, False)
            tile(NT - 1, False, True)


def layer0(c):
    with ExitStack() as st:
        sb = lambda n, s: st.enter_context(c.nc.sbuf_tensor(n, s, F32))
        keep = sb("neigh", [P, NT, D]), sb("kv", [P, KC, D])
        ahead = sb("ws", [P, KC, D]), sb("keys", [P, HEADS, NKEYS]), sb("bias", [P, D]), sb("gamma", [P, D])
        stage_prepare(c, keep, ahead)
        c.end_stage()
        stage_layer0(c, keep, ahead)
        c.end_stage()


PAIRS = HEADS // 2


def chunked(w):
    return w.rearrange("(k p) n -> p k n", p=P)


def transposed_norm(c, tag, ahead):
    nc = c.nc
    with ExitStack() as st:
        norm = RowStats(c, st, tag)
        rows = st.enter_context(nc.sbuf_tensor(tag + "rows", [P, 2, D], F32))
        psT = st.enter_context(nc.psum_tensor(tag + "psT", [P, 2, D], F32))
        s_rows, s_tr, s_out, s_ahead = (c.sem(tag + n) for n in ("rows_ready", "turned", "stored", "ahead"))
        block = st.enter_context(nc.Block())

        @block.sync
        def _(sp):
            for dst, src in ahead:
                sp.dma_start(dst, src).then_inc(s_ahead, 16)
            sp.wait_ge(s_ahead, 16 * len(ahead))

        @block.vector
        def _(dve):
            norm.moments(dve, 0)
            for b in range(2):
                norm.normalise(dve, b, rows[:, b, :]).then_inc(s_rows, 1)
            norm.moments(dve, 1)
            with dve.Fori(1, NT // 2) as j:
                for b in range(2):
                    dve.wait_ge(s_tr, j * 2 + b)
                    norm.normalise(dve, j * 2 + b, rows[:, b, :]).then_inc(s_rows, 1)

        @block.tensor
        def _(pe):
            pe.sem_inc(s_tr, 1)
            pe.sem_inc(s_out, 1)
            with pe.Fori(0, NT // 2) as j:
                for b in range(2):
                    pe.wait_ge(s_rows, j * 2 + (b + 1))
                    pe.wait_ge(s_out, j * 2 + b)
                    for k in range(KC):
                        mm = pe.transpose(psT[:, b, k * P:(k + 1) * P], rows[:, b, k * P:(k + 1) * P], c.ident[:, :])
                    mm.then_inc(s_tr, 1)

        @block.scalar
        def _(act):
            norm.roots(act)
            with act.Fori(0, NT // 2) as j:
                for b in range(2):
                    wait_alone(c, act, s_tr, j * 2 + (b + 2))
                    act.activation(c.xnT[:, :, column(j * 2 + b)], psT[:, b, :].rearrange("p (k n) -> p k n", k=KC),
                                   ACT.Copy).then_inc(s_out, 1)


def stage_token_mix(c, mix, weights, ahead):
    nc, ins = c.nc, c.ins
    with ExitStack() as st:
        sb = lambda n, s, d=F32: st.enter_context(nc.sbuf_tensor("t_" + n, s, d))
        ps = lambda n, s: st.enter_context(nc.psum_tensor("t_" + n, s, F32))
        wqk, wv, wo = weights
        q, k_rows = sb("q", [P, NT, D]), sb("k_rows", [P, NT, P])
        kT = sb("kT", [P, 2, NP])
        low, ksum, rk = sb("low", [P, PAIRS]), sb("ksum", [P, PAIRS]), sb("rk", [P, PAIRS])
        qmax, qsum, qr = sb("qmax", [P, HEADS]), sb("qsum", [P, HEADS]), sb("qr", [P, HEADS])
        qe, qs = sb("qe", [P, 2, D]), sb("qs", [P, 2, D])
        kq, z = sb("kq", [P, PAIRS, P]), sb("z", [P, PAIRS, D])
        psQ, psK, psR, psM = ps("psQ", [P, 2, D]), ps("psK", [P, 3 * D]), ps("psR", [P, 2, D]), ps("psM", [P, D])
        names = ("ahead", "q", "qd", "qexp", "qout", "kq0", "k", "low", "kexp", "tr", "krows", "kq", "kqout", "z", "zout", "y", "yout",
                 "rk", "pad")
        s = {n: c.sem("t_" + n) for n in names}
        block = st.enter_context(nc.Block())

        @block.sync
        def _(sp):
            for dst, src in ahead:
                sp.dma_start(dst, src).then_inc(s["ahead"], 16)
            sp.wait_ge(s["ahead"], 16 * len(ahead))

        @block.gpsimd
        def _(pool):
            pool.memset(kq[:, :, :], 0.0).then_inc(s["kq0"], 1)
            pool.memset(kT[:, :, N:NP], 0.0).then_inc(s["pad"], 1)

        @block.tensor
        def _(pe):
            for t in range(NT):
                if t >= 2:
                    pe.wait_ge(s["qd"], t - 1)
                for k in range(KC):
                    mm = pe.matmul(psQ[:, t % 2, :], c.xnT[:, k, t * P:(t + 1) * P], wqk[:, k, 0:D], start=k == 0, stop=k == KC - 1)
                mm.then_inc(s["q"], 1)
            def keys(m):
                if m:
                    pe.wait_ge(s["kexp"], m)
                for a, n in CHUNKS:
                    for k in range(KC):
                        mm = pe.matmul(psK[:, a:a + n], wqk[:, k, D + m * P:D + (m + 1) * P], c.xnT[:, k, a:a + n],
                                       start=k == 0, stop=k == KC - 1)
                mm.then_inc(s["k"], 1)

            keys(0)
            pe.wait_ge(s["qout"], NT)
            for m in range(PAIRS):
                if m + 1 < PAIRS:
                    keys(m + 1)
                pe.wait_ge(s["kexp"], m + 1)
                for g in range(3):
                    if 3 * m + g >= 2:
                        pe.wait_ge(s["krows"], 3 * m + g - 1)
                    for a in range(4 * g, min(4 * g + 4, NT)):
                        mm = pe.transpose(psR[:, (3 * m + g) % 2, a % 4 * P:(a % 4 + 1) * P], kT[:, m % 2, a * P:(a + 1) * P], c.ident[:, :])
                    mm.then_inc(s["tr"], 1)
                pe.wait_ge(s["krows"], 3 * m + 3)
                if m:
                    pe.wait_ge(s["kqout"], 2 * m)
                for t in range(NT):
                    mm = pe.matmul(psM[:, 0:P], k_rows[:, t, :], q[:, t, m * P:(m + 1) * P], start=t == 0, stop=t == NT - 1)
                mm.then_inc(s["kq"], 1)
            pe.wait_ge(s["kqout"], 2 * PAIRS)
            for m in range(PAIRS):
                if m >= 2:
                    pe.wait_ge(s["zout"], m - 1)
                pe.transpose(psM[:, 0:P], kq[:, m, :], c.ident[:, :]).then_inc(s["z"], 1)
                pe.wait_ge(s["zout"], 2 * m + 1)
                pe.matmul(psQ[:, m % 2, :], kT[:, 0, 0:P], wo[:, m, :], start=True, stop=True).then_inc(s["z"], 1)
                pe.wait_ge(s["zout"], 2 * m + 2)
            for m in range(KC):
                if m >= 2:
                    pe.wait_ge(s["yout"], m - 1)
                for k in range(KC):
                    mm = pe.matmul(psQ[:, m % 2, :], wv[:, k, m * P:(m + 1) * P], z[:, k, :], start=k == 0, stop=k == KC - 1)
                mm.then_inc(s["y"], 1)

        def heads(ap):
            return ap.rearrange("p (h e) -> p h e", h=HEADS)

        @block.vector
        def _(dve):
            dve.wait_ge(s["kq0"], 1)
            dve.wait_ge(s["pad"], 1)
            for t in range(NT):
                b = t % 2
                dve.wait_ge(s["q"], t + 1)
                dve.tensor_reduce(qmax[:, :], heads(psQ[:, b, :]), AX, ALU.max)
                dve.drain()
                dve.tensor_tensor(heads(qs[:, b, :]), heads(psQ[:, b, :]), qmax[:, :].unsqueeze(2).to_broadcast([P, HEADS, D // HEADS]),
                                  ALU.subtract).then_inc(s["qd"], 1)
                dve.wait_ge(s["qexp"], t + 1)
                dve.tensor_reduce(qsum[:, :], heads(qe[:, b, :]), AX, ALU.add)
                dve.drain()
                dve.reciprocal(qr[:, :], qsum[:, :])
                dve.drain()
                dve.tensor_tensor(heads(q[:, t, :]), heads(qe[:, b, :]), qr[:, :].unsqueeze(2).to_broadcast([P, HEADS, D // HEADS]),
                                  ALU.mult).then_inc(s["qout"], 1)
                dve.drain()
            def lowest(m):
                dve.wait_ge(s["k"], m + 1)
                dve.tensor_reduce(low[:, m:m + 1], psK[:, 0:N], AX, ALU.max)
                dve.drain()
                dve.tensor_scalar(low[:, m:m + 1], low[:, m:m + 1], -1.0, None, ALU.mult).then_inc(s["low"], 1)

            lowest(0)
            for m in range(PAIRS):
                dve.wait_ge(s["kexp"], m + 1)
                dve.reciprocal(rk[:, m:m + 1], ksum[:, m:m + 1]).then_inc(s["rk"], 1)
                if m + 1 < PAIRS:
                    lowest(m + 1)
                dve.wait_ge(s["kq"], m + 1)
                dve.drain()
                for i in range(2):
                    a = slice(64 * i, 64 * i + 64)
                    dve.tensor_scalar(kq[a, m, a], psM[a, a], rk[a, m:m + 1], None, ALU.mult).then_inc(s["kqout"], 1)

        @block.scalar
        def _(act):
            for t in range(NT):
                act.wait_ge(s["qd"], t + 1)
                act.activation(qe[:, t % 2, :], qs[:, t % 2, :], ACT.Exp).then_inc(s["qexp"], 1)
            def exponent(m):
                act.wait_ge(s["low"], m + 1)
                if m >= 2:
                    act.wait_ge(s["tr"], 3 * m - 3)
                act.activation(kT[:, m % 2, 0:N], psK[:, 0:N], ACT.Exp, bias=low[:, m:m + 1],
                               accum_out=ksum[:, m:m + 1]).then_inc(s["kexp"], 1)

            exponent(0)
            for m in range(PAIRS):
                for g in range(3):
                    n = min(4, NT - 4 * g)
                    act.wait_ge(s["tr"], 3 * m + g + 1)
                    if m:
                        act.wait_ge(s["kq"], m)
                    act.activation(k_rows[:, 4 * g:4 * g + n, :], psR[:, (3 * m + g) % 2, 0:n * P].rearrange("p (a n) -> p a n", a=n),
                                   ACT.Copy).then_inc(s["krows"], 1)
                if m + 1 < PAIRS:
                    exponent(m + 1)
            for m in range(PAIRS):
                act.wait_ge(s["z"], 2 * m + 1)
                act.activation(kT[:, 0, 0:P], psM[:, 0:P], ACT.Copy).then_inc(s["zout"], 1)
                act.wait_ge(s["z"], 2 * m + 2)
                act.activation(z[:, m, :], psQ[:, m % 2, :], ACT.Copy).then_inc(s["zout"], 1)
            for m in range(KC):
                act.wait_ge(s["y"], m + 1)
                act.activation(mix[:, m, :], psQ[:, m % 2, :], ACT.Copy).then_inc(s["yout"], 1)
            act.wait_ge(s["yout"], KC)


def stage_projections(c, v, w, join_loads):
    nc, ins = c.nc, c.ins
    with ExitStack() as st:
        sb = lambda n, s, d=F32: st.enter_context(nc.sbuf_tensor("p3_" + n, s, d))
        ps = lambda n, s: st.enter_context(nc.psum_tensor("p3_" + n, s, F32))
        bqk, bq8, bv = sb("bqk", [P, 2 * PAIRS]), sb("bq8", [P, PAIRS]), sb("bv", [P, D])
        full, parts = sb("full", [P, 2, NP]), sb("parts", [P, 2, 2, NP], F32R)
        psP, psV = ps("psP", [P, 2, 3, D]), ps("psV", [P, 2, D])
        s = {n: c.sem("p3_" + n) for n in ("ahead", "b", "bq8", "made", "full", "split", "kept_0", "kept_1", "v", "vout")}
        block = st.enter_context(nc.Block())

        @block.sync
        def _(sp):
            sp.dma_start(bqk[:, :], ins["b_qkT"]).then_inc(s["b"], 16)
            sp.dma_start(bv[:, :], ins["b_v"].partition_broadcast(P)).then_inc(s["b"], 16)
            for dst, src in join_loads:
                sp.dma_start(dst, src).then_inc(s["ahead"], 16)
            for i in range(2 * PAIRS):
                sp.wait_ge(s["split"], i + 1)
                for part in range(2):
                    for h in range(2):
                        sp.dma_start(c.qk_parts[2 * i + h, part, :, :], parts[64 * h:64 * h + 64, i % 2, part, :].bitcast(F32))\
                          .then_inc(s[f"kept_{i % 2}"], 16)
            for b in range(2):
                sp.wait_ge(s[f"kept_{b}"], 64 * PAIRS)
            sp.wait_ge(s["ahead"], 16 * len(join_loads))

        @block.tensor
        def _(pe):
            for i in range(2 * PAIRS):
                if i >= 2:
                    pe.wait_ge(s["full"], i - 1)
                for g, (a, n) in enumerate(CHUNKS):
                    for k in range(KC):
                        mm = pe.matmul(psP[:, i % 2, g, 0:n], w[:, k, i * P:(i + 1) * P], c.xnT[:, k, a:a + n],
                                       start=k == 0, stop=k == KC - 1)
                mm.then_inc(s["made"], 1)
            for t in range(NT):
                if t >= 2:
                    pe.wait_ge(s["vout"], t - 1)
                for k in range(KC):
                    mm = pe.matmul(psV[:, t % 2, :], c.xnT[:, k, t * P:(t + 1) * P], w[:, k, 2 * D:3 * D], start=k == 0, stop=k == KC - 1)
                mm.then_inc(s["v"], 1)

        @block.scalar
        def _(act):
            act.wait_ge(s["bq8"], 1)
            for i in range(2 * PAIRS):
                act.wait_ge(s["made"], i + 1)
                if i >= 2:
                    act.wait_ge(s["split"], i - 1)
                bias, scale = (bq8[:, i:i + 1], 64 ** -0.5) if i < PAIRS else (bqk[:, i:i + 1], 1.0)
                act.activation(full[:, i % 2, :], psP[:, i % 2, :, :].rearrange("p a n -> p (a n)")[:, 0:NP], ACT.Identity,
                               bias=bias, scale=scale).then_inc(s["full"], 1)

        @block.vector
        def _(dve):
            dve.wait_ge(s["b"], 32)
            dve.tensor_scalar(bq8[:, :], bqk[:, 0:PAIRS], 64 ** -0.5, None, ALU.mult).then_inc(s["bq8"], 1)
            for i in range(2 * PAIRS):
                b = i % 2
                dve.wait_ge(s["full"], i + 1)
                if i >= 2:
                    dve.wait_ge(s[f"kept_{b}"], 64 * (i // 2))
                dve.tensor_copy(parts[:, b, 0, :], full[:, b, :])
                dve.drain()
                dve.tensor_tensor(parts[:, b, 1, :], full[:, b, :], parts[:, b, 0, :], ALU.subtract).then_inc(s["split"], 1)
            for t in range(NT):
                dve.wait_ge(s["v"], t + 1)
                dve.tensor_tensor(v[:, t, :], psV[:, t % 2, :], bv[:, :], ALU.add).then_inc(s["vout"], 1)


def stage_edge_attention(c, v, msg):
    nc = c.nc
    with ExitStack() as st:
        sb = lambda n, s, d=F32: st.enter_context(nc.sbuf_tensor("a_" + n, s, d))
        ps = lambda n, s: st.enter_context(nc.psum_tensor("a_" + n, s, F32))
        cnt, mask = sb("cnt", [P, 2, NP], U16), sb("mask", [P, 2, NP], BF16)
        q, k = sb("q", [P, 4, P], F32R), sb("k", [P, 2, 2, 2, NP], F32R)
        prob, pT = sb("prob", [P, 2, NP]), sb("pT", [P, 2, NT, P])
        low, den, rden = sb("low", [P, 2]), sb("den", [P, 4]), sb("rden", [P, 4])
        junk = sb("junk", [P, N], BF16)
        psS, psT = ps("psS", [P, 2, 3 * D]), ps("psT", [P, 2, D])
        names = ("score", "low", "exp", "weighed", "turned", "pT", "sums", "msg", "rden", "pad",
                 "mask0", "mask1", "cnt0", "cnt1", "q0", "q1", "q2", "q3", "k0", "k1")
        s = {n: c.sem("a_" + n) for n in names}
        U, GROUP = 2 * NT, 4
        GROUPS = PAIRS * U // GROUP
        J = U // GROUP
        PIECES = [(1, 0, 4), (1, 4, 8), (0, 8, NT)]
        block = st.enter_context(nc.Block())

        @block.sync
        def _(sp):
            def load_keys(m):
                if m >= 2:
                    sp.wait_ge(s["score"], (m - 1) * U + 4)
                for h in range(2):
                    for part in range(2):
                        for half in range(2):
                            sp.dma_start(k[64 * half:64 * half + 64, m % 2, h, part, :].bitcast(F32), c.qk_parts[HEADS + 2 * m + h, part, :, :])\
                              .then_inc(s[f"k{m % 2}"], 16)

            def load_group(m, j):
                g = m * J + j
                for b in range(2):
                    tile = bass.ds(j * 2 + b, 1)
                    sp.wait_ge(s["low"], g * GROUP + (2 * b + 2))
                    sp.dma_start(mask[:, b, :], c.masks[tile, :, :].rearrange("a p n -> p (a n)")).then_inc(s[f"mask{b}"], 16)
                    sp.wait_ge(s["weighed"], g * GROUP + (2 * b + 2))
                    sp.dma_start(cnt[:, b, :], c.counts[tile, :, :].rearrange("a p n -> p (a n)")).then_inc(s[f"cnt{b}"], 16)

            load_keys(0)
            for m in range(PAIRS):
                load_group(m, 0)
                load_group(m, 1)
                if m + 1 < PAIRS:
                    load_keys(m + 1)
                with sp.Fori(2, J) as j:
                    load_group(m, j)

        @block.gpsimd
        def _(pool):
            pool.memset(prob[:, :, N:NP], 0.0).then_inc(s["pad"], 1)
            for m in range(PAIRS):
                with pool.Fori(0, J) as j:
                    for i in range(GROUP):
                        wait_alone(c, pool, s["score"], m * U + j * GROUP + (i + 1))
                        pool.dma_start(q[:, i, :].bitcast(F32),
                                       c.qk_parts[2 * m + i % 2, :, :, :].rearrange("a p n -> (a p) n")[:, column(j * 2 + i // 2)])                            .then_inc(s[f"q{i}"], 16)

        @block.tensor
        def _(pe):
            pe.sem_inc(s["score"], 4)
            pe.sem_inc(s["turned"], 6)
            pe.sem_inc(s["sums"], 2)

            def score(g, i, kb):
                n, h = g * GROUP + i, i % 2
                pe.wait_ge(s[f"q{i}"], g * 16 + 16)
                pe.wait_ge(s["exp"], n + 1)
                for part in range(2):
                    for a, width in CHUNKS:
                        mm = pe.matmul(psS[:, h, a:a + width], q[:, i, :], k[:, kb, h, part, a:a + width],
                                       start=part == 0, stop=part == 1)
                mm.then_inc(s["score"], 1)

            def turn(n, h, piece):
                bank, a, z = PIECES[piece]
                if piece == 0:
                    pe.wait_ge(s["weighed"], n + 5)
                    if not isinstance(n, int) or n:
                        pe.wait_ge(s["pT"], n * 3 - 1)
                elif piece == 1:
                    pe.wait_ge(s["pT"], n * 3 + 1)
                else:
                    pe.wait_ge(s["msg"], n + 4)
                for x in range(a, z):
                    mm = pe.transpose(psT[:, bank, (x - a) * P:(x - a + 1) * P], prob[:, h, x * P:(x + 1) * P], c.ident[:, :])
                mm.then_inc(s["turned"], 1)

            def sums(m, n, h):
                pe.wait_ge(s["pT"], n * 3 + 3)
                for a in range(NT):
                    mm = pe.matmul(psT[:, 0, 2 * P:3 * P], pT[:, h, a, :], v[:, a, m * P:(m + 1) * P], start=a == 0, stop=a == NT - 1)
                mm.then_inc(s["sums"], 1)

            def group(m, j, following):
                g = m * J + j
                for i in range(GROUP):
                    n = g * GROUP + i
                    last = following is None and i == GROUP - 1
                    if i == 0:
                        score(g, 3, m % 2)
                    elif following is not None:
                        if following != m and i == 1:
                            pe.wait_ge(s[f"k{following % 2}"], 128 * (following // 2 + 1))
                        score(g + 1, i - 1, following % 2)
                    turn(n, i % 2, 2)
                    if not last:
                        turn(n + 1, (i + 1) % 2, 0)
                    sums(m, n, i % 2)
                    if not last:
                        turn(n + 1, (i + 1) % 2, 1)

            pe.wait_ge(s["k0"], 128)
            for i in range(3):
                score(0, i, 0)
            for piece in range(2):
                turn(0, 0, piece)
            for m in range(PAIRS):
                with pe.Fori(0, J - 1) as j:
                    group(m, j, m)
                group(m, J - 1, m + 1 if m + 1 < PAIRS else None)

        @block.vector
        def _(dve):
            dve.sem_inc(s["weighed"], 4)
            dve.sem_inc(s["low"], 4)
            dve.wait_ge(s["pad"], 1)

            def lowest(g, i):
                n, b, h = g * GROUP + i, i // 2, i % 2
                if h == 0:
                    wait_alone(c, dve, s[f"mask{b}"], g * 16 + 16)
                wait_alone(c, dve, s["score"], n + 5)
                dve.tensor_tensor_reduce(junk[:, :], psS[:, h, 0:N], mask[:, b, 0:N], -1.0, 3e38, ALU.add, ALU.min,
                                         low[:, h:h + 1])
                dve.drain()
                dve.scalar_tensor_tensor(out=low[:, h:h + 1], in0=low[:, h:h + 1], scalar=-0.1 * NEG, in1=low[:, h:h + 1],
                                         op0=ALU.is_lt, op1=ALU.mult).then_inc(s["low"], 1)

            def weigh(g, i):
                n, b, h = g * GROUP + i, i // 2, i % 2
                if h == 0:
                    dve.wait_ge(s[f"cnt{b}"], g * 16 + 16)
                dve.wait_ge(s["exp"], n + 3)
                dve.scalar_tensor_tensor(out=prob[:, h, 0:N], in0=prob[:, h, 0:N], scalar=1.0, in1=cnt[:, b, 0:N],
                                         op0=ALU.min, op1=ALU.mult, accum_out=den[:, i:i + 1]).then_inc(s["weighed"], 1)
                if h == 1:
                    both = slice(i - 1, i + 1)
                    dve.drain()
                    dve.tensor_scalar(den[:, both], den[:, both], 1e-30, None, ALU.max)
                    dve.drain()
                    dve.wait_ge(s["msg"], n + 1)
                    dve.reciprocal(rden[:, both], den[:, both]).then_inc(s["rden"], 1)

            lowest(0, 0)
            with dve.Fori(0, GROUPS - 1) as g:
                for i in range(GROUP):
                    lowest(g + (i + 1) // GROUP, (i + 1) % GROUP)
                    weigh(g, i)
            for i in range(GROUP):
                if i + 1 < GROUP:
                    lowest(GROUPS - 1, i + 1)
                weigh(GROUPS - 1, i)

        @block.scalar
        def _(act):
            act.sem_inc(s["msg"], 4)
            act.sem_inc(s["exp"], 2)

            def exponent(n, h):
                act.wait_ge(s["turned"], n * 3 + 3)
                act.wait_ge(s["low"], n + 5)
                act.activation(prob[:, h, 0:N], psS[:, h, 0:N], ACT.Exp, bias=low[:, h:h + 1]).then_inc(s["exp"], 1)

            def keep_turned(n, h, piece):
                bank, a, z = PIECES[piece]
                act.wait_ge(s["turned"], n * 3 + (7 + piece))
                act.wait_ge(s["sums"], n + 1)
                act.activation(pT[:, h, a:z, :], psT[:, bank, 0:(z - a) * P].rearrange("p (a n) -> p a n", n=P),
                               ACT.Copy).then_inc(s["pT"], 1)

            def message(g, i):
                n, at, h = g * GROUP + i, g * 2 + i // 2, i % 2
                if h == 0:
                    act.wait_ge(s["rden"], at + 1)
                wait_alone(c, act, s["sums"], n + 3)
                act.activation(msg[:, bass.ds(at, 1), 64 * h:64 * h + 64].rearrange("p a n -> p (a n)"),
                               psT[:, 0, 2 * P + 64 * h:2 * P + 64 * h + 64], ACT.Copy, scale=rden[:, i:i + 1]).then_inc(s["msg"], 1)

            def step(g, i, last):
                n = g * GROUP + i
                keep_turned(n, i % 2, 2)
                if not (last and i + 1 >= GROUP):
                    keep_turned(n + 1, (i + 1) % 2, 0)
                if not (last and i + 2 >= GROUP):
                    exponent(n + 2, i % 2)
                message(g, i)
                if not (last and i + 1 >= GROUP):
                    keep_turned(n + 1, (i + 1) % 2, 1)

            exponent(0, 0)
            exponent(1, 1)
            for piece in range(2):
                keep_turned(0, 0, piece)
            with act.Fori(0, GROUPS - 1) as g:
                for i in range(GROUP):
                    step(g, i, False)
            for i in range(GROUP):
                step(GROUPS - 1, i, True)


def stage_join(c, msg, mix, weights, ahead):
    nc = c.nc
    with ExitStack() as st:
        sb = lambda n, s, d=F32: st.enter_context(nc.sbuf_tensor("j_" + n, s, d))
        ps = lambda n, s: st.enter_context(nc.psum_tensor("j_" + n, s, F32))
        wff, bff, bout = weights
        mT, y, rows = sb("mT", [P, 2, KC, P]), sb("y", [P, 2, D]), sb("rows", [P, 2, D])
        stats, mv, var, root, rstd = sb("stats", [P, NT, 6]), sb("mv", [P, NT, 2]), sb("var", [P, NT]), sb("root", [P, NT]), sb("rstd", [P, NT])
        psT, psO, psN = ps("psT", [P, 2, D]), ps("psO", [P, 2, D]), ps("psN", [P, 2, D])
        s = {n: c.sem("j_" + n) for n in ("turned", "mT", "out", "sum_out", "var", "root", "rows", "norm_turned", "norm_out",
                                          "saved0", "saved1", "ahead")}
        block = st.enter_context(nc.Block())

        @block.sync
        def _(sp):
            for dst, src in ahead:
                sp.dma_start(dst, src).then_inc(s["ahead"], 16)
            for t in range(NT):
                sp.wait_ge(s["rows"], t + 1)
                sp.dma_start(c.norm_rows[t * P:(t + 1) * P, :], rows[:, t % 2, :]).then_inc(s[f"saved{t % 2}"], 16)
            for b in range(2):
                sp.wait_ge(s[f"saved{b}"], 16 * (NT // 2))
            sp.wait_ge(s["ahead"], 16 * len(ahead))

        @block.scalar
        def _(act):
            for t in range(NT + 2):
                if t < NT:
                    act.wait_ge(s["turned"], t + 1)
                    if t >= 2:
                        act.wait_ge(s["out"], t - 1)
                    act.activation(mT[:, t % 2, :, :], psT[:, t % 2, :].rearrange("p (k n) -> p k n", k=KC), ACT.Copy).then_inc(s["mT"], 1)
                if 1 <= t <= NT:
                    act.wait_ge(s["var"], t)
                    act.activation(root[:, t - 1:t], var[:, t - 1:t], ACT.Sqrt).then_inc(s["root"], 1)
                if t >= 2:
                    act.wait_ge(s["norm_turned"], t - 1)
                    act.activation(c.xnT[:, :, (t - 2) * P:(t - 1) * P], psN[:, t % 2, :].rearrange("p (k n) -> p k n", k=KC),
                                   ACT.Copy).then_inc(s["norm_out"], 1)

        @block.tensor
        def _(pe):
            def turn(t):
                if t >= 2:
                    pe.wait_ge(s["mT"], t - 1)
                for m in range(PAIRS):
                    mm = pe.transpose(psT[:, t % 2, m * P:(m + 1) * P], msg[:, m * NT + t, :], c.ident[:, :])
                mm.then_inc(s["turned"], 1)

            turn(0)
            for t in range(NT + 2):
                if t + 1 < NT:
                    turn(t + 1)
                if t < NT:
                    if t >= 2:
                        pe.wait_ge(s["sum_out"], t - 1)
                    for k in range(KC):
                        pe.matmul(psO[:, t % 2, :], c.xnT[:, k, t * P:(t + 1) * P], mix[:, k, :], start=k == 0, stop=False)
                    pe.wait_ge(s["mT"], t + 1)
                    for k in range(KC):
                        mm = pe.matmul(psO[:, t % 2, :], mT[:, t % 2, k, :], wff[:, k, :], start=False, stop=k == KC - 1)
                    mm.then_inc(s["out"], 1)
                if t >= 2:
                    pe.wait_ge(s["rows"], t - 1)
                    if t >= 4:
                        pe.wait_ge(s["norm_out"], t - 3)
                    for k in range(KC):
                        mm = pe.transpose(psN[:, t % 2, k * P:(k + 1) * P], rows[:, t % 2, k * P:(k + 1) * P], c.ident[:, :])
                    mm.then_inc(s["norm_turned"], 1)

        @block.vector
        def _(dve):
            dve.tensor_tensor(bff[:, :], bff[:, :], bout[:, :], ALU.add)
            dve.drain()
            for t in range(NT + 1):
                if t < NT:
                    dve.wait_ge(s["out"], t + 1)
                    dve.tensor_tensor(y[:, t % 2, :], psO[:, t % 2, :], bff[:, :], ALU.add).then_inc(s["sum_out"], 1)
                    dve.drain()
                    dve.tensor_tensor(c.x[:, t, :], c.x[:, t, :], y[:, t % 2, :], ALU.add)
                    dve.drain()
                    dve.bn_stats(stats[:, t, :], c.x[:, t, :])
                    dve.drain()
                    dve.bn_aggr(mv[:, t, :], stats[:, t, :])
                    dve.drain()
                    dve.tensor_scalar(var[:, t:t + 1], mv[:, t, 1:2], EPS, None, ALU.add).then_inc(s["var"], 1)
                if t >= 1:
                    u = t - 1
                    dve.wait_ge(s["root"], u + 1)
                    dve.reciprocal(rstd[:, u:u + 1], root[:, u:u + 1])
                    dve.drain()
                    if u >= 2:
                        dve.wait_ge(s["norm_turned"], u - 1)
                        dve.wait_ge(s[f"saved{u % 2}"], 16 * (u // 2))
                    dve.tensor_scalar(rows[:, u % 2, :], c.x[:, u, :], mv[:, u, 0:1], rstd[:, u:u + 1],
                                      ALU.subtract, ALU.mult).then_inc(s["rows"], 1)


def stage_attention(c, ahead):
    ins = c.ins
    with ExitStack() as st:
        sb = lambda n, s: st.enter_context(c.nc.sbuf_tensor(n, s, F32))
        mix, join = sb("mix", [P, KC, D]), (sb("wff", [P, KC, D]), sb("bff", [P, D]), sb("bout", [P, D]))
        v = sb("v", [P, NT, D])
        with ExitStack() as early:
            eb = lambda n, s: early.enter_context(c.nc.sbuf_tensor(n, s, F32))
            w_qkv, w_mix = eb("w_qkv", [P, KC, 3 * D]), (eb("wqk", [P, KC, 2 * D]), eb("mix_wv", [P, KC, D]), eb("mix_wo", [P, KC, D]))
            transposed_norm(c, "n3_", [(w[:, :, :], chunked(ins[name])) for w, name in
                                             zip(w_mix, ("mix_qkT", "mix_v", "mix_outT"))])
            c.end_stage()
            stage_token_mix(c, mix, w_mix, [(w_qkv[:, :, i * D:(i + 1) * D], chunked(ins["W_qkvT"])[:, :, i * D:(i + 1) * D])
                                            for i in range(3)])
            c.end_stage()
            stage_projections(c, v, w_qkv, [(join[0][:, :, :], chunked(ins["W_ffT"])), (join[1][:, :], ins["b_ff"].partition_broadcast(P)),
                                            (join[2][:, :], ins["b_out"].partition_broadcast(P))])
            c.end_stage()
        msg = sb("msg", [P, PAIRS * NT, P])
        stage_edge_attention(c, v, msg)
        c.end_stage()
        stage_join(c, msg, mix, join, ahead)
        c.end_stage()


CHOICES = 2
BLOCKS = (CHOICES * N + EXP * (P - 1)) // P
FEWEST = -(-CHOICES * N // P)


def rows_of(t):
    return P if t < NT - 1 else TAIL


def stage_gate(c, route, weights, ahead):
    nc, ins = c.nc, c.ins
    share, slot_of, slots, first_block, block_count = route
    with ExitStack() as st:
        sb = lambda n, s, d=F32: st.enter_context(nc.sbuf_tensor("r_" + n, s, d))
        ps = lambda n, s: st.enter_context(nc.psum_tensor("r_" + n, s, F32))
        gw1, gw2, gb1, gb2, be2 = weights
        gT = sb("gT", [P, 2, NP])
        logit, expo, gate = sb("logit", [P, NT, EXP]), sb("expo", [P, NT, EXP]), sb("gate", [P, NT, EXP])
        peak, total, top, top_at = sb("peak", [P, NT]), sb("total", [P, NT]), sb("top", [P, NT, 8]), sb("top_at", [P, NT, 8], U32)
        at, expert_i, expert = sb("at", [P, NT, 8]), sb("expert_i", [P, EXP], I32), sb("expert", [P, EXP])
        gap, second, first, hit = sb("gap", [P, NT]), sb("second", [P, NT]), sb("first", [P, NT]), sb("hit", [P, 2, NT, EXP])
        part, comb = sb("part", [P, 2, NT, EXP]), sb("comb", [P, NT, EXP])
        member, below, ones = sb("member", [P, NT, EXP]), sb("below", [P, P]), sb("ones", [P, P])
        rank, tally, before = sb("rank", [P, NT, EXP]), sb("tally", [P, NT, EXP]), sb("before", [P, NT + 1, EXP])
        filled_f, filled, blocks = sb("filled_f", [P, EXP]), sb("filled", [P, EXP], I32), sb("blocks", [P, EXP])
        start, base = sb("start", [P, EXP + 1]), sb("base", [P, EXP])
        slot_f = sb("slot_f", [P, 2, NT])
        blank = sb("blank", [P, D])
        row_id, spare = sb("row_id", [P, NT], U32), sb("spare", [P, BLOCKS], U32)
        combT = sb("combT", [EXP, NT, P])
        psG, psL, psC, psB = ps("psG", [P, 2, D]), ps("psL", [P, 3, NT, EXP]), ps("psC", [EXP, 3, D]), ps("psB", [P, 2, D])
        s = {n: c.sem("r_" + n) for n in ("iota", "expert", "hidden", "relu", "logits", "shifted", "exp", "gap", "exp2", "comb",
                                          "turned", "combT", "bias", "x", "tri", "both", "member", "ranked", "slot", "list0",
                                          "listed", "slots", "blank", "blanked", "ahead")}
        block = st.enter_context(nc.Block())

        def wide(ap):
            return ap.unsqueeze(2).to_broadcast([P, NT, EXP])

        @block.sync
        def _(sp):
            sp.wait_ge(s["iota"], 7)
            sp.dma_start(c.slot_list.rearrange("(p b) a -> p (b a)", p=P), spare[:, :]).then_inc(s["list0"], 16)
            sp.wait_ge(s["blank"], 1)
            for dst, src in ahead:
                sp.dma_start(dst, src).then_inc(s["ahead"], 16)
            for i in range(FEWEST, BLOCKS):
                sp.dma_start(c.slot_rows[i * P:(i + 1) * P, :], blank[:, :]).then_inc(s["blanked"], 16)
            sp.wait_ge(s["blanked"], 16 * (BLOCKS - FEWEST))
            sp.wait_ge(s["listed"], 16 * CHOICES * NT)
            sp.dma_start(slots[:, 0:BLOCKS], c.slot_list.rearrange("(b p) a -> p (b a)", p=P), allow_slow_non_contiguous=True).then_inc(s["slots"], 16)
            sp.wait_ge(s["slots"], 16)
            sp.wait_ge(s["ahead"], 16 * len(ahead))

        @block.gpsimd
        def _(pool):
            pool.iota(expert_i[:, :], pattern=[[1, EXP]], base=0, channel_multiplier=0).then_inc(s["iota"], 1)
            pool.iota(row_id[:, :], pattern=[[P, NT]], base=0, channel_multiplier=1).then_inc(s["iota"], 1)
            pool.iota(spare[:, :], pattern=[[0, BLOCKS]], base=NP - 1, channel_multiplier=0).then_inc(s["iota"], 1)
            pool.memset(below[:, :], 1.0).then_inc(s["iota"], 1)
            pool.memset(ones[:, :], 1.0).then_inc(s["iota"], 1)
            pool.memset(blank[:, :], 0.0).then_inc(s["blank"], 1)
            pool.wait_ge(s["iota"], 5)
            pool.tensor_copy(expert[:, :], expert_i[:, :]).then_inc(s["iota"], 1)
            pool.tensor_copy(slots[:, BLOCKS:BLOCKS + 1], spare[:, 0:1]).then_inc(s["iota"], 1)
            pool.affine_select(out=below[:, :], in_=below[:, :], compare_op=ALU.is_gt, fill=0.0, base=0,
                               pattern=[[1, P]], channel_multiplier=-1).then_inc(s["tri"], 1)
            pool.wait_ge(s["both"], 1)
            pool.affine_select(out=member[:, NT - 1, :], in_=member[:, NT - 1, :], compare_op=ALU.is_ge, fill=0.0,
                               base=TAIL - 1, pattern=[[0, EXP]], channel_multiplier=-1).then_inc(s["member"], 1)
            pool.wait_ge(s["slot"], 1)
            pool.wait_ge(s["list0"], 16)
            for i in range(CHOICES):
                for t in range(NT):
                    r = rows_of(t)
                    pool.indirect_dma_start(c.slot_list, bass.IndirectOffsetOnAxis(slot_of[0:r, i, t:t + 1], 0),
                                            row_id[0:r, t:t + 1], None).then_inc(s["listed"], 16)

        @block.tensor
        def _(pe):
            for m in range(2):
                for i, (a, n) in enumerate(CHUNKS):
                    u = 3 * m + i
                    if u >= 2:
                        pe.wait_ge(s["relu"], u - 1)
                    for k in range(KC):
                        mm = pe.matmul(psG[:, u % 2, 0:n], gw1[:, k, m * P:(m + 1) * P], c.xnT[:, k, a:a + n],
                                       start=k == 0, stop=k == KC - 1)
                    mm.then_inc(s["hidden"], 1)
            pe.wait_ge(s["relu"], 6)
            for t in range(NT):
                for m in range(2):
                    mm = pe.matmul(psL[:, 0, t, :], gT[:, m, t * P:(t + 1) * P], gw2[:, m, :], start=m == 0, stop=m == 1)
            mm.then_inc(s["logits"], 1)
            pe.wait_ge(s["tri"], 1)
            pe.wait_ge(s["member"], 1)
            pe.matmul(psL[:, 1, :, :], below[:, :], member[:, :, :], start=True, stop=True)
            pe.matmul(psL[:, 2, :, :], ones[:, :], member[:, :, :], start=True, stop=True).then_inc(s["ranked"], 1)
            pe.wait_ge(s["comb"], 1)
            for t in range(NT):
                mm = pe.transpose(psC[:, t // 4, t % 4 * P:(t % 4 + 1) * P], comb[:, t, :], c.ident[:, :])
            mm.then_inc(s["turned"], 1)
            pe.wait_ge(s["combT"], 1)
            for t in range(NT):
                if t >= 2:
                    pe.wait_ge(s["x"], t - 1)
                pe.matmul(psB[:, t % 2, :], combT[:, t, :], be2[:, :], start=True, stop=True).then_inc(s["bias"], 1)

        @block.scalar
        def _(act):
            for m in range(2):
                for i, (a, n) in enumerate(CHUNKS):
                    u = 3 * m + i
                    act.wait_ge(s["hidden"], u + 1)
                    act.activation(gT[:, m, a:a + n], psG[:, u % 2, 0:n], ACT.Relu, bias=gb1[:, m:m + 1]).then_inc(s["relu"], 1)
            act.wait_ge(s["shifted"], 1)
            act.activation(expo[:, :, :], logit[:, :, :], ACT.Exp).then_inc(s["exp"], 1)
            act.wait_ge(s["gap"], 1)
            act.activation(second[:, :], gap[:, :], ACT.Exp).then_inc(s["exp2"], 1)
            act.wait_ge(s["turned"], 1)
            act.activation(combT[:, :, :], psC[:, :, :].rearrange("p a (b n) -> p (a b) n", n=P)[:, 0:NT, :],
                           ACT.Copy).then_inc(s["combT"], 1)

        @block.vector
        def _(dve):
            dve.wait_ge(s["logits"], 1)
            dve.tensor_tensor(logit[:, :, :], psL[:, 0, :, :], gb2[:, :].unsqueeze(1).to_broadcast([P, NT, EXP]), ALU.add)
            dve.drain()
            dve.tensor_reduce(peak[:, :], logit[:, :, :], AX, ALU.max)
            dve.drain()
            dve.tensor_tensor(logit[:, :, :], logit[:, :, :], wide(peak[:, :]), ALU.subtract).then_inc(s["shifted"], 1)
            dve.wait_ge(s["exp"], 1)
            dve.tensor_reduce(total[:, :], expo[:, :, :], AX, ALU.add)
            dve.drain()
            dve.reciprocal(peak[:, :], total[:, :])
            dve.drain()
            dve.tensor_tensor(gate[:, :, :], expo[:, :, :], wide(peak[:, :]), ALU.mult)
            dve.drain()
            for t in range(NT):
                dve.max(top[:, t, :], gate[:, t, :])
            dve.drain()
            for t in range(NT):
                dve.max_index(top_at[:, t, :], top[:, t, :], gate[:, t, :])
            dve.tensor_tensor(gap[:, :], top[:, :, 1], top[:, :, 0], ALU.subtract).then_inc(s["gap"], 1)
            dve.drain()
            dve.tensor_copy(at[:, :, :], top_at[:, :, :])
            dve.wait_ge(s["exp2"], 1)
            dve.tensor_scalar(first[:, :], second[:, :], 1.0, None, ALU.add)
            dve.drain()
            dve.reciprocal(gap[:, :], first[:, :])
            dve.drain()
            dve.tensor_tensor(share[:, 1, :], second[:, :], gap[:, :], ALU.mult)
            dve.tensor_copy(share[:, 0, :], gap[:, :])
            dve.wait_ge(s["iota"], 7)
            ids = expert[:, :].unsqueeze(1).to_broadcast([P, NT, EXP])
            for i in range(CHOICES):
                dve.tensor_tensor(hit[:, i, :, :], wide(at[:, :, i]), ids, ALU.is_equal)
            dve.drain()
            dve.tensor_tensor(member[:, :, :], hit[:, 0, :, :], hit[:, 1, :, :], ALU.add).then_inc(s["both"], 1)
            for i in range(CHOICES):
                dve.tensor_tensor(part[:, i, :, :], hit[:, i, :, :], wide(share[:, i, :]), ALU.mult)
            dve.drain()
            dve.tensor_tensor(comb[:, :, :], part[:, 0, :, :], part[:, 1, :, :], ALU.add).then_inc(s["comb"], 1)
            dve.wait_ge(s["ranked"], 1)
            dve.tensor_copy(tally[:, :, :], psL[:, 2, :, :])
            dve.memset(before[:, 0, :], 0.0)
            dve.memset(start[:, 0:1], 0.0)
            dve.drain()
            for t in range(NT):
                dve.tensor_tensor(before[:, t + 1, :], before[:, t, :], tally[:, t, :], ALU.add)
                dve.drain()
            dve.tensor_scalar(filled_f[:, :], before[:, NT, :], float(P - 1), None, ALU.add)
            dve.drain()
            dve.tensor_copy(filled[:, :], filled_f[:, :])
            dve.drain()
            dve.tensor_scalar(filled[:, :], filled[:, :], 7, None, ALU.arith_shift_right)
            dve.drain()
            dve.tensor_copy(blocks[:, :], filled[:, :])
            dve.drain()
            dve.tensor_scalar(blocks[:, :], blocks[:, :], 1.0, None, ALU.max)
            dve.drain()
            dve.tensor_copy(block_count[:, :], blocks[:, :])
            for e in range(EXP):
                dve.tensor_tensor(start[:, e + 1:e + 2], start[:, e:e + 1], blocks[:, e:e + 1], ALU.add)
                dve.drain()
            dve.tensor_copy(first_block[:, :], start[:, :])
            dve.tensor_scalar(base[:, :], start[:, 0:EXP], float(P), None, ALU.mult)
            dve.tensor_tensor(rank[:, :, :], psL[:, 1, :, :], before[:, 0:NT, :], ALU.add)
            dve.drain()
            dve.tensor_tensor(rank[:, :, :], rank[:, :, :], base[:, :].unsqueeze(1).to_broadcast([P, NT, EXP]), ALU.add)
            dve.drain()
            for i in range(CHOICES):
                dve.tensor_tensor(part[:, i, :, :], hit[:, i, :, :], rank[:, :, :], ALU.mult)
            dve.drain()
            dve.tensor_reduce(slot_f[:, :, :], part[:, :, :, :], AX, ALU.add)
            dve.drain()
            dve.tensor_copy(slot_of[:, :, :], slot_f[:, :, :]).then_inc(s["slot"], 1)
            for t in range(NT):
                dve.wait_ge(s["bias"], t + 1)
                dve.tensor_tensor(c.x[:, t, :], c.x[:, t, :], psB[:, t % 2, :], ALU.add).then_inc(s["x"], 1)


def stage_expert_layers(c, route, weights):
    nc, ins = c.nc, c.ins
    share, slot_of, slots, first_block, block_count = route
    with ExitStack() as st:
        sb = lambda n, s, d=F32: st.enter_context(nc.sbuf_tensor("e_" + n, s, d))
        ps = lambda n, s: st.enter_context(nc.psum_tensor("e_" + n, s, F32))
        w1, w2, be1 = weights
        at, rows, rowsT = sb("at", [P, 1], U32), sb("rows", [P, D]), sb("rowsT", [P, KC, P])
        hT, y = sb("hT", [P, HC, P]), sb("y", [P, D])
        psT, psU, psY = ps("psT", [P, D]), ps("psU", [P, HC, P]), ps("psY", [P, D])
        s = {n: c.sem("e_" + n) for n in ("w0", "w1", "at", "rows", "turned", "rowsT", "up", "hidden", "gelu", "down", "y", "stored")}
        block = st.enter_context(nc.Block())

        def first_of(eng, e):
            return eng.value_load(first_block[0:1, bass.ds(e, 1)], min_val=0, max_val=BLOCKS)

        def count_of(eng, e):
            return eng.value_load(block_count[0:1, bass.ds(e, 1)], min_val=1, max_val=BLOCKS)

        def total_of(eng):
            return eng.value_load(first_block[0:1, EXP:EXP + 1], min_val=FEWEST, max_val=BLOCKS)

        @block.sync
        def _(sp):
            def load(e, b):
                sp.dma_start(w1[:, b, :, :], ins["we1"][bass.ds(e, 1), :, :].rearrange("e (k p) n -> p (e k) n", p=P)).then_inc(s[f"w{b}"], 16)
                sp.dma_start(w2[:, b, :, :], ins["we2"][bass.ds(e, 1), :, :].rearrange("e (k p) n -> p (e k) n", p=P)).then_inc(s[f"w{b}"], 16)

            sp.sem_inc(s["w0"], 32)
            load(1, 1)
            with sp.Fori(1, EXP // 2) as i:
                for b in range(2):
                    done = first_of(sp, i * 2 + (b - 1))
                    wait_alone(c, sp, s["down"], done)
                    load(i * 2 + b, b)

        @block.gpsimd
        def _(pool):
            total = total_of(pool)

            def fetch(n):
                wait_alone(c, pool, s["turned"], n)
                pool.tensor_copy(at[:, :], slots[:, bass.ds(n, 1)]).then_inc(s["at"], 1)
                wait_alone(c, pool, s["at"], n + 1)
                pool.indirect_dma_start(rows[:, :], None, c.norm_rows, bass.IndirectOffsetOnAxis(at[:, 0:1], 0)).then_inc(s["rows"], 16)

            def store(n):
                wait_alone(c, pool, s["y"], n + 1)
                pool.dma_start(c.slot_rows[bass.ds(n * P, P), :], y[:, :]).then_inc(s["stored"], 16)

            pool.tensor_copy(at[:, :], slots[:, 0:1]).then_inc(s["at"], 1)
            pool.wait_ge(s["at"], 1)
            pool.indirect_dma_start(rows[:, :], None, c.norm_rows, bass.IndirectOffsetOnAxis(at[:, 0:1], 0)).then_inc(s["rows"], 16)
            fetch(1)
            with pool.Fori(0, total - 1) as n:
                fetch(n + 2)
                store(n)
            store(total - 1)
            wait_alone(c, pool, s["stored"], total * 16)
            wait_alone(c, pool, s["rows"], total * 16 + 16)

        @block.tensor
        def _(pe):
            def turn(n):
                pe.wait_ge(s["rows"], n * 16 + 16)
                for k in range(KC):
                    mm = pe.transpose(psT[:, k * P:(k + 1) * P], rows[:, k * P:(k + 1) * P], c.ident[:, :])
                mm.then_inc(s["turned"], 1)

            turn(0)
            with pe.Fori(0, EXP // 2) as i:
                for b in range(2):
                    first, many = first_of(pe, i * 2 + b), count_of(pe, i * 2 + b)
                    wait_alone(c, pe, s[f"w{b}"], i * 32 + 32)
                    with pe.Fori(0, many) as j:
                        n = first + j
                        pe.wait_ge(s["rowsT"], n + 1)
                        pe.wait_ge(s["gelu"], n * HC)
                        for m in range(HC):
                            for k in range(KC):
                                mm = pe.matmul(psU[:, m, :], w1[:, b, k, m * P:(m + 1) * P], rowsT[:, k, :],
                                               start=k == 0, stop=k == KC - 1)
                            if m % (HC // 2) == HC // 2 - 1:
                                mm.then_inc(s["up" if m < HC // 2 else "hidden"], 1)
                        turn(n + 1)
                        pe.wait_ge(s["y"], n)
                        for m in range(HC):
                            if m % (HC // 4) == 0:
                                pe.wait_ge(s["gelu"], n * HC + (m + HC // 4))
                            mm = pe.matmul(psY[:, :], hT[:, m, :], w2[:, b, m, :], start=m == 0, stop=m == HC - 1)
                        mm.then_inc(s["down"], 1)

        @block.scalar
        def _(act):
            with act.Fori(0, EXP) as e:
                first, many = first_of(act, e), count_of(act, e)
                with act.Fori(0, many) as j:
                    n = first + j
                    wait_alone(c, act, s["down"], n)
                    for m in range(HC):
                        if m % (HC // 2) == 0:
                            wait_alone(c, act, s["hidden" if m else "up"], n + 1)
                        act.activation(hT[:, m, :], psU[:, m, :], ACT.Gelu,
                                       bias=be1[:, bass.ds(e * HC + m, 1)]).then_inc(s["gelu"], 1)

        @block.vector
        def _(dve):
            total = total_of(dve)

            def keep_turned(n):
                dve.wait_ge(s["turned"], n + 1)
                dve.tensor_copy(rowsT[:, :, :], psT[:, :].rearrange("p (k n) -> p k n", k=KC)).then_inc(s["rowsT"], 1)

            def keep_output(n):
                dve.wait_ge(s["down"], n + 1)
                dve.wait_ge(s["stored"], n * 16)
                dve.tensor_copy(y[:, :], psY[:, :]).then_inc(s["y"], 1)

            keep_turned(0)
            with dve.Fori(0, total) as n:
                dve.wait_ge(s["hidden"], n + 1)
                keep_turned(n + 1)
                keep_output(n)


def stage_combine(c, route):
    nc = c.nc
    share, slot_of, slots, first_block, block_count = route
    depth = 8
    with ExitStack() as st:
        got = st.enter_context(nc.sbuf_tensor("c_got", [P, depth, D], F32))
        s_got = [c.sem(f"c_got{i}") for i in range(depth)]
        s_used, s_out = c.sem("c_used"), c.sem("c_out")
        block = st.enter_context(nc.Block())

        @block.gpsimd
        def _(pool):
            for t in range(NT):
                for i in range(CHOICES):
                    n, r = t * CHOICES + i, rows_of(t)
                    if n >= depth:
                        pool.wait_ge(s_used, n - depth + 1)
                    pool.indirect_dma_start(got[0:r, n % depth, :], None, c.slot_rows,
                                            bass.IndirectOffsetOnAxis(slot_of[0:r, i, t:t + 1], 0)).then_inc(s_got[n % depth], 16)

        @block.vector
        def _(dve):
            for t in range(NT):
                for i in range(CHOICES):
                    n, r = t * CHOICES + i, rows_of(t)
                    dve.wait_ge(s_got[n % depth], 16 * (n // depth + 1))
                    dve.drain()
                    dve.scalar_tensor_tensor(out=c.x[0:r, t, :], in0=got[0:r, n % depth, :], scalar=share[0:r, i, t:t + 1],
                                             in1=c.x[0:r, t, :], op0=ALU.mult, op1=ALU.add).then_inc(s_used, 1)

        @block.sync
        def _(sp):
            for t in range(NT):
                r = rows_of(t)
                sp.wait_ge(s_used, CHOICES * (t + 1))
                sp.dma_start(c.out[t * P:t * P + r, :], c.x[0:r, t, :]).then_inc(s_out, 16)
            sp.wait_ge(s_out, 16 * NT)


def gate_weights(c, st):
    ins = c.ins
    sb = lambda n, s: st.enter_context(c.nc.sbuf_tensor("x_" + n, s, F32))
    gate = sb("gw1", [P, KC, 2 * P]), sb("gw2", [P, 2, EXP]), sb("gb1", [P, 2]), sb("gb2", [P, EXP]), sb("be2", [EXP, D])
    gw1, gw2, gb1, gb2, be2 = gate
    return gate, [(gw1[:, :, :], chunked(ins["gw1"])), (gw2[:, :, :], chunked(ins["gw2"])), (gb1[:, :], ins["gb1T"]),
                  (gb2[:, :], ins["gb2"].partition_broadcast(P)), (be2[:, :], ins["be2"])]


def stage_experts(c, gate):
    ins = c.ins
    with ExitStack() as st:
        sb = lambda n, s, d: st.enter_context(c.nc.sbuf_tensor("x_" + n, s, d))
        route = (sb("share", [P, CHOICES, NT], F32), sb("slot_of", [P, CHOICES, NT], U32), sb("slots", [P, BLOCKS + 1], U32),
                 sb("first_block", [P, EXP + 1], I32), sb("block_count", [P, EXP], I32))
        layers = sb("w1", [P, 2, KC, HID], F32), sb("w2", [P, 2, HC, D], F32), sb("be1", [P, EXP * HC], F32)
        stage_gate(c, route, gate, [(layers[0][:, 0, :, :], chunked(ins["we1"][0])), (layers[1][:, 0, :, :], chunked(ins["we2"][0])),
                                    (layers[2][:, :], ins["be1T"])])
        c.end_stage()
        stage_expert_layers(c, route, layers)
        c.end_stage()
        stage_combine(c, route)
        c.end_stage()
def build(nc, ins, out):
    with ExitStack() as ctx:
        c = Core(nc, ctx, ins, out)
        layer0(c)
        gate, loads = gate_weights(c, ctx)
        stage_attention(c, loads)
        stage_experts(c, gate)


def host_layout(a):
    import numpy as np

    def cc(v):
        return np.ascontiguousarray(v)

    def T(v):
        return cc(np.asarray(v).T)

    return {
        "x": cc(a["x"]), "src": cc(a["src"]), "dst": cc(a["dst"]),
        "W_selfT": T(a["L0_gnn_W_self"]), "W_neighT": T(a["L0_gnn_W_neigh"]),
        "bias": cc(a["L0_gnn_bias"]), "gamma": cc(a["L0_gnn_gamma"]), "beta": cc(a["L0_gnn_beta"]),
        "W_vT": T(a["L0_mix_W_v"]), "W_thetaT": T(a["L0_mix_W_theta"]),
        "Wq": cc(a["L0_ffn_Wq"]), "bqT": T(np.asarray(a["L0_ffn_bq"]).reshape(HEADS, P)),
        "keysT": cc(np.asarray(a["L0_ffn_keys"]).transpose(1, 3, 0, 2)),
        "mix_qkT": T(np.asarray(a["L1_mix_w_qkv"])[0:2 * D]), "mix_v": cc(np.asarray(a["L1_mix_w_qkv"])[2 * D:]),
        "mix_outT": T(a["L1_mix_w_out"]), "b_out": cc(a["L1_mix_b_out"]),
        "W_qkvT": T(a["L1_gnn_W_qkv"]), "W_ffT": T(a["L1_gnn_W_ff"]), "b_ff": cc(a["L1_gnn_b_ff"]),
        "b_qkT": T(np.asarray(a["L1_gnn_b_qkv"])[0:2 * D].reshape(2 * PAIRS, P)), "b_v": cc(np.asarray(a["L1_gnn_b_qkv"])[2 * D:]),
        "gw1": cc(a["L1_ffn_gw1"]), "gb1T": T(np.asarray(a["L1_ffn_gb1"]).reshape(2, P)), "gw2": cc(a["L1_ffn_gw2"]),
        "gb2": cc(a["L1_ffn_gb2"]), "we1": cc(a["L1_ffn_we1"]), "we2": cc(a["L1_ffn_we2"]), "be2": cc(a["L1_ffn_be2"]),
        "be1T": T(np.asarray(a["L1_ffn_be1"]).reshape(EXP * HC, P)),
        "table": np.concatenate([np.asarray(a["L0_ffn_w_down"]), np.asarray(a["L0_ffn_w_up"])], axis=1),
    }


def kernel(**inputs):
    import concourse.bacc as bacc
    from concourse.bass_utils import run_bass_kernel_spmd

    arrays = host_layout(inputs)
    nc = bacc.Bacc("TRN2", target_bir_lowering=False, num_devices=1)
    ins = {name: nc.dram_tensor("in_" + name, a.shape, mybir.dt.from_np(a.dtype), kind="ExternalInput").ap()
           for name, a in arrays.items()}
    out = nc.dram_tensor("out", (N, D), F32, kind="ExternalOutput").ap()
    build(nc, ins, out)
    return run_bass_kernel_spmd(nc, [{"in_" + name: a for name, a in arrays.items()}], core_ids=[0]).results[0]["out"]
```
